# Optimizing a Trainium2 kernel written in Bass

```python
import numpy as np
import jax
import jax.numpy as jnp

def _softmax(x, axis=-1):
    return jax.nn.softmax(x, axis=axis)

def _gelu(x):
    return jax.nn.gelu(x, approximate=True)

def _silu(x):
    return jax.nn.silu(x)

def _sigmoid(x):
    return jax.nn.sigmoid(x)

def _layernorm(x, axis=-1, eps=1e-05):
    m = jnp.mean(x, axis=axis, keepdims=True)
    v = jnp.var(x, axis=axis, keepdims=True)
    return (x - m) / jnp.sqrt(v + eps)

def _scatter_add(tgt, idx, src, axis=0):
    return tgt.at[idx].add(src)

def _segment_sum(src, seg, n):
    return jax.ops.segment_sum(src, seg, n)
kernel_name = 'mk_conv_attn_hybrid_d4_conv_nchw512_r4_86b449'

def setup_inputs(seed: int=0):
    np.random.seed(seed)
    _w = jnp.asarray

    def _rec_inputs():
        import jax
        import jax.numpy as jnp
        _gk = jax.random.key(seed)
        x = -0.000125 + 0.9999 * jax.random.normal(jax.random.fold_in(_gk, 1), (16, 128, 32, 32), jnp.float32)
        return x
    x = _rec_inputs()

    def _L0_conv_setup():
        import jax, jax.numpy as jnp
        import numpy as np
        from jax import lax
        EPS = 1e-05
        GROUPS = 16

        def _batchnorm(x, gamma, beta):
            m = jnp.mean(x, axis=(0, 2, 3), keepdims=True)
            v = jnp.mean((x - m) ** 2, axis=(0, 2, 3), keepdims=True)
            xhat = (x - m) * lax.rsqrt(v + EPS)
            return xhat * gamma[None, :, None, None] + beta[None, :, None, None]

        @jax.custom_vjp
        def binary_act(x):
            return jnp.sign(x)

        def _ba_fwd(x):
            return (jnp.sign(x), x)

        def _ba_bwd(x, g):
            return (jnp.clip(2.0 - 2.0 * jnp.abs(x), a_min=0.0) * g,)
        binary_act.defvjp(_ba_fwd, _ba_bwd)

        @jax.custom_vjp
        def binary_weight(w):
            return jnp.sign(w)

        def _bw_fwd(w):
            return (jnp.sign(w), w)

        def _bw_bwd(w, g):
            mask = jnp.logical_or(w >= 1.0, w <= -1.0)
            return (jnp.where(mask, 0.0, g),)
        binary_weight.defvjp(_bw_fwd, _bw_bwd)

        def _weight_scale(w):
            co = w.shape[0]
            wf = w.reshape(co, -1)
            bw = wf - jnp.mean(wf, axis=-1, keepdims=True)
            std = jnp.std(wf - jnp.mean(wf, axis=-1, keepdims=True), axis=-1, ddof=1, keepdims=True)
            bw = bw / std
            sw = jnp.mean(jnp.abs(bw), axis=-1).reshape(co, 1, 1, 1)
            return lax.stop_gradient(sw)
        key = jax.random.key(seed)
        ks = jax.random.split(key, 7)
        N, C, H, W = (16, 128, 32, 32)
        k = 3
        x = jax.random.normal(ks[0], (N, C, H, W), dtype=jnp.float32)
        conv_w = jax.random.normal(ks[1], (C, C // GROUPS, k, k), dtype=jnp.float32) * 0.1
        bn1_gamma = jnp.ones((C,), jnp.float32)
        bn1_beta = jnp.zeros((C,), jnp.float32)
        bn2_gamma = jnp.ones((C,), jnp.float32)
        bn2_beta = jnp.zeros((C,), jnp.float32)
        prelu_a = jnp.full((C,), 0.25, jnp.float32)
        return {'x': x, 'conv_w': conv_w, 'bn1_gamma': bn1_gamma, 'bn1_beta': bn1_beta, 'bn2_gamma': bn2_gamma, 'bn2_beta': bn2_beta, 'prelu_a': prelu_a}
    _L0_conv_all = _L0_conv_setup()
    _L0_conv_in = {k: v for k, v in _L0_conv_all.items() if k in ('conv_w', 'bn1_gamma', 'bn1_beta', 'bn2_gamma', 'bn2_beta', 'prelu_a')}
    del _L0_conv_all

    def _L1_conv_setup():
        import jax, jax.numpy as jnp
        import numpy as np
        DIM = 8
        HEADS = 16
        INNER = HEADS * DIM
        CIN = 128
        COUT = 128
        SCALE = 5
        G = 3 * HEADS
        EPS_ATT = 1e-15
        EPS_BN = 1e-05

        def _aggreg(qkv, w_dw, w_pw):
            y = jax.lax.conv_general_dilated(qkv, w_dw, window_strides=(1, 1), padding=[(2, 2), (2, 2)], dimension_numbers=('NCHW', 'OIHW', 'NCHW'), feature_group_count=3 * INNER)
            B, C, H, W = y.shape
            yg = y.reshape(B, G, DIM, H, W)
            out = jnp.einsum('gok,bgkhw->bgohw', w_pw, yg)
            return out.reshape(B, C, H, W)

        def _relu_linear_att(qkv):
            B, C, H, W = qkv.shape
            N = H * W
            qkv = qkv.astype(jnp.float32).reshape(B, -1, 3 * DIM, N)
            q = jax.nn.relu(qkv[:, :, :DIM])
            k = jax.nn.relu(qkv[:, :, DIM:2 * DIM])
            v = qkv[:, :, 2 * DIM:]
            v1 = jnp.concatenate([v, jnp.ones_like(v[:, :, :1])], axis=2)
            vk = jnp.einsum('bhdn,bhen->bhde', v1, k)
            out = jnp.einsum('bhde,bhen->bhdn', vk, q)
            out = out[:, :, :-1] / (out[:, :, -1:] + EPS_ATT)
            return out.reshape(B, -1, H, W)
        key = jax.random.key(seed)
        ks = jax.random.split(key, 7)
        B, H, W = (2, 32, 32)
        x = jax.random.normal(ks[0], (B, CIN, H, W), dtype=jnp.float32)
        w_qkv = jax.random.normal(ks[1], (3 * INNER, CIN), dtype=jnp.float32) * 0.02
        w_dw = jax.random.normal(ks[2], (3 * INNER, 1, SCALE, SCALE), dtype=jnp.float32) * 0.05
        w_pw = jax.random.normal(ks[3], (G, DIM, DIM), dtype=jnp.float32) * 0.1
        w_proj = jax.random.normal(ks[4], (COUT, 2 * INNER), dtype=jnp.float32) * 0.02
        bn_gamma = jnp.ones((COUT,), dtype=jnp.float32)
        bn_beta = jnp.zeros((COUT,), dtype=jnp.float32)
        return {'x': x, 'w_qkv': w_qkv, 'w_dw': w_dw, 'w_pw': w_pw, 'w_proj': w_proj, 'bn_gamma': bn_gamma, 'bn_beta': bn_beta}
    _L1_conv_all = _L1_conv_setup()
    _L1_conv_in = {k: v for k, v in _L1_conv_all.items() if k in ('w_qkv', 'w_dw', 'w_pw', 'w_proj', 'bn_gamma', 'bn_beta')}
    del _L1_conv_all

    def _L2_attn_setup():
        import jax, jax.numpy as jnp
        import numpy as np
        S, R, DH = (8, 2, 16)
        key = jax.random.key(seed)
        ks = jax.random.split(key, 7)
        b, n, dim = (2, 512, 128)

        def w(k, i, o):
            return jax.random.normal(k, (i, o), dtype=jnp.float32) / np.sqrt(i)
        return {'x': jax.random.normal(ks[0], (b, n, dim), dtype=jnp.float32), 'wq_s': w(ks[1], dim, S * DH), 'wk_s': w(ks[2], dim, S * DH), 'wv_r': w(ks[3], dim, R * DH), 'wq_r': w(ks[4], dim, S * DH), 'wk_ret': w(ks[5], DH, DH), 'w_out': w(ks[6], S * DH, dim)}
    _L2_attn_all = _L2_attn_setup()
    _L2_attn_in = {k: v for k, v in _L2_attn_all.items() if k in ('wq_s', 'wk_s', 'wv_r', 'wq_r', 'wk_ret', 'w_out')}
    del _L2_attn_all

    def _L2_ffn_setup():
        import jax, jax.numpy as jnp
        import numpy as np
        N_CONST = 6
        PARTITIONS_OF_6 = [(6,), (5, 1), (4, 2), (4, 1, 1), (3, 3), (3, 2, 1), (3, 1, 1, 1), (2, 2, 2), (2, 2, 1, 1), (2, 1, 1, 1, 1), (1, 1, 1, 1, 1, 1)]
        N_EXPERTS = 6
        TOP_K = 2

        def _partition_weights():
            w = np.zeros((len(PARTITIONS_OF_6), N_EXPERTS), dtype=np.float32)
            for i, partition in enumerate(PARTITIONS_OF_6):
                for j, part in enumerate(partition):
                    if j < N_EXPERTS:
                        w[i, j] = part / N_CONST
            return jnp.asarray(w)
        key = jax.random.key(seed)
        ks = jax.random.split(key, 6)
        B, S, D, F, E, P = (32, 512, 128, 341, 6, 11)
        scale_in = 1.0 / np.sqrt(D)
        scale_hid = 1.0 / np.sqrt(F)
        return {'x': jax.random.normal(ks[0], (B, S, D), dtype=jnp.float32), 'router_w': jax.random.normal(ks[1], (P, D), dtype=jnp.float32) * scale_in, 'W1': jax.random.normal(ks[2], (E, D, F), dtype=jnp.float32) * scale_in, 'b1': jax.random.normal(ks[3], (E, F), dtype=jnp.float32) * 0.01, 'W2': jax.random.normal(ks[4], (E, F, D), dtype=jnp.float32) * scale_hid, 'b2': jax.random.normal(ks[5], (E, D), dtype=jnp.float32) * 0.01}
    _L2_ffn_all = _L2_ffn_setup()
    _L2_ffn_in = {k: v for k, v in _L2_ffn_all.items() if k in ('router_w', 'W1', 'b1', 'W2', 'b2')}
    del _L2_ffn_all

    def _L3_attn_setup():
        import jax, jax.numpy as jnp
        import numpy as np
        B, S, D, G, H = (2, 512, 128, 8, 4)
        key = jax.random.key(seed)
        ks = jax.random.split(key, 5)
        sc = 0.02
        return {'x': jax.random.normal(ks[0], (B, S, D), jnp.float32), 'Wq': jax.random.normal(ks[1], (D, D * G * H), jnp.float32) * sc, 'bq': jnp.zeros((D * G * H,), jnp.float32), 'Wk': jax.random.normal(ks[2], (D, D * G), jnp.float32) * sc, 'bk': jnp.zeros((D * G,), jnp.float32), 'Wv': jax.random.normal(ks[3], (D, D * G), jnp.float32) * sc, 'bv': jnp.zeros((D * G,), jnp.float32), 'Wo': jax.random.normal(ks[4], (D * G, D), jnp.float32) * sc, 'bo': jnp.zeros((D,), jnp.float32)}
    _L3_attn_all = _L3_attn_setup()
    _L3_attn_in = {k: v for k, v in _L3_attn_all.items() if k in ('Wq', 'bq', 'Wk', 'bk', 'Wv', 'bv', 'Wo', 'bo')}
    del _L3_attn_all

    def _L3_ffn_setup():
        import jax, jax.numpy as jnp
        import numpy as np
        SINKHORN_ITERS = 8
        TEMPERATURE = 1.0
        EPS = 1e-10

        def sinkhorn(gates):
            t = jnp.log(jnp.clip(gates, EPS)) / TEMPERATURE

            def body(t, _):
                t = t - jax.nn.logsumexp(t, axis=-2, keepdims=True)
                t = t - jax.nn.logsumexp(t, axis=-1, keepdims=True)
                return (t, None)
            t, _ = jax.lax.scan(body, t, None, length=SINKHORN_ITERS)
            return jnp.exp(t)
        key = jax.random.key(seed)
        k1, k2, k3 = jax.random.split(key, 3)
        b, n, d, e, h = (4, 2048, 128, 8, 1)
        x = jax.random.normal(k1, (b, n, d), dtype=jnp.float32)
        gate_w = jax.random.normal(k2, (h, d, e), dtype=jnp.float32)
        experts = jax.random.normal(k3, (e, d, d), dtype=jnp.float32) / np.sqrt(d)
        return {'x': x, 'gate_w': gate_w, 'experts': experts}
    _L3_ffn_all = _L3_ffn_setup()
    _L3_ffn_in = {k: v for k, v in _L3_ffn_all.items() if k in ('gate_w', 'experts')}
    del _L3_ffn_all
    return {'x': x, 'L0_conv_conv_w': _L0_conv_in['conv_w'], 'L0_conv_bn1_gamma': _L0_conv_in['bn1_gamma'], 'L0_conv_bn1_beta': _L0_conv_in['bn1_beta'], 'L0_conv_bn2_gamma': _L0_conv_in['bn2_gamma'], 'L0_conv_bn2_beta': _L0_conv_in['bn2_beta'], 'L0_conv_prelu_a': _L0_conv_in['prelu_a'], 'L1_conv_w_qkv': _L1_conv_in['w_qkv'], 'L1_conv_w_dw': _L1_conv_in['w_dw'], 'L1_conv_w_pw': _L1_conv_in['w_pw'], 'L1_conv_w_proj': _L1_conv_in['w_proj'], 'L1_conv_bn_gamma': _L1_conv_in['bn_gamma'], 'L1_conv_bn_beta': _L1_conv_in['bn_beta'], 'L2_attn_wq_s': _L2_attn_in['wq_s'], 'L2_attn_wk_s': _L2_attn_in['wk_s'], 'L2_attn_wv_r': _L2_attn_in['wv_r'], 'L2_attn_wq_r': _L2_attn_in['wq_r'], 'L2_attn_wk_ret': _L2_attn_in['wk_ret'], 'L2_attn_w_out': _L2_attn_in['w_out'], 'L2_ffn_router_w': _L2_ffn_in['router_w'], 'L2_ffn_W1': _L2_ffn_in['W1'], 'L2_ffn_b1': _L2_ffn_in['b1'], 'L2_ffn_W2': _L2_ffn_in['W2'], 'L2_ffn_b2': _L2_ffn_in['b2'], 'L3_attn_Wq': _L3_attn_in['Wq'], 'L3_attn_bq': _L3_attn_in['bq'], 'L3_attn_Wk': _L3_attn_in['Wk'], 'L3_attn_bk': _L3_attn_in['bk'], 'L3_attn_Wv': _L3_attn_in['Wv'], 'L3_attn_bv': _L3_attn_in['bv'], 'L3_attn_Wo': _L3_attn_in['Wo'], 'L3_attn_bo': _L3_attn_in['bo'], 'L3_ffn_gate_w': _L3_ffn_in['gate_w'], 'L3_ffn_experts': _L3_ffn_in['experts']}

def reference(x, L0_conv_conv_w, L0_conv_bn1_gamma, L0_conv_bn1_beta, L0_conv_bn2_gamma, L0_conv_bn2_beta, L0_conv_prelu_a, L1_conv_w_qkv, L1_conv_w_dw, L1_conv_w_pw, L1_conv_w_proj, L1_conv_bn_gamma, L1_conv_bn_beta, L2_attn_wq_s, L2_attn_wk_s, L2_attn_wv_r, L2_attn_wq_r, L2_attn_wk_ret, L2_attn_w_out, L2_ffn_router_w, L2_ffn_W1, L2_ffn_b1, L2_ffn_W2, L2_ffn_b2, L3_attn_Wq, L3_attn_bq, L3_attn_Wk, L3_attn_bk, L3_attn_Wv, L3_attn_bv, L3_attn_Wo, L3_attn_bo, L3_ffn_gate_w, L3_ffn_experts):
    import jax
    import jax.numpy as jnp

    def _L0_conv_ref(x, conv_w, bn1_gamma, bn1_beta, bn2_gamma, bn2_beta, prelu_a):
        import jax, jax.numpy as jnp
        import numpy as np
        from jax import lax
        EPS = 1e-05
        GROUPS = 16

        def _batchnorm(x, gamma, beta):
            m = jnp.mean(x, axis=(0, 2, 3), keepdims=True)
            v = jnp.mean((x - m) ** 2, axis=(0, 2, 3), keepdims=True)
            xhat = (x - m) * lax.rsqrt(v + EPS)
            return xhat * gamma[None, :, None, None] + beta[None, :, None, None]

        @jax.custom_vjp
        def binary_act(x):
            return jnp.sign(x)

        def _ba_fwd(x):
            return (jnp.sign(x), x)

        def _ba_bwd(x, g):
            return (jnp.clip(2.0 - 2.0 * jnp.abs(x), a_min=0.0) * g,)
        binary_act.defvjp(_ba_fwd, _ba_bwd)

        @jax.custom_vjp
        def binary_weight(w):
            return jnp.sign(w)

        def _bw_fwd(w):
            return (jnp.sign(w), w)

        def _bw_bwd(w, g):
            mask = jnp.logical_or(w >= 1.0, w <= -1.0)
            return (jnp.where(mask, 0.0, g),)
        binary_weight.defvjp(_bw_fwd, _bw_bwd)

        def _weight_scale(w):
            co = w.shape[0]
            wf = w.reshape(co, -1)
            bw = wf - jnp.mean(wf, axis=-1, keepdims=True)
            std = jnp.std(wf - jnp.mean(wf, axis=-1, keepdims=True), axis=-1, ddof=1, keepdims=True)
            bw = bw / std
            sw = jnp.mean(jnp.abs(bw), axis=-1).reshape(co, 1, 1, 1)
            return lax.stop_gradient(sw)
        res = x
        h = _batchnorm(x, bn1_gamma, bn1_beta)
        h = binary_act(h)
        sw = _weight_scale(conv_w)
        bw = binary_weight(conv_w) * sw
        h = lax.conv_general_dilated(h, bw, window_strides=(1, 1), padding=((1, 1), (1, 1)), feature_group_count=GROUPS, dimension_numbers=('NCHW', 'OIHW', 'NCHW'))
        h = _batchnorm(h, bn2_gamma, bn2_beta)
        h = h + res
        a = prelu_a[None, :, None, None]
        return jnp.where(h > 0, h, a * h)

    def _L1_conv_ref(x, w_qkv, w_dw, w_pw, w_proj, bn_gamma, bn_beta):
        import jax, jax.numpy as jnp
        import numpy as np
        DIM = 8
        HEADS = 16
        INNER = HEADS * DIM
        CIN = 128
        COUT = 128
        SCALE = 5
        G = 3 * HEADS
        EPS_ATT = 1e-15
        EPS_BN = 1e-05

        def _aggreg(qkv, w_dw, w_pw):
            y = jax.lax.conv_general_dilated(qkv, w_dw, window_strides=(1, 1), padding=[(2, 2), (2, 2)], dimension_numbers=('NCHW', 'OIHW', 'NCHW'), feature_group_count=3 * INNER)
            B, C, H, W = y.shape
            yg = y.reshape(B, G, DIM, H, W)
            out = jnp.einsum('gok,bgkhw->bgohw', w_pw, yg)
            return out.reshape(B, C, H, W)

        def _relu_linear_att(qkv):
            B, C, H, W = qkv.shape
            N = H * W
            qkv = qkv.astype(jnp.float32).reshape(B, -1, 3 * DIM, N)
            q = jax.nn.relu(qkv[:, :, :DIM])
            k = jax.nn.relu(qkv[:, :, DIM:2 * DIM])
            v = qkv[:, :, 2 * DIM:]
            v1 = jnp.concatenate([v, jnp.ones_like(v[:, :, :1])], axis=2)
            vk = jnp.einsum('bhdn,bhen->bhde', v1, k)
            out = jnp.einsum('bhde,bhen->bhdn', vk, q)
            out = out[:, :, :-1] / (out[:, :, -1:] + EPS_ATT)
            return out.reshape(B, -1, H, W)
        residual = x
        qkv = jnp.einsum('oc,bchw->bohw', w_qkv, x)
        qkv_ms = jnp.concatenate([qkv, _aggreg(qkv, w_dw, w_pw)], axis=1)
        out = _relu_linear_att(qkv_ms).astype(qkv_ms.dtype)
        out = jnp.einsum('oc,bchw->bohw', w_proj, out)
        mean = jnp.mean(out, axis=(0, 2, 3), keepdims=True)
        var = jnp.var(out, axis=(0, 2, 3), keepdims=True)
        out = (out - mean) * jax.lax.rsqrt(var + EPS_BN)
        out = out * bn_gamma[None, :, None, None] + bn_beta[None, :, None, None]
        return out + residual

    def _L2_attn_ref(x, wq_s, wk_s, wv_r, wq_r, wk_ret, w_out):
        import jax, jax.numpy as jnp
        import numpy as np
        S, R, DH = (8, 2, 16)
        b, n, dim = x.shape
        scale = DH ** (-0.5)
        sq = (x @ wq_s).reshape(b, n, S, DH).transpose(0, 2, 1, 3) * scale
        sk = (x @ wk_s).reshape(b, n, S, DH).transpose(0, 2, 1, 3)
        rv = (x @ wv_r).reshape(b, n, R, DH).transpose(0, 2, 1, 3)
        search_sim = jnp.einsum('bsid,bsjd->bsij', sq, sk)
        search_attn = jax.nn.softmax(search_sim, axis=-1)
        retrieved = jnp.einsum('bsij,brjd->bsird', search_attn, rv)
        rq = (x @ wq_r).reshape(b, n, S, DH).transpose(0, 2, 1, 3) * scale
        rk = retrieved @ wk_ret
        retrieval_sim = jnp.einsum('bsid,bsird->bsir', rq, rk)
        retrieval_attn = jax.nn.softmax(retrieval_sim, axis=-1)
        out = jnp.einsum('bsir,bsird->bsid', retrieval_attn, retrieved)
        out = out.transpose(0, 2, 1, 3).reshape(b, n, S * DH)
        return out @ w_out

    def _L2_ffn_ref(x, router_w, W1, b1, W2, b2):
        import jax, jax.numpy as jnp
        import numpy as np
        N_CONST = 6
        PARTITIONS_OF_6 = [(6,), (5, 1), (4, 2), (4, 1, 1), (3, 3), (3, 2, 1), (3, 1, 1, 1), (2, 2, 2), (2, 2, 1, 1), (2, 1, 1, 1, 1), (1, 1, 1, 1, 1, 1)]
        N_EXPERTS = 6
        TOP_K = 2

        def _partition_weights():
            w = np.zeros((len(PARTITIONS_OF_6), N_EXPERTS), dtype=np.float32)
            for i, partition in enumerate(PARTITIONS_OF_6):
                for j, part in enumerate(partition):
                    if j < N_EXPERTS:
                        w[i, j] = part / N_CONST
            return jnp.asarray(w)
        pw = _partition_weights()
        token_repr = x.mean(axis=1)
        logits = token_repr @ router_w.T
        probs = jax.nn.softmax(logits, axis=-1)
        topk_vals, topk_idx = jax.lax.top_k(probs, TOP_K)
        topk_vals = topk_vals / topk_vals.sum(axis=-1, keepdims=True)
        expert_weights = jnp.einsum('bk,bke->be', topk_vals, pw[topk_idx])
        expert_weights = jnp.where(expert_weights > 1e-06, expert_weights, 0.0)
        h = jax.nn.gelu(jnp.einsum('bsd,edf->ebsf', x, W1) + b1[:, None, None, :], approximate=False)
        out_e = jnp.einsum('ebsf,efd->ebsd', h, W2) + b2[:, None, None, :]
        return jnp.einsum('be,ebsd->bsd', expert_weights, out_e)

    def _L3_attn_ref(x, Wq, bq, Wk, bk, Wv, bv, Wo, bo):
        import jax, jax.numpy as jnp
        import numpy as np
        B, S, D, G, H = (2, 512, 128, 8, 4)
        b, s, d = x.shape
        q = (x @ Wq + bq).reshape(b, s, G, H, d)
        k = (x @ Wk + bk).reshape(b, s, G, d)
        v = (x @ Wv + bv).reshape(b, s, G, d)
        scores = jnp.einsum('bqghd,bkgd->bqhg', q, k) / jnp.sqrt(jnp.float32(d))
        weights = jax.nn.softmax(scores, axis=-1)
        out = jnp.einsum('bqhg,bsgd->bsgd', weights, v).reshape(b, s, G * d)
        return out @ Wo + bo

    def _L3_ffn_ref(x, gate_w, experts):
        import jax, jax.numpy as jnp
        import numpy as np
        SINKHORN_ITERS = 8
        TEMPERATURE = 1.0
        EPS = 1e-10

        def sinkhorn(gates):
            t = jnp.log(jnp.clip(gates, EPS)) / TEMPERATURE

            def body(t, _):
                t = t - jax.nn.logsumexp(t, axis=-2, keepdims=True)
                t = t - jax.nn.logsumexp(t, axis=-1, keepdims=True)
                return (t, None)
            t, _ = jax.lax.scan(body, t, None, length=SINKHORN_ITERS)
            return jnp.exp(t)
        b, n, d = x.shape
        h = gate_w.shape[0]
        e = experts.shape[0]
        N = b * n
        m = n // e
        x4 = x[:, None]
        gates = jnp.einsum('bhnd,hde->bhne', x4, gate_w)
        xf = jnp.transpose(x4, (1, 0, 2, 3)).reshape(h, N, d)
        gf = jnp.transpose(gates, (1, 0, 2, 3)).reshape(h, N, e)
        cg = sinkhorn(gf)
        vals, idx = jax.lax.top_k(jnp.transpose(cg, (0, 2, 1)), m)
        gate_values = (vals > 0.5).astype(x.dtype)
        gate_values = jnp.transpose(gate_values, (0, 2, 1))
        idx = jnp.transpose(idx, (0, 2, 1))
        routed = xf[jnp.arange(h)[:, None, None], idx]
        outputs = jnp.einsum('hmei,eio->hmeo', routed, experts)
        outputs = outputs * gate_values[..., None]
        o_dim = outputs.shape[-1]
        src = outputs.reshape(h, m * e, o_dim)
        idx_flat = idx.reshape(h, m * e)

        def combine(idxf, srcf):
            s = jnp.zeros((N, o_dim), srcf.dtype).at[idxf].add(srcf)
            c = jnp.zeros((N,), srcf.dtype).at[idxf].add(1.0)
            return s / (c + 1.0)[:, None]
        out = jax.vmap(combine)(idx_flat, src)
        out = out.reshape(h, b, n, o_dim)
        out = jnp.transpose(out, (1, 0, 2, 3))[:, 0]
        return out

    def _gn(v, G=32, eps=1e-05):
        B_, C_, H_, W_ = v.shape
        g = v.reshape(B_, G, C_ // G, H_, W_)
        m = jnp.mean(g, axis=(2, 3, 4), keepdims=True)
        s = jnp.var(g, axis=(2, 3, 4), keepdims=True)
        return ((g - m) / jnp.sqrt(s + eps)).reshape(v.shape)

    def _ln_c(v, eps=1e-06):
        m = jnp.mean(v, axis=1, keepdims=True)
        s = jnp.var(v, axis=1, keepdims=True)
        return (v - m) / jnp.sqrt(s + eps)

    def _ln_t(v, eps=1e-05):
        m = jnp.mean(v, axis=-1, keepdims=True)
        s = jnp.var(v, axis=-1, keepdims=True)
        return (v - m) / jnp.sqrt(s + eps)

    def _to_tokens(v):
        B_, C_, H_, W_ = v.shape
        return v.reshape(B_, C_, H_ * W_).transpose(0, 2, 1)

    def _from_tokens(t, like):
        B_, C_, H_, W_ = like.shape
        return t.transpose(0, 2, 1).reshape(B_, C_, H_, W_)
    x = x + _L0_conv_ref(_gn(x), L0_conv_conv_w, L0_conv_bn1_gamma, L0_conv_bn1_beta, L0_conv_bn2_gamma, L0_conv_bn2_beta, L0_conv_prelu_a)
    x = _L1_conv_ref(x, L1_conv_w_qkv, L1_conv_w_dw, L1_conv_w_pw, L1_conv_w_proj, L1_conv_bn_gamma, L1_conv_bn_beta)
    t = _to_tokens(x)
    t = t + _L2_attn_ref(_ln_t(t), L2_attn_wq_s, L2_attn_wk_s, L2_attn_wv_r, L2_attn_wq_r, L2_attn_wk_ret, L2_attn_w_out)
    t = t + _L2_ffn_ref(_ln_t(t), L2_ffn_router_w, L2_ffn_W1, L2_ffn_b1, L2_ffn_W2, L2_ffn_b2)
    t = t + _L3_attn_ref(_ln_t(t), L3_attn_Wq, L3_attn_bq, L3_attn_Wk, L3_attn_bk, L3_attn_Wv, L3_attn_bv, L3_attn_Wo, L3_attn_bo)
    t = t + _L3_ffn_ref(_ln_t(t), L3_ffn_gate_w, L3_ffn_experts)
    x = _from_tokens(t, x)
    return x

_drawn_inputs = setup_inputs


def setup_inputs(seed=0):
    import zlib

    import numpy as np

    out = dict(_drawn_inputs(seed))
    spreads = {'L0_conv_bn1_gamma': (1.0, 0.2),
     'L0_conv_bn1_beta': (0.0, 0.1),
     'L0_conv_bn2_gamma': (1.0, 0.2),
     'L0_conv_bn2_beta': (0.0, 0.1),
     'L0_conv_prelu_a': (0.25, 0.2),
     'L1_conv_bn_gamma': (1.0, 0.2),
     'L1_conv_bn_beta': (0.0, 0.1),
     'L3_attn_bq': (0.0, 0.1),
     'L3_attn_bk': (0.0, 0.1),
     'L3_attn_bv': (0.0, 0.1),
     'L3_attn_bo': (0.0, 2.0)}
    factors = {'L2_attn_wq_r': 3.975,
     'L2_attn_wk_ret': 3.975,
     'L2_ffn_b1': 24.467,
     'L2_ffn_b2': 8.0,
     'L3_ffn_gate_w': 38.997,
     'L3_ffn_experts': 38.967}
    for name, (base, spread) in spreads.items():
        noise = np.random.default_rng([zlib.crc32(name.encode()), seed]).standard_normal(out[name].shape)
        drawn = base * np.exp(spread * noise) if base else spread * noise
        out[name] = jnp.asarray(drawn.astype(out[name].dtype))
    for name, factor in factors.items():
        out[name] = (out[name] * factor).astype(out[name].dtype)
    return out
```

```python
from contextlib import ExitStack

import concourse.bass as bass
from concourse import mybir

F32 = mybir.dt.float32
BF16 = mybir.dt.bfloat16
ALU = mybir.AluOpType
ACT = mybir.ActivationFunctionType
AX = mybir.AxisListType

C = 128
B = 16
HW = 32
N = HW * HW
T = B * N
CH = 512
NCH = T // CH
EPS = 1e-5


class Chain:

    def __init__(self, eng, sem, base=0):
        self.eng, self.sem, self.base, self.n = eng, sem, base, 0

    def __call__(self, ins):
        self.n += 1
        ins.then_inc(self.sem, 1)
        self.eng.wait_ge(self.sem, self.base + self.n)


class Mem:

    def __init__(self, nc, tag):
        self.nc, self.tag, self.ctx, self.sems = nc, tag, ExitStack(), []

    def __enter__(self):
        return self

    def __exit__(self, *e):
        if self.sems:
            self.nc.clear_and_free_semaphores(self.sems)
            self.nc.all_engine_barrier()
        return self.ctx.__exit__(*e)

    def sb(self, name, shape, dt=F32):
        return self.ctx.enter_context(self.nc.sbuf_tensor(f"{self.tag}_{name}", shape, dt))

    def ps(self, name, shape, dt=F32):
        return self.ctx.enter_context(self.nc.psum_tensor(f"{self.tag}_{name}", shape, dt))

    def sem(self, name):
        self.sems.append(self.nc.alloc_semaphore(f"{self.tag}_{name}"))
        return self.sems[-1]

    def block(self):
        return self.ctx.enter_context(self.nc.Block())


def col(v):
    return v.rearrange("(p o) -> p o", o=1)


def block_mask(g, out, k):
    cols = out.shape[1]
    view = out.rearrange("p (b k) -> p b k", k=k)
    keep = dict(compare_op=ALU.is_ge, fill=0.0)
    return (lambda: g.affine_select(out=view, in_=view, pattern=[[-k, cols // k], [0, k]],
                                    base=0, channel_multiplier=1, **keep),
            lambda: g.affine_select(out=view, in_=view, pattern=[[k, cols // k], [0, k]],
                                    base=k - 1, channel_multiplier=-1, **keep))


def phase_constants(nc, K):
    with Mem(nc, "const") as m:
        s = m.sem("step")
        with nc.Block() as block:
            @block.gpsimd
            def _(g):
                step = Chain(g, s)
                step(g.memset(K["ident"][:, :], 1.0))
                step(g.memset(K["ones"][:, :], 1.0))
                step(g.memset(K["neghalf"][:, :], -0.5))
                step(g.memset(K["eps"][:, :], EPS))
                step(g.memset(K["negone"][:, :], -1.0))
                step(g.memset(K["mask8"][:, :], 1.0))
                for one in block_mask(g, K["ident"][:, :], 1):
                    step(one())
                for one in block_mask(g, K["mask8"][:, :], 8):
                    step(one())


def rsqrt_eps(g, step, K, out, var, eps):
    n = out.shape[-1]
    step(g.tensor_scalar(out, var, float(eps), None, ALU.add))
    step(g.tensor_tensor(out, out, K["neghalf"][:, 0:n], ALU.pow))


def phase_conv(nc, K, D, X):
    P = HW + 2
    TAPS = 9
    CIN = 8
    NW = CIN * TAPS
    with Mem(nc, "conv") as m:
        Y = m.sb("Y", [C, T])
        stats = K["stats"]
        mv = m.sb("mv", [C, B, 2])
        gmask = m.sb("gmask", [C, C])
        sm = m.sb("small", [C, 20, B])
        cv = m.sb("colv", [C, 16])
        wrow = m.sb("wrow", [C, NW])
        wtmp = m.sb("wtmp", [C, NW])
        wtap = m.sb("wtap", [C, TAPS, C])
        wsig = m.sb("wsig", [C, TAPS, C], BF16)
        par = m.sb("par", [C, 5])
        img = [m.sb(f"img{u}", [C, P, P], BF16) for u in range(2)]
        pg = m.ps("pg", [C, 2, B])
        acc = [m.ps(f"acc{u}", [C, CH]) for u in range(2)]
        x_in = [m.sem(f"x_in{q}") for q in range(4)]
        par_in = m.sem("par_in")
        pool = m.sem("pool")
        vec = m.sem("vec")
        act = m.sem("act")
        pe_s = m.sem("pe")
        coef1_ready = m.sem("coef1_ready")
        mean_ready, dev_ready, v1_ready, v2_ready = (m.sem(x) for x in ("mean_ready", "dev_ready", "v1_ready", "v2_ready"))
        rg_ready, s1_ready, s2_ready, sw_ready = (m.sem(x) for x in ("rg_ready", "s1_ready", "s2_ready", "sw_ready"))
        wvar_ready = m.sem("wvar_ready")
        mask_ready = m.sem("mask_ready")
        img_ready = m.sem("img_ready")
        acc_ready, stat_done, acc_saved = m.sem("acc_ready"), m.sem("stat_done"), m.sem("acc_saved")
        wsig_ready = m.sem("wsig_ready")
        border_ready = m.sem("border_ready")
        coef2_ready = m.sem("coef2_ready")
        lin_ready, sum_ready, negpart_ready = m.sem("lin_ready"), m.sem("sum_ready"), m.sem("negpart_ready")
        res_ready = m.sem("res_ready")
        negpart = [m.sb(f"negpart{u}", [C, N]) for u in range(2)]
        G1, B1v, G2, B2v, PA = (par[:, i:i + 1] for i in range(5))
        MEAN, VAR = mv[:, :, 0], mv[:, :, 1]
        MG, VG, DEV, T0, RG, RDEV, RV, C0, A1, BB1, T2, T1 = (sm[:, i, :] for i in range(12))
        M1, V1, S1, MC, VC, S2, SW, WM, WV, WR, V2, T2C, TC, ONEMA = (cv[:, i:i + 1] for i in range(14))
        csum = m.sb("csum", [C, 2])

        with nc.Block() as block:
            @block.sync
            def _(sp):
                for q in range(4):
                    sp.dma_start(X[:, q * 4 * N:(q + 1) * 4 * N].rearrange("c (b n) -> c b n", n=N),
                                 D["x"][4 * q:4 * q + 4].rearrange("b c n -> c b n")).then_inc(x_in[q], 16)

            @block.gpsimd
            def _(g):
                for i, name in enumerate(("bn1_gamma", "bn1_beta", "bn2_gamma", "bn2_beta", "prelu_a")):
                    g.dma_start(par[:, i:i + 1], col(D["L0_conv_" + name])).then_inc(par_in, 16)
                g.dma_start(wrow[:, :], D["conv_w"]).then_inc(par_in, 16)
                g.dma_start(wtap[:, :, :], D["conv_wt"]).then_inc(par_in, 16)
                step = Chain(g, pool)
                step(g.memset(gmask[:, :], 0.25))
                for one in block_mask(g, gmask[:, :], 4):
                    last = one()
                    step(last)
                g.sem_inc(mask_ready, 1)
                g.memset(img[0][:, :, :], 0.0).then_inc(border_ready, 1)
                g.memset(img[1][:, :, :], 0.0).then_inc(border_ready, 1)
                g.wait_ge(dev_ready, 2)
                rsqrt_eps(g, step, K, RG, VG, EPS)
                g.sem_inc(rg_ready, 1)
                g.wait_ge(v1_ready, 1)
                rsqrt_eps(g, step, K, S1, V1, EPS)
                g.sem_inc(s1_ready, 1)
                g.wait_ge(wvar_ready, 1)
                rsqrt_eps(g, step, K, WR, WV, 0.0)
                g.sem_inc(sw_ready, 1)
                g.wait_ge(v2_ready, 1)
                rsqrt_eps(g, step, K, S2, V2, EPS)
                g.sem_inc(s2_ready, 1)

            @block.tensor
            def _(pe):
                pe.wait_ge(mask_ready, 1)
                pe.wait_ge(mean_ready, 1)
                pe.matmul(pg[:, 0, :], gmask[:, :], T1, start=True, stop=True).then_inc(pe_s, 1)
                pe.wait_ge(dev_ready, 1)
                pe.matmul(pg[:, 1, :], gmask[:, :], T0, start=True, stop=True).then_inc(pe_s, 1)
                pe.wait_ge(wsig_ready, 1)

                with pe.Fori(0, B // 2) as i:
                    for u in range(2):
                        pe.wait_ge(img_ready, 2 * i + u + 1)
                        for h in range(2):
                            pe.wait_ge(acc_saved, 4 * i + 2 * u + h - 1 + 2)
                            for t in range(TAPS):
                                dy, dx = divmod(t, 3)
                                last = pe.matmul(acc[h][:, :], wsig[:, t, :],
                                                 img[u][:, 16 * h + dy:16 * h + dy + 16, dx:dx + HW],
                                                 start=(t == 0), stop=(t == TAPS - 1))
                            last.then_inc(acc_ready, 1)

            @block.vector
            def _(v):
                step = Chain(v, vec)
                for q in range(4):
                    v.wait_ge(x_in[q], 16)
                    for b in range(4 * q, 4 * q + 4):
                        for h in range(2):
                            last = v.bn_stats(stats[:, 2 * b + h, :], X[:, b * N + h * CH:b * N + (h + 1) * CH])
                        step(last)
                        step(v.bn_aggr(mv[:, b, :], stats[:, 2 * b:2 * b + 2, :]))
                step(v.tensor_copy(T1, MEAN))
                v.sem_inc(mean_ready, 1)
                v.wait_ge(pe_s, 1)
                step(v.tensor_copy(MG, pg[:, 0, :]))
                step(v.tensor_sub(DEV, MEAN, MG))
                step(v.tensor_mul(T0, DEV, DEV))
                step(v.tensor_add(T0, T0, VAR))
                v.sem_inc(dev_ready, 1)
                v.wait_ge(pe_s, 2)
                step(v.tensor_copy(VG, pg[:, 1, :]))
                v.sem_inc(dev_ready, 1)
                v.wait_ge(rg_ready, 1)
                v.wait_ge(par_in, 7 * 16)
                step(v.tensor_mul(RDEV, RG, DEV))
                step(v.tensor_mul(C0, RG, MG))
                step(v.tensor_scalar(C0, C0, -1.0, None, ALU.mult))
                step(v.reduce_sum(M1, RDEV, AX.X))
                step(v.tensor_scalar(M1, M1, 1.0 / B, None, ALU.mult))
                step(v.tensor_scalar(RDEV, RDEV, M1, None, ALU.subtract))
                step(v.tensor_mul(RDEV, RDEV, RDEV))
                step(v.tensor_mul(RV, RG, RG))
                step(v.tensor_mul(RV, RV, VAR))
                step(v.tensor_add(RV, RV, RDEV))
                step(v.reduce_sum(V1, RV, AX.X))
                step(v.tensor_scalar(V1, V1, 1.0 / B, None, ALU.mult))
                v.sem_inc(v1_ready, 1)
                v.wait_ge(s1_ready, 1)
                step(v.tensor_mul(S1, S1, G1))
                step(v.tensor_scalar(A1, RG, S1, None, ALU.mult))
                step(v.tensor_scalar(BB1, C0, M1, S1, ALU.subtract, ALU.mult))
                step(v.tensor_scalar(BB1, BB1, B1v, None, ALU.add))
                v.sem_inc(coef1_ready, 1)
                v.wait_ge(act, 1)
                v.tensor_tensor(wsig[:, :, :], wtap[:, :, :],
                                K["mask8"][:, :].rearrange("p (o c) -> p o c", o=1).to_broadcast([C, TAPS, C]),
                                ALU.mult).then_inc(wsig_ready, 1)
                step(v.reduce_sum(WM, wrow[:, :], AX.X))
                step(v.tensor_scalar(WM, WM, 1.0 / NW, None, ALU.mult))
                step(v.tensor_scalar(wrow[:, :], wrow[:, :], WM, None, ALU.subtract))
                step(v.reduce_sum(WM, wrow[:, :], AX.X))
                step(v.tensor_scalar(WM, WM, 1.0 / NW, None, ALU.mult))
                step(v.tensor_scalar(wtmp[:, :], wrow[:, :], WM, None, ALU.subtract))
                step(v.tensor_mul(wtmp[:, :], wtmp[:, :], wtmp[:, :]))
                step(v.reduce_sum(WV, wtmp[:, :], AX.X))
                step(v.tensor_scalar(WV, WV, 1.0 / (NW - 1), None, ALU.mult))
                v.sem_inc(wvar_ready, 1)
                step(v.tensor_reduce(SW, wrow[:, :], AX.X, ALU.add, apply_absolute_value=True))
                step(v.tensor_scalar(SW, SW, 1.0 / NW, None, ALU.mult))
                v.wait_ge(sw_ready, 1)
                step(v.tensor_mul(SW, SW, WR))
                with v.Fori(0, NCH // 2) as i:
                    for h in range(2):
                        v.wait_ge(acc_saved, 2 * i + h + 1 + 2)
                        v.bn_stats(stats[:, bass.ds(2 * i + h, 1), :],
                                   Y[:, bass.ds((2 * i + h) * CH, CH)]).then_inc(stat_done, 1)
                v.wait_ge(stat_done, NCH)
                step(v.bn_aggr(csum[:, :], stats[:, :, :]))
                step(v.tensor_mul(V2, csum[:, 1:2], SW))
                step(v.tensor_mul(V2, V2, SW))
                v.sem_inc(v2_ready, 1)
                v.wait_ge(s2_ready, 1)
                step(v.tensor_mul(S2, S2, SW))
                step(v.tensor_mul(S2, S2, G2))
                step(v.tensor_mul(TC, csum[:, 0:1], S2))
                step(v.tensor_sub(T2C, B2v, TC))
                step(v.tensor_scalar(ONEMA, PA, -1.0, 1.0, ALU.mult, ALU.add))
                step(v.tensor_scalar(T2, C0, T2C, None, ALU.add))
                v.sem_inc(coef2_ready, 1)
                with v.Fori(0, B // 2) as i:
                    for u in range(2):
                        b = 2 * i + u
                        xb, yb = X[:, bass.ds(b * N, N)], Y[:, bass.ds(b * N, N)]
                        v.wait_ge(lin_ready, b + 1)
                        v.scalar_tensor_tensor(yb, xb, sm[:, 4, bass.ds(b, 1)], yb, ALU.mult, ALU.add)\
                         .then_inc(sum_ready, 1)
                        v.wait_ge(sum_ready, 2 * b + 1)
                        v.tensor_add(xb, xb, yb).then_inc(sum_ready, 1)
                        v.wait_ge(sum_ready, 2 * b + 2)
                        v.wait_ge(negpart_ready, b + 1)
                        v.scalar_tensor_tensor(xb, negpart[u][:, :], ONEMA, xb, ALU.mult, ALU.add)\
                         .then_inc(res_ready, 1)

            @block.scalar
            def _(a):
                a.wait_ge(par_in, 7 * 16)
                a.activation(wtap[:, :, :], wtap[:, :, :], ACT.Sign).then_inc(act, 1)
                a.wait_ge(coef1_ready, 1)
                a.wait_ge(border_ready, 2)
                a.sem_inc(acc_saved, 2)

                def signs(b, u):
                    a.activation(img[u][:, 1:HW + 1, 1:HW + 1],
                                 X[:, bass.ds(b * N, N)].rearrange("c (y x) -> c y x", x=HW), ACT.Sign,
                                 bias=sm[:, 9, bass.ds(b, 1)], scale=sm[:, 8, bass.ds(b, 1)]).then_inc(img_ready, 1)

                def save(b, h):
                    a.wait_ge(acc_ready, 2 * b + h + 1)
                    a.copy(Y[:, bass.ds(b * N + h * CH, CH)], acc[h][:, :]).then_inc(acc_saved, 1)

                signs(0, 0)
                signs(1, 1)
                with a.Fori(0, B // 2 - 1) as i:
                    for u in range(2):
                        save(2 * i + u, 0)
                        save(2 * i + u, 1)
                        signs(2 * i + u + 2, u)
                for b in (B - 2, B - 1):
                    save(b, 0)
                    save(b, 1)
                a.wait_ge(coef2_ready, 1)

                def affine(b):
                    yb = Y[:, bass.ds(b * N, N)]
                    a.activation(yb, yb, ACT.Identity, bias=sm[:, 10, bass.ds(b, 1)], scale=S2).then_inc(lin_ready, 1)

                def negative_part(b, u):
                    a.wait_ge(sum_ready, 2 * b + 1)
                    a.activation(negpart[u][:, :], Y[:, bass.ds(b * N, N)], ACT.Relu, scale=-1.0)\
                     .then_inc(negpart_ready, 1)

                affine(0)
                affine(1)
                for b in (0, 1):
                    negative_part(b, b)
                    affine(b + 2)
                with a.Fori(1, B // 2 - 1) as i:
                    for u in range(2):
                        a.wait_ge(res_ready, 2 * i + u - 1)
                        negative_part(2 * i + u, u)
                        affine(2 * i + u + 2)
                for b in (B - 2, B - 1):
                    a.wait_ge(res_ready, b - 1)
                    negative_part(b, b % 2)



HD = 8
PARTS = 3
SIDE = 36
PATTERN = ((0, 0), (0, 1), (0, 3), (1, 3))
PLACES = ((0, 1), (0, 0), (1, -1), (1, 1), (2, 0), (3, -1), (3, 1), (4, 0))
NG = len(PLACES)
SHIFTS = tuple(SIDE * y + x for y, x in PATTERN)
MARGIN = 1
REP = SIDE * SIDE + 2
PAD = MARGIN + REP + max(SHIFTS) + 2
EPS_ATT = 1e-15


def tap_weights(w_dw):
    import numpy as np
    w = w_dw.reshape(16, PARTS, HD, 5, 5).transpose(1, 0, 2, 3, 4).reshape(PARTS, 4, 32, 5, 5)
    w = w[1:]
    out = np.zeros((4, 32, 2, 4, NG), w.dtype)
    seen = set()
    for g, (gy, gx) in enumerate(PLACES):
        for t, (py, px) in enumerate(PATTERN):
            y, x = gy + py, gx + px
            if 0 <= y < 5 and 0 <= x < 5 and (y, x) not in seen:
                seen.add((y, x))
                out[t, :, :, :, g] = w[:, :, :, y, x].transpose(2, 0, 1)
    assert len(seen) == 25
    return out.reshape(C, 2, 4, NG)


def wait_if(eng, sem, value):
    if not isinstance(value, int) or value > 0:
        eng.wait_ge(sem, value)


def over_batches(eng, batch):
    batch(0, 0, 0)
    batch(1, 1, 0)
    with eng.Fori(1, B // 2 - 1) as i:
        for u in range(2):
            batch(2 * i + u, u, 0)
    batch(B - 2, 0, 0)
    batch(B - 1, 1, 1)


SLOT = {0: [("tp", "agg", 0)], 1: [("tp", "agg", 1)], 2: [("tp", "agg", 2)], 3: [("tp", "agg", 3)],
        5: [("vk", "agg")], 7: [("den",), ("nb", 0)],
        8: [("tp", "base", 0)], 9: [("tp", "base", 1)], 10: [("tp", "base", 2)], 11: [("tp", "base", 3)],
        14: [("rb", 0)], 16: [("nb", 1), ("rb", 1)], 18: [("nb", 2)], 19: [("y", 0), ("rb", 2)],
        21: [("nb", 3), ("rb", 3)], 22: [("tp", "base", 4)], 23: [("tp", "base", 5)], 24: [("y", 1)],
        26: [("vk", "base")]}
BASE_STEPS = [s for g in sorted(SLOT) for s in SLOT[g] if "base" in s]
OUTPUTS = [s for g in sorted(SLOT) for s in SLOT[g] if "base" not in s]
TAPS = 25


def slot_work(first, last):
    for g in range(4 * NG):
        yield g, [s for s in SLOT.get(g, ()) if not (last if "base" in s else first)]


def phase_linatt(nc, K, D, X):
    with Mem(nc, "la") as m:
        wqkv = m.sb("wqkv", [C, PARTS, C])
        wproj = m.sb("wproj", [C, 2, C])
        pwt = m.sb("pwt", [C, PARTS, 4, 32])
        dwt = m.sb("dwt", [C, 2, 4, NG])
        taps = m.sb("taps", [C, TAPS])
        wpq = m.sb("wpq", [C, C])
        dwq = m.sb("dwq", [C, N])
        mask32 = m.sb("mask32", [C, 32])
        wagg = m.sb("wagg", [C, 2, 4, NG, 32])
        densel = m.sb("densel", [C, 2, 32])
        spread = m.sb("spread", [64, 2, C])
        pad = [m.sb(f"pad{u}", [C, PARTS, PAD]) for u in range(2)]
        rep = m.sb("rep", [C, 2, 4, REP])
        agg = m.sb("agg", [C, 2, N])
        q_base = [m.sb(f"qb{u}", [C, N]) for u in range(2)]
        q_agg = m.sb("qa", [C, N])
        kT = m.sb("kT", [C, 9, C])
        vT = m.sb("vT", [C, 9, C + 2])
        num_w = [m.sb(f"nw{u}", [C, C]) for u in range(3)]
        den_w = [m.sb(f"dw{u}", [C, 32]) for u in range(3)]
        ksum = m.sb("ksum", [C, 1])
        rec = m.sb("rec", [64, CH])
        recs = [m.sb(f"recs{u}", [C, CH]) for u in range(2)]
        o = [m.sb(f"o{u}", [C, CH]) for u in range(2)]
        y = [m.sb(f"y{u}", [C, CH]) for u in range(2)]
        stats = K["stats"]
        acc = [m.ps(f"acc{u}", [C, CH]) for u in range(2)]
        tp = [m.ps(f"tp{u}", [C, 4, C]) for u in range(2)]
        vkp = m.ps("vkp", [C, CH])
        nb = m.ps("nb", [C, CH])
        rb = m.ps("rb", [C, CH])
        dp = m.ps("dp", [C, CH])
        w_in = m.sem("w_in")
        pool, vec = m.sem("pool"), m.sem("vec")
        const_ready, pad_zero, wagg_ready = m.sem("const_ready"), m.sem("pad_zero"), m.sem("wagg_ready")
        acc_ready, acc_saved = m.sem("acc_ready"), m.sem("acc_saved")
        rep_in = {p: m.sem(f"rep_in{p}") for p in (1, 2)}
        tap_done = m.sem("tap_done")
        tp_ready, tp_saved = m.sem("tp_ready"), m.sem("tp_saved")
        vk_ready, vk_saved = m.sem("vk_ready"), m.sem("vk_saved")
        q_ready = m.sem("q_ready")
        den_ready, den_read, rec_ready = m.sem("den_ready"), m.sem("den_read"), m.sem("rec_ready")
        nb_ready, rb_ready, recs_ready, o_ready = (m.sem(x) for x in ("nb_ready", "rb_ready", "recs_ready", "o_ready"))
        y_mm, y_saved, y_stat = m.sem("y_mm"), m.sem("y_saved"), m.sem("y_stat")
        y_out = [m.sem("y_out0"), m.sem("y_out1")]

        def window(u, p, dy, dx, rows=HW):
            at = MARGIN + dy * SIDE + dx
            return pad[u][:, p, at:at + rows * SIDE].rearrange("c (y x) -> c y x", x=SIDE)[:, :, 0:HW]

        def interior(u, p, row, rows):
            return window(u, p, 2 + row, 2, rows)

        def fills(tiles):
            return [(p, lo, min(lo + 4, tiles)) for p in (1, 2) for lo in range(0, tiles, 4)]

        ROW0 = MARGIN + 2 * SIDE

        def acc_project(b):
            return 12 * b - 6 if not isinstance(b, int) or b else 0

        def acc_aggregate(b, last):
            return 12 * b + (6 if last else 12)

        def tp_base(b):
            return 10 * b - 4 if not isinstance(b, int) or b else 0

        def tp_aggregate(b, last):
            return 10 * b + (6 if last else 12)

        def vk_base(b):
            return 2 * b - 1 if not isinstance(b, int) or b else 0

        def vk_aggregate(b, last):
            return 2 * b + (1 if last else 2)

        with nc.Block() as block:
            @block.sync
            def _(sp):
                sp.dma_start(wqkv[:, :, :], D["w_qkvT"]).then_inc(w_in, 16)
                sp.dma_start(wproj[:, :, :], D["w_projT"]).then_inc(w_in, 16)
                sp.dma_start(pwt[:, :, :, :], D["w_pwT"]).then_inc(w_in, 16)
                sp.dma_start(dwt[:, :, :, :], D["w_taps"]).then_inc(w_in, 16)
                sp.dma_start(taps[:, :], D["w_qtaps"]).then_inc(w_in, 16)

                def replicate(b, u):
                    for p in (1, 2):
                        sp.wait_ge(acc_saved, 12 * b + 2 * p if not isinstance(b, int) or b else 2 * p + 2)
                        for j in range(4):
                            for t in range(4):
                                sp.dma_start(rep[32 * t:32 * t + 32, p - 1, j, :],
                                             pad[u][32 * j:32 * j + 32, p, SHIFTS[t]:SHIFTS[t] + REP]).then_inc(rep_in[p], 16)

                over_batches(sp, lambda b, u, last: replicate(b, u))

            @block.gpsimd
            def _(g):
                step = Chain(g, pool)
                g.memset(pad[0][:, :, :], 0.0).then_inc(pad_zero, 1)
                g.memset(pad[1][:, :, :], 0.0).then_inc(pad_zero, 1)
                step(g.memset(vT[:, :, :], 1.0))
                step(g.memset(spread[:, :, :], 1.0))
                for q in range(2):
                    for s in range(2):
                        v = spread[32 * q:32 * q + 32, s, :].rearrange("p (b k) -> p b k", k=HD)
                        for sign in (1, -1):
                            step(g.affine_select(out=v, in_=v, pattern=[[-sign, 16], [0, HD]], base=-16 * s * sign,
                                                 channel_multiplier=sign, compare_op=ALU.is_ge, fill=0.0))
                g.sem_inc(const_ready, 1)
                with g.Fori(0, B) as b:
                    for h in range(2):
                        g.wait_ge(y_saved, 2 * b + h + 1)
                        g.dma_start(D["proj"][:, bass.ds(b * N + h * CH, CH)], y[h][:, :]).then_inc(y_out[h], 16)
                g.wait_ge(y_out[0], 16 * B)
                g.wait_ge(y_out[1], 16 * B)

            @block.tensor
            def _(pe):
                pe.wait_ge(w_in, 80)
                pe.wait_ge(wagg_ready, 1)
                pe.wait_ge(const_ready, 1)

                def project(b):
                    n = acc_project(b)
                    for c in range(6):
                        p, h = divmod(c, 2)
                        wait_if(pe, acc_saved, n + c - 1)
                        pe.matmul(acc[h][:, :], wqkv[:, p, :], X[:, bass.ds(b * N + h * CH, CH)],
                                  start=True, stop=True).then_inc(acc_ready, 1)

                def group(b, n, i):
                    c, g = divmod(i, NG)
                    p, h = c // 2 + 1, c % 2
                    if g == 0:
                        pe.wait_ge(rep_in[p], 256 * b + 256)
                        wait_if(pe, acc_saved, n + c - 1)
                    gy, gx = PLACES[g]
                    at = MARGIN + (gy + 16 * h) * SIDE + gx
                    for j in range(4):
                        view = rep[:, p - 1, j, at:at + 16 * SIDE].rearrange("c (y x) -> c y x", x=SIDE)
                        last = pe.matmul(acc[h][32 * j:32 * j + 32, :], wagg[:, p - 1, j, g, :],
                                         view[:, :, 0:HW], start=(g == 0), stop=(g == NG - 1))
                    if g == NG - 1:
                        last.then_inc(acc_ready, 1)

                def queries(b, n):
                    pe.wait_ge(tap_done, TAPS * b + TAPS)
                    for h in range(2):
                        wait_if(pe, acc_saved, n + 4 + h - 1)
                        pe.matmul(acc[h][:, :], wpq[:, :], dwq[:, h * CH:(h + 1) * CH], start=True, stop=True)\
                          .then_inc(acc_ready, 1)

                def work(step, b, u, last):
                    kind = step[0]
                    base = "base" in step
                    if kind == "tp":
                        c = step[2]
                        p, lo, hi = fills(9 if base else 8)[c]
                        n = tp_base(b) if base else tp_aggregate(b, last)
                        if c == 0:
                            pe.wait_ge(acc_saved, (acc_project(b) if base else acc_aggregate(b, last)) + 6)
                        wait_if(pe, tp_saved, n + c - 1)
                        for r in range(lo, hi):
                            source = pad[u][:, p, ROW0 + r * C:ROW0 + (r + 1) * C] if base else agg[:, p - 1, r * C:(r + 1) * C]
                            done = pe.transpose(tp[c % 2][:, r - lo, :], source, K["ident"][:, :])
                        done.then_inc(tp_ready, 1)
                    elif kind == "vk":
                        tiles = 9 if base else 8
                        n, k = (tp_base(b), vk_base(b)) if base else (tp_aggregate(b, last), vk_aggregate(b, last))
                        pe.wait_ge(tp_saved, n + len(fills(tiles)))
                        wait_if(pe, vk_saved, k)
                        for r in range(tiles):
                            done = pe.matmul(vkp[:, 0:C + 1], kT[:, r, :], vT[:, r, 0:C + 1],
                                             start=(r == 0), stop=(r == tiles - 1))
                        done.then_inc(vk_ready, 1)
                    elif kind == "den":
                        pe.wait_ge(vk_saved, vk_aggregate(b, last) + 1)
                        wait_if(pe, y_saved, 2 * b)
                        pe.wait_ge(q_ready, b + 1)
                        for h in range(2):
                            cols = slice(h * CH, (h + 1) * CH)
                            pe.matmul(dp[32 * h:32 * h + 32, :], den_w[u][:, :], q_base[u][:, cols], start=True, stop=False)
                            done = pe.matmul(dp[32 * h:32 * h + 32, :], den_w[2][:, :], q_agg[:, cols], start=False, stop=True)
                        done.then_inc(den_ready, 1)
                    elif kind == "nb":
                        h, s = divmod(step[1], 2)
                        wait_if(pe, o_ready, 4 * b + 2 * h + s)
                        pe.matmul(nb[:, :], num_w[u if s == 0 else 2][:, :],
                                  (q_base[u] if s == 0 else q_agg)[:, h * CH:(h + 1) * CH],
                                  start=True, stop=True).then_inc(nb_ready, 1)
                    elif kind == "rb":
                        h, s = divmod(step[1], 2)
                        pe.wait_ge(rec_ready, b + 1)
                        wait_if(pe, recs_ready, 4 * b + 2 * h + s)
                        pe.matmul(rb[:, :], spread[32 * h:32 * h + 32, s, :], rec[32 * h:32 * h + 32, :],
                                  start=True, stop=True).then_inc(rb_ready, 1)
                    else:
                        h = step[1]
                        pe.wait_ge(o_ready, 4 * b + 2 * h + 2)
                        if h == 1:
                            pe.wait_ge(y_saved, 2 * b + 1)
                        pe.matmul(dp[:, :], wproj[:, 0, :], o[0][:, :], start=True, stop=False)
                        pe.matmul(dp[:, :], wproj[:, 1, :], o[1][:, :], start=False, stop=True).then_inc(y_mm, 1)

                project(0)
                for step in BASE_STEPS:
                    work(step, 0, 0, False)

                def batch(b, u, last):
                    if not last:
                        project(b + 1)
                    n = acc_aggregate(b, last)
                    for i, steps in slot_work(isinstance(b, int) and b == 0, last):
                        group(b, n, i)
                        for step in steps:
                            work(step, b + 1 if "base" in step else b - 1, 1 - u, False)
                    queries(b, n)

                over_batches(pe, batch)
                for step in OUTPUTS:
                    work(step, B - 1, 1, True)

            @block.vector
            def _(v):
                step = Chain(v, vec)
                v.wait_ge(w_in, 80)
                step(v.reduce_sum(mask32[:, :], K["mask8"][:, :].rearrange("p (t c) -> p c t", t=4), AX.X))
                step(v.tensor_tensor(wpq[:, :], pwt[:, 0, :, :].rearrange("p j c -> p (j c)"), K["mask8"][:, :], ALU.mult))
                step(v.tensor_tensor(pwt[:, :, :, :].rearrange("p a j c -> p (a j) c"),
                                     pwt[:, :, :, :].rearrange("p a j c -> p (a j) c"),
                                     mask32[:, :].rearrange("p (o c) -> p o c", o=1).to_broadcast([C, PARTS * 4, 32]), ALU.mult))
                for p in range(2):
                    step(v.tensor_tensor(wagg[:, p, :, :, :],
                                         pwt[:, p + 1, :, :].rearrange("p j (o c) -> p j o c", o=1).to_broadcast([C, 4, NG, 32]),
                                         dwt[:, p, :, :].rearrange("p j (g o) -> p j g o", o=1).to_broadcast([C, 4, NG, 32]),
                                         ALU.mult))
                v.sem_inc(wagg_ready, 1)
                step(v.memset(densel[:, :, :], 0.0))
                for s in range(2):
                    step(v.tensor_copy(densel[:, s, 16 * s:16 * s + 16], K["mask8"][:, 0:C:HD]))
                v.wait_ge(const_ready, 1)

                def work(step, b, u, last):
                    kind = step[0]
                    base = "base" in step
                    if kind == "tp":
                        c = step[2]
                        p, lo, hi = fills(9 if base else 8)[c]
                        n = tp_base(b) if base else tp_aggregate(b, last)
                        v.wait_ge(tp_ready, n + c + 1)
                        if p == 1:
                            v.tensor_scalar(kT[:, lo:hi, :], tp[c % 2][:, 0:hi - lo, :], 0.0, None, ALU.max)\
                             .then_inc(tp_saved, 1)
                        else:
                            v.tensor_copy(vT[:, lo:hi, 0:C], tp[c % 2][:, 0:hi - lo, :]).then_inc(tp_saved, 1)
                    elif kind == "vk":
                        w, s = (u, 0) if base else (2, 1)
                        v.wait_ge(vk_ready, (vk_base(b) if base else vk_aggregate(b, last)) + 1)
                        if base:
                            v.tensor_scalar(q_base[u][:, :].rearrange("c (y x) -> c y x", x=HW), interior(u, 0, 0, HW),
                                            0.0, None, ALU.max).then_inc(q_ready, 1)
                        v.tensor_tensor(num_w[w][:, :], vkp[:, 0:C], K["mask8"][:, :], ALU.mult)
                        v.tensor_scalar(den_w[w][:, :], densel[:, s, :], vkp[:, C:C + 1], None, ALU.mult).then_inc(vk_saved, 1)
                    elif kind == "den":
                        v.wait_ge(den_ready, b + 1)
                        v.tensor_scalar(rec[:, :], dp[0:64, :], EPS_ATT, None, ALU.add).then_inc(den_read, 1)
                        v.wait_ge(den_read, b + 1)
                        v.reciprocal(rec[:, :], rec[:, :]).then_inc(rec_ready, 1)
                    elif kind == "rb":
                        h, s = divmod(step[1], 2)
                        k = 4 * b + 2 * h + s
                        v.wait_ge(nb_ready, k + 1)
                        v.wait_ge(recs_ready, k + 1)
                        wait_if(v, y_mm, 2 * b + h)
                        v.tensor_tensor(o[s][:, :], nb[:, :], recs[s][:, :], ALU.mult).then_inc(o_ready, 1)

                def tap(b, u, t):
                    image = window(u, 0, *divmod(t, 5))
                    out = dwq[:, :].rearrange("c (y x) -> c y x", x=HW)
                    if t == 0:
                        wait_if(v, acc_ready, 12 * b + 6)
                        v.tensor_scalar(out, image, taps[:, 0:1], None, ALU.mult).then_inc(tap_done, 1)
                    else:
                        v.wait_ge(tap_done, TAPS * b + t)
                        v.scalar_tensor_tensor(out, image, taps[:, t:t + 1], out, ALU.mult, ALU.add).then_inc(tap_done, 1)

                def statistics(b):
                    for h in range(2):
                        v.wait_ge(y_saved, 2 * b + h + 1)
                        v.bn_stats(stats[:, bass.ds(2 * b + h, 1), :], y[h][:, :]).then_inc(y_stat, 1)

                for step in BASE_STEPS:
                    work(step, 0, 0, False)

                def batch(b, u, last):
                    first = isinstance(b, int) and b == 0
                    for i, steps in slot_work(first, last):
                        if i < TAPS:
                            tap(b, u, i)
                        for step in steps:
                            work(step, b + 1 if "base" in step else b - 1, 1 - u, False)
                    if not first:
                        statistics(b - 1)

                over_batches(v, batch)
                for step in OUTPUTS:
                    work(step, B - 1, 1, True)
                statistics(B - 1)

            @block.scalar
            def _(a):
                a.wait_ge(pad_zero, 2)

                def project(b, u):
                    n = acc_project(b)
                    for c in range(6):
                        p, h = divmod(c, 2)
                        if h == 0 and (not isinstance(b, int) or b >= 2):
                            if p == 0:
                                a.wait_ge(tap_done, TAPS * (b - 1))
                            else:
                                a.wait_ge(rep_in[p], 256 * (b - 1))
                                a.wait_ge(tp_ready, tp_base(b - 2) + 3 * p)
                        a.wait_ge(acc_ready, n + c + 1)
                        a.copy(interior(u, p, 16 * h, 16), acc[h][:, :].rearrange("c (y x) -> c y x", x=HW)).then_inc(acc_saved, 1)

                def chunk(b, c, last):
                    a.wait_ge(acc_ready, acc_aggregate(b, last) + c + 1)
                    part, h = c // 2, c % 2
                    cols = slice(h * CH, (h + 1) * CH)
                    if part == 2:
                        a.activation(q_agg[:, cols], acc[h][:, :], ACT.Relu).then_inc(acc_saved, 1)
                    else:
                        if h == 0:
                            wait_if(a, tp_ready, tp_aggregate(b - 1, False) + 2 * part + 2 if not isinstance(b, int) or b else 0)
                        a.copy(agg[:, part, cols], acc[h][:, :]).then_inc(acc_saved, 1)

                def work(step, b):
                    if step[0] == "rb":
                        h, s = divmod(step[1], 2)
                        k = 4 * b + 2 * h + s
                        a.wait_ge(rb_ready, k + 1)
                        wait_if(a, o_ready, k - 1)
                        a.copy(recs[s][:, :], rb[:, :]).then_inc(recs_ready, 1)
                    elif step[0] == "y":
                        h = step[1]
                        a.wait_ge(y_mm, 2 * b + h + 1)
                        wait_if(a, y_stat, 2 * b + h - 1)
                        wait_if(a, y_out[h], 16 * b)
                        a.copy(y[h][:, :], dp[:, :]).then_inc(y_saved, 1)

                project(0, 0)

                def batch(b, u, last):
                    if not last:
                        project(b + 1, 1 - u)
                    for i, steps in slot_work(isinstance(b, int) and b == 0, last):
                        if i % NG == NG - 1:
                            chunk(b, i // NG, last)
                        for step in steps:
                            work(step, b - 1)
                    for c in (4, 5):
                        chunk(b, c, last)

                over_batches(a, batch)
                for step in OUTPUTS:
                    work(step, B - 1)


def phase_linatt_norm(nc, K, D, X):
    with Mem(nc, "lan") as m:
        y = [m.sb(f"y{u}", [C, 2 * N]) for u in range(2)]
        par = m.sb("par", [C, 2])
        mv = m.sb("mv", [C, 2])
        cv = m.sb("cv", [C, 4])
        S, T0, V = (cv[:, i:i + 1] for i in range(3))
        par_in, var_ready, s_ready, coef_ready = (m.sem(x) for x in ("par_in", "var_ready", "s_ready", "coef_ready"))
        y_in = [m.sem("y_in0"), m.sem("y_in1")]
        lin_ready, sum_ready = m.sem("lin_ready"), m.sem("sum_ready")
        pool, vec = m.sem("pool"), m.sem("vec")
        W = 2 * N
        NT = T // W
        with nc.Block() as block:
            @block.sync
            def _(sp):
                def load(k, u):
                    sp.dma_start(y[u][:, :], D["proj"][:, bass.ds(k * W, W)]).then_inc(y_in[u], 16)

                load(0, 0)
                load(1, 1)
                with sp.Fori(1, NT // 2) as i:
                    for u in range(2):
                        sp.wait_ge(sum_ready, 2 * i + u - 1)
                        load(2 * i + u, u)

            @block.gpsimd
            def _(g):
                for i, name in enumerate(("bn_gamma", "bn_beta")):
                    g.dma_start(par[:, i:i + 1], col(D["L1_conv_" + name])).then_inc(par_in, 16)
                g.wait_ge(var_ready, 1)
                step = Chain(g, pool)
                rsqrt_eps(g, step, K, S, mv[:, 1:2], EPS)
                g.sem_inc(s_ready, 1)

            @block.vector
            def _(v):
                step = Chain(v, vec)
                step(v.bn_aggr(mv[:, :], K["stats"][:, :, :]))
                v.sem_inc(var_ready, 1)
                v.wait_ge(s_ready, 1)
                v.wait_ge(par_in, 32)
                step(v.tensor_mul(S, S, par[:, 0:1]))
                step(v.tensor_mul(T0, S, mv[:, 0:1]))
                step(v.tensor_sub(T0, par[:, 1:2], T0))
                v.sem_inc(coef_ready, 1)
                with v.Fori(0, NT // 2) as i:
                    for u in range(2):
                        v.wait_ge(lin_ready, 2 * i + u + 1)
                        xb = X[:, bass.ds((2 * i + u) * W, W)]
                        v.tensor_add(xb, xb, y[u][:, :]).then_inc(sum_ready, 1)

            @block.scalar
            def _(a):
                a.wait_ge(coef_ready, 1)
                with a.Fori(0, NT // 2) as i:
                    for u in range(2):
                        a.wait_ge(y_in[u], 16 * i + 16)
                        a.activation(y[u][:, :], y[u][:, :], ACT.Identity, bias=T0, scale=S).then_inc(lin_ready, 1)



def over(eng, total, step):
    step(0, 0, False)
    step(1, 1, False)
    with eng.Fori(1, total // 2 - 1) as i:
        for u in range(2):
            step(2 * i + u, u, False)
    step(total - 2, 0, False)
    step(total - 1, 1, True)


class LayerNorm:

    def __init__(self, m, K, X):
        self.K, self.X = K, X
        self.xs = [m.sb(f"ln_xs{u}", [C, CH]) for u in range(2)]
        self.xt = [m.sb(f"ln_xt{u}", [C, 4, C]) for u in range(2)]
        self.st = [m.sb(f"ln_st{u}", [C, 4, 6]) for u in range(2)]
        self.mv = [m.sb(f"ln_mv{u}", [C, 4, 2]) for u in range(2)]
        self.ab = [m.sb(f"ln_ab{u}", [C, 2, 4]) for u in range(2)]
        self.front = [m.ps(f"ln_front{u}", [C, 4, C]) for u in range(2)]
        self.back = m.ps("ln_back", [C, CH])
        self.staged = [m.sem(f"ln_staged{u}") for u in range(2)]
        self.front_ready, self.stat, self.mv_ready, self.gp, self.ab_ready, self.xt_ready, self.back_ready, self.saved = (
            m.sem("ln_" + x) for x in ("front_ready", "stat", "mv_ready", "gp", "ab_ready", "xt_ready", "back_ready", "saved"))

    def sync(self, sp, n, u):
        wait_if(sp, self.front_ready, n - 1)
        sp.dma_start(self.xs[u][:, :], self.X[:, bass.ds(n * CH, CH)]).then_inc(self.staged[u], 16)

    def tensor_front(self, pe, n, u):
        pe.wait_ge(self.staged[u], (n // 2 + 1) * 16 if isinstance(n, int) else 8 * n + (16 - 8 * u))
        wait_if(pe, self.xt_ready, n - 1)
        for r in range(4):
            last = pe.transpose(self.front[u][:, r, :], self.xs[u][:, r * C:(r + 1) * C], self.K["ident"][:, :])
        last.then_inc(self.front_ready, 1)

    def tensor_back(self, pe, n, u):
        pe.wait_ge(self.xt_ready, n + 1)
        wait_if(pe, self.saved, n)
        for r in range(4):
            last = pe.transpose(self.back[:, r * C:(r + 1) * C], self.xt[u][:, r, :], self.K["ident"][:, :])
        last.then_inc(self.back_ready, 1)

    def vector_stats(self, v, n, u):
        v.wait_ge(self.front_ready, n + 1)
        for r in range(4):
            last = v.bn_stats(self.st[u][:, r, :], self.front[u][:, r, :])
        last.then_inc(self.stat, 1)
        v.wait_ge(self.stat, 1)
        v.wait_ge(self.stat, n + 1)
        wait_if(v, self.ab_ready, n - 1)
        for r in range(4):
            last = v.bn_aggr(self.mv[u][:, r, :], self.st[u][:, r, :])
        last.then_inc(self.mv_ready, 1)

    def gpsimd(self, g, n, u):
        g.wait_ge(self.mv_ready, n + 1)
        wait_if(g, self.xt_ready, n - 1)
        rstd, shift = self.ab[u][:, 0, :], self.ab[u][:, 1, :]
        g.tensor_tensor(rstd, self.mv[u][:, :, 1], self.K["eps"][:, :], ALU.add).then_inc(self.gp, 1)
        g.wait_ge(self.gp, 3 * n + 1)
        g.tensor_tensor(rstd, rstd, self.K["neghalf"][:, 0:4], ALU.pow).then_inc(self.gp, 1)
        g.wait_ge(self.gp, 3 * n + 2)
        g.tensor_tensor(shift, self.mv[u][:, :, 0], rstd, ALU.mult).then_inc(self.gp, 1)
        g.wait_ge(self.gp, 3 * n + 3)
        g.tensor_tensor(shift, shift, self.K["negone"][:, :], ALU.mult).then_inc(self.ab_ready, 1)

    def scalar(self, a, n, u, used=None):
        a.wait_ge(self.ab_ready, n + 1)
        wait_if(a, self.back_ready, n - 1)
        if used is not None:
            used(n, u)
        for r in range(4):
            last = a.activation(self.xt[u][:, r, :], self.front[u][:, r, :], ACT.Identity,
                                bias=self.ab[u][:, 1, r:r + 1], scale=self.ab[u][:, 0, r:r + 1])
        last.then_inc(self.xt_ready, 1)

    def vector_save(self, v, n, out):
        v.wait_ge(self.back_ready, n + 1)
        v.tensor_copy(out, self.back[:, :]).then_inc(self.saved, 1)



SH = 8
DH = 16
RH = 2
Q_TERMS = (0, 0, 1, 0, 2, 1)
K_TERMS = (0, 1, 0, 2, 0, 1)
KQ = DH * len(Q_TERMS)
KM = KQ + 3
SCALE = DH ** -0.5


def phase_attn_prep(nc, K, D, X):
    RVW = RH * DH
    with Mem(nc, "ap") as m:
        ln = LayerNorm(m, K, X)
        wq, wk = m.sb("wq", [C, C]), m.sb("wk", [C, C])
        wqr, wkr = m.sb("wqr", [C, C]), m.sb("wkr", [C, C])
        mask16 = m.sb("mask16", [C, C])
        wuv = m.sb("wuv", [C, C + RVW])
        xc = [m.sb(f"xc{u}", [C, CH]) for u in range(2)]
        part = [[[m.sb(f"part{u}{z}{t}", [C, CH], BF16) for t in range(3)] for z in range(2)] for u in range(2)]
        left = [[m.sb(f"left{u}{z}", [C, CH]) for z in range(2)] for u in range(2)]
        us = [m.sb(f"us{u}", [C, 4, C]) for u in range(2)]
        pz = [m.ps(f"pz{z}", [C, CH]) for z in range(2)]
        puv = [m.ps(f"puv{h}", [C, 2, C + RVW]) for h in range(2)]
        pw = m.ps("pw", [C, C])
        w_in, pool, m_ready, w_ready, wu_mm = (m.sem(x) for x in ("w_in", "pool", "m_ready", "w_ready", "wu_mm"))
        vec = m.sem("vec")
        z_ready, uv_ready, high, left1, mid, low = (m.sem(x) for x in ("z_ready", "uv_ready", "high", "left1", "mid", "low"))
        uv_saved = m.sem("uv_saved")
        z_out = [m.sem("z_out0"), m.sem("z_out1")]
        u_out = [m.sem("u_out0"), m.sem("u_out1")]
        RV = K["rv"]

        with nc.Block() as block:
            @block.sync
            def _(sp):
                for dst, src in ((wq, "wq_s"), (wk, "wk_s"), (wqr, "wq_rT"), (wkr, "wk_retT")):
                    sp.dma_start(dst[:, :], D[src]).then_inc(w_in, 16)
                sp.dma_start(wuv[:, C:C + RVW], D["wv_r"]).then_inc(w_in, 16)

                def step(n, u, last):
                    ln.sync(sp, n, u)
                    if not isinstance(n, int) or n >= 2:
                        store(n - 2, u)

                def store(k, u):
                    sp.wait_ge(low, 2 * k + 2)
                    for z in range(2):
                        for t in range(3):
                            sp.dma_start(D["qk"][z, t, :, bass.ds(k * CH, CH)], part[u][z][t][:, :]).then_inc(z_out[u], 16)
                    sp.wait_ge(uv_saved, 2 * k + 2)
                    sp.dma_start(D["u"][:, bass.ds(4 * k, 4), :], us[u][:, :, :]).then_inc(u_out[u], 16)

                over(sp, NCH, step)
                store(NCH - 2, 0)
                store(NCH - 1, 1)
                for u in range(2):
                    sp.wait_ge(z_out[u], 96 * NCH // 2)
                    sp.wait_ge(u_out[u], 16 * NCH // 2)

            @block.gpsimd
            def _(g):
                step = Chain(g, pool)
                step(g.memset(mask16[:, :], 1.0))
                for one in block_mask(g, mask16[:, :], DH):
                    step(one())
                g.sem_inc(m_ready, 1)

                def lows(n, u):
                    for z in range(2):
                        g.wait_ge(mid, 2 * n + z + 1)
                        g.tensor_tensor(part[u][z][2][:, :], left[u][z][:, :], part[u][z][1][:, :], ALU.subtract).then_inc(low, 1)

                def step(n, u, last):
                    ln.gpsimd(g, n, u)
                    if not isinstance(n, int) or n > 0:
                        lows(n - 1, 1 - u)

                over(g, NCH, step)
                lows(NCH - 1, 1)

            @block.tensor
            def _(pe):
                pe.wait_ge(w_ready, 1)
                pe.matmul(pw[:, :], wqr[:, :], wkr[:, :], start=True, stop=True).then_inc(wu_mm, 1)
                pe.wait_ge(w_ready, 2)
                pe.wait_ge(w_in, 80)

                def step(n, u, last):
                    if not last:
                        ln.tensor_front(pe, n + 1, 1 - u)
                    ln.tensor_back(pe, n, u)
                    pe.wait_ge(ln.saved, n + 1)
                    for z, w in enumerate((wq, wk)):
                        wait_if(pe, left1, 2 * n - 1 + z)
                        pe.matmul(pz[z][:, :], w[:, :], xc[u][:, :], start=True, stop=True).then_inc(z_ready, 1)
                    for h in range(2):
                        wait_if(pe, uv_saved, 2 * n - 1 + h)
                        for r in range(2):
                            k = 2 * h + r
                            done = pe.matmul(puv[h][:, r, :], xc[u][:, k * C:(k + 1) * C], wuv[:, :], start=True, stop=True)
                        done.then_inc(uv_ready, 1)

                ln.tensor_front(pe, 0, 0)
                over(pe, NCH, step)

            @block.vector
            def _(v):
                step = Chain(v, vec)
                v.wait_ge(w_in, 80)
                v.wait_ge(m_ready, 1)
                step(v.tensor_mul(wkr[:, :], wkr[:, :], mask16[:, :]))
                v.sem_inc(w_ready, 1)
                v.wait_ge(wu_mm, 1)
                v.tensor_copy(wuv[:, 0:C], pw[:, :]).then_inc(w_ready, 1)

                def step(n, u, last):
                    if not last:
                        ln.vector_stats(v, n + 1, 1 - u)
                    wait_if(v, uv_ready, 2 * n - 2)
                    ln.vector_save(v, n, xc[u][:, :])
                    for z in range(2):
                        v.wait_ge(high, 2 * n + z + 1)
                        wait_if(v, low, 2 * n + z - 3)
                        v.scalar_tensor_tensor(left[u][z][:, :], pz[z][:, :], SCALE if z == 0 else 1.0,
                                               part[u][z][0][:, :], ALU.mult, ALU.subtract).then_inc(left1, 1)
                    for h in range(2):
                        v.wait_ge(uv_ready, 2 * n + h + 1)
                        wait_if(v, u_out[u], 8 * (n - u))
                        v.tensor_copy(us[u][:, 2 * h:2 * h + 2, :], puv[h][:, :, 0:C])
                        v.tensor_copy(RV[:, bass.ds(4 * n + 2 * h, 2), :], puv[h][:, :, C:C + RVW]).then_inc(uv_saved, 1)

                ln.vector_stats(v, 0, 0)
                over(v, NCH, step)

            @block.scalar
            def _(a):
                def step(n, u, last):
                    if not last:
                        ln.scalar(a, n + 1, 1 - u)
                    for z in range(2):
                        a.wait_ge(z_ready, 2 * n + z + 1)
                        wait_if(a, z_out[u], 48 * (n - u))
                        a.activation(part[u][z][0][:, :], pz[z][:, :], ACT.Copy, scale=SCALE if z == 0 else 1.0).then_inc(high, 1)
                    for z in range(2):
                        a.wait_ge(left1, 2 * n + z + 1)
                        a.copy(part[u][z][1][:, :], left[u][z][:, :]).then_inc(mid, 1)

                ln.scalar(a, 0, 0)
                over(a, NCH, step)


STEPS = 32
MAX_UNITS = 128
VW = 2 * RH * DH
FIRST_MAX = 4
LAST_MAX = STEPS - 3
PER_STEP = -(-MAX_UNITS // (LAST_MAX + 1 - FIRST_MAX))
EXP_AT, SUM_AT, OUT_AT, WOUT_AT = 13, 15, 19, 22


def side_work(k, post, following):
    work = []
    if post:
        if k < 8:
            work.append(("tokens", k))
        if k == OUT_AT:
            work += [("back", 0), ("back", 1)]
        if k == WOUT_AT:
            work += [("wout", 0), ("wout", 1)]
    if following and k >= FIRST_MAX:
        first = (k - FIRST_MAX) * PER_STEP
        work += [("max", n) for n in range(first, min(first + PER_STEP, MAX_UNITS))]
        if k == LAST_MAX + 1:
            work.append(("rows", 0))
    return work


def phase_attn(nc, K, D, X):
    SIDE1 = MAX_UNITS + 1
    SIDE2 = SIDE1 + 12
    with Mem(nc, "at") as m:
        qo = [m.sb(f"qo{u}", [KM, SH, N], BF16) for u in range(2)]
        ko = [m.sb(f"ko{u}", [KM, SH, N], BF16) for u in range(2)]
        P = [m.sb(f"P{u}", [C, 4, CH]) for u in range(2)]
        sums = m.sb("sums", [C, 4, N])
        numT = m.sb("numT", [C, 8, 2 * C])
        prod = m.sb("prod", [C, 8, 2 * C])
        ub = m.sb("ub", [C, 8, C])
        oc = prod[:, :, :].rearrange("p i n -> p (i n)")[:, 0:N]
        wout = m.sb("wout", [C, C])
        recT = m.sb("recT", [C, 64])
        sim = m.sb("sim", [C, 64, 2])
        sm1 = m.sb("sm1", [C, 64])
        mx = m.sb("mx", [C, SH * 8, 2])
        negmax = m.sb("negmax", [C, SH * 8])
        rvb = [m.sb(f"rvb{u}", [C, 8, VW]) for u in range(2)]
        mleft = m.sb("mleft", [64, C])
        mrow = m.sb("mrow", [64, 3, C], BF16)
        RV = K["rv"]
        side = [m.ps(f"side{u}", [C, CH]) for u in range(2)]
        S = [m.ps(f"S{u}", [C, 2, CH]) for u in range(2)]
        pv_acc = [m.ps(f"pv{h}", [C, CH]) for h in range(2)]
        w_in, const_ready = m.sem("w_in"), m.sem("const_ready")
        op_in, row_in = [m.sem("op_in0"), m.sem("op_in1")], [m.sem("row_in0"), m.sem("row_in1")]
        u_in, rv_ready = m.sem("u_in"), m.sem("rv_ready")
        side_ready, side_saved = m.sem("side_ready"), m.sem("side_saved")
        s_ready, p_ready, pv_done, grp_saved = (m.sem(x) for x in ("s_ready", "p_ready", "pv_done", "grp_saved"))
        row_step, row_ready = m.sem("row_step"), m.sem("row_ready")
        far_ready = m.sem("far_ready")
        post_step, sim_ready, e_ready, esum_ready, rsum_ready, out_ready = (
            m.sem(x) for x in ("post_step", "sim_ready", "e_ready", "esum_ready", "rsum_ready", "out_ready"))

        def side_base(b):
            return SIDE2 * b + 2 * SIDE1 - SIDE2 if not isinstance(b, int) or b else SIDE1

        def side_at(b, k, what, post=True, following=True):
            n = 0
            for j in range(STEPS):
                for w in side_work(j, post, following):
                    n += 1
                    if j == k and w == what:
                        return side_base(b) + n
            raise ValueError(what)

        with nc.Block() as block:
            @block.sync
            def _(sp):
                sp.dma_start(wout[:, :], D["w_out"]).then_inc(w_in, 16)

                def load(b, u):
                    for z, (dst, terms) in enumerate(((qo[u], Q_TERMS), (ko[u], K_TERMS))):
                        for i, t in enumerate(terms):
                            sp.dma_start(dst[DH * i:DH * i + DH, :, :],
                                         D["qk"][z, t, :, bass.ds(b * N, N)].rearrange("(s d) n -> d s n", d=DH))\
                              .then_inc(op_in[u], 16)

                def rows(b, u):
                    sp.wait_ge(row_ready, b + 1)
                    for t in range(3):
                        sp.dma_start(qo[u][KQ + t:KQ + t + 1, :, :], mrow[:, t, :]).then_inc(row_in[u], 16)

                load(0, 0)
                load(1, 1)
                rows(0, 0)

                def slot(b, u, last):
                    if not isinstance(b, int) or b:
                        sp.wait_ge(side_ready, side_at(b, OUT_AT, ("back", 1), following=not last))
                    sp.dma_start(ub[:, :, :], D["u"][:, bass.ds(8 * b, 8), :]).then_inc(u_in, 16)
                    if not last:
                        rows(b + 1, 1 - u)
                    if not isinstance(b, int) or b < B - 2:
                        sp.wait_ge(s_ready, 64 * b + 64)
                        load(b + 2, u)

                over(sp, B, slot)

            @block.gpsimd
            def _(g):
                for u in range(2):
                    g.memset(rvb[u][:, :, RH * DH:VW], 1.0).then_inc(const_ready, 1)
                for u in range(2):
                    g.wait_ge(const_ready, u + 2)
                    g.memset(ko[u][KQ:KM, :, :], 1.0).then_inc(const_ready, 1)

                def retrieve(b, tokens):
                    step = Chain(g, post_step, 11 * b)
                    g.wait_ge(side_saved, tokens)
                    g.wait_ge(u_in, 16 * b + 16)
                    heads = prod[:, :, :].rearrange("p i (s d) -> p (i s) d", d=DH)
                    nv = numT[:, :, :].rearrange("p i (s r d) -> p (i s) r d", r=RH, d=DH)
                    pv = prod[:, :, :].rearrange("p i (s r d) -> p (i s) r d", r=RH, d=DH)
                    step(g.tensor_tensor(pv, nv, ub[:, :, :].rearrange("p i (s o d) -> p (i s) o d", o=1, d=DH)
                                         .to_broadcast([C, 64, RH, DH]), ALU.mult))
                    for w in (8, 4, 2):
                        step(g.tensor_tensor(heads[:, :, 0:w], heads[:, :, 0:w], heads[:, :, w:2 * w], ALU.add))
                    step(g.tensor_tensor(sim[:, :, :].rearrange("p s r -> p (s r)"), heads[:, :, 0], heads[:, :, 1], ALU.add))
                    step(g.tensor_tensor(sim[:, :, :], sim[:, :, :],
                                         recT[:, :].rearrange("p (s o) -> p s o", o=1).to_broadcast([C, 64, 2]), ALU.mult))
                    step(g.tensor_tensor(sm1[:, :], sim[:, :, 0], sim[:, :, 1], ALU.subtract))
                    g.sem_inc(sim_ready, 1)
                    g.wait_ge(e_ready, b + 1)
                    g.tensor_tensor(sm1[:, :], sim[:, :, 0], sim[:, :, 1], ALU.add).then_inc(esum_ready, 1)
                    g.wait_ge(rsum_ready, b + 1)
                    step(g.tensor_tensor(sm1[:, :], sm1[:, :], recT[:, :], ALU.mult))
                    step(g.tensor_tensor(sim[:, :, :], sim[:, :, :],
                                         sm1[:, :].rearrange("p (s o) -> p s o", o=1).to_broadcast([C, 64, 2]), ALU.mult))
                    step(g.tensor_tensor(heads, numT[:, :, :].rearrange("p i (s d) -> p (i s) d", d=DH),
                                         sim[:, :, :].rearrange("p s (r o) -> p (s r) o", o=1).to_broadcast([C, 128, DH]),
                                         ALU.mult))
                    step(g.tensor_tensor(ub[:, :, :].rearrange("p i (s d) -> p (i s) d", d=DH),
                                         pv[:, :, 0, :], pv[:, :, 1, :], ALU.add))
                    assert step.n == 11
                    g.sem_inc(out_ready, 1)

                with g.Fori(1, B - 1) as b:
                    retrieve(b - 1, side_at(b, 7, ("tokens", 7)))
                retrieve(B - 2, side_at(B - 1, 7, ("tokens", 7), following=False))
                retrieve(B - 1, side_base(B) - SIDE1 + 8)

            @block.tensor
            def _(pe):
                pe.wait_ge(w_in, 16)
                pe.wait_ge(const_ready, 4)

                def fill(w, b, u, at, bank):
                    kind, n = w
                    wait_if(pe, side_saved, at - 1)
                    if kind == "max":
                        s, rest = divmod(n, 16)
                        i, h = divmod(rest, 2)
                        return pe.matmul(side[bank][:, :], qo[1 - u][0:KQ, s, i * C:(i + 1) * C],
                                         ko[1 - u][0:KQ, s, h * CH:(h + 1) * CH], start=True, stop=True)
                    if kind == "rows":
                        pe.wait_ge(row_step, 4 * (b + 1) + 1)
                        return pe.matmul(side[bank][0:64, 0:C], negmax[:, :], K["ident"][:, :], start=True, stop=True)
                    if kind == "tokens":
                        for q in range(4):
                            last = pe.transpose(side[bank][:, q * C:(q + 1) * C], sums[:, q, n * C:(n + 1) * C], K["ident"][:, :])
                        return last
                    if kind == "back":
                        pe.wait_ge(out_ready, b)
                        for r in range(4):
                            last = pe.transpose(side[bank][:, r * C:(r + 1) * C], ub[:, 4 * n + r, :], K["ident"][:, :])
                        return last
                    pe.wait_ge(side_saved, at - n)
                    return pe.matmul(side[bank][:, :], wout[:, :], oc[:, n * CH:(n + 1) * CH], start=True, stop=True)

                def scores(b, u, k, hp):
                    g, j = divmod(k, 8)
                    quad, half = divmod(g, 2)
                    wait_if(pe, p_ready, 64 * b + 2 * k - 1 + hp)
                    for i in range(2):
                        s = 4 * quad + 2 * hp + i
                        last = pe.matmul(S[hp][:, i, :], ko[u][:, s, j * C:(j + 1) * C],
                                         qo[u][:, s, half * CH:(half + 1) * CH], start=True, stop=True)
                    last.then_inc(s_ready, 1)

                def values(b, u, k, hp):
                    g, j = divmod(k, 8)
                    pe.wait_ge(p_ready, 64 * b + 2 * k + hp + 1)
                    if j == 0:
                        wait_if(pe, grp_saved, 4 * b + g)
                    for i in range(2):
                        last = pe.matmul(pv_acc[hp][64 * i:64 * i + 64, :], rvb[u][:, j, :], P[k % 2][:, 2 * hp + i, :],
                                         start=(j == 0), stop=(j == 7))
                    if hp:
                        last.then_inc(pv_done, 1)

                pe.wait_ge(op_in[0], 192)
                for n in range(MAX_UNITS):
                    fill(("max", n), -1, 1, n, n % 2).then_inc(side_ready, 1)
                fill(("rows", 0), -1, 1, MAX_UNITS, 0).then_inc(side_ready, 1)

                def slot(b, u, last):
                    post = not isinstance(b, int) or b > 0
                    at = 0
                    pe.wait_ge(row_in[u], 24 * (b - u) + 48)
                    pe.wait_ge(rv_ready, b + 1)
                    for hp in range(2):
                        scores(b, u, 0, hp)
                    for k in range(STEPS):
                        if k == FIRST_MAX and not last:
                            pe.wait_ge(op_in[1 - u], 96 * (b + 1 - (1 - u)) + 192)
                        work = side_work(k, post, not last)
                        for part in range(4):
                            for w in work[part * len(work) // 4:(part + 1) * len(work) // 4]:
                                fill(w, b, u, side_base(b) + at, (u + 1 + at) % 2).then_inc(side_ready, 1)
                                at += 1
                            if part % 2:
                                values(b, u, k, part // 2)
                            elif k + 1 < STEPS:
                                scores(b, u, k + 1, part // 2)

                over(pe, B, slot)
                pe.wait_ge(grp_saved, 4 * B)
                for at, w in enumerate([("tokens", k) for k in range(8)] + [("back", 0), ("back", 1), ("wout", 0), ("wout", 1)]):
                    fill(w, B, 0, side_base(B) - SIDE1 + at, at % 2).then_inc(side_ready, 1)

            @block.vector
            def _(v):
                def drain(w, b, at, bank):
                    kind, n = w
                    v.wait_ge(side_ready, at + 1)
                    if kind == "max":
                        v.reduce_max(mx[:, n // 2, n % 2:n % 2 + 1], side[bank][:, :], AX.X).then_inc(side_saved, 1)
                        if n == MAX_UNITS - 1:
                            v.wait_ge(side_saved, at + 1)
                            v.tensor_reduce(negmax[:, :], mx[:, :, :], AX.X, ALU.max, negate=True).then_inc(row_step, 1)
                    elif kind == "rows":
                        base = 4 * (b + 1)
                        src = side[bank][0:64, 0:C]
                        rows_free(b)
                        v.tensor_copy(mrow[:, 0, :], src).then_inc(row_step, 1)
                        v.wait_ge(row_step, base + 2)
                        v.tensor_tensor(mleft[:, :], src, mrow[:, 0, :], ALU.subtract).then_inc(row_step, 1)
                        v.wait_ge(row_step, base + 3)
                        v.tensor_copy(mrow[:, 1, :], mleft[:, :]).then_inc(row_step, 1)
                        v.wait_ge(row_step, base + 4)
                        v.tensor_tensor(mrow[:, 2, :], mleft[:, :], mrow[:, 1, :], ALU.subtract).then_inc(row_ready, 1)
                        v.sem_inc(side_saved, 1)
                    elif kind == "tokens":
                        if n == 0:
                            wait_if(v, out_ready, b - 1)
                        v.tensor_copy(numT[:, n, :].rearrange("p (s d) -> p s d", d=RH * DH),
                                      side[bank][:, :].rearrange("p (s w) -> p s w", w=VW)[:, :, 0:RH * DH])
                        v.reciprocal(recT[:, 8 * n:8 * n + 8], side[bank][:, RH * DH::VW]).then_inc(side_saved, 1)
                    elif kind == "back":
                        v.tensor_copy(oc[:, n * CH:(n + 1) * CH], side[bank][:, :]).then_inc(side_saved, 1)
                    else:
                        xb = X[:, bass.ds((b - 1) * N + n * CH, CH)]
                        v.tensor_tensor(xb, xb, side[bank][:, :], ALU.add).then_inc(side_saved, 1)

                def rows_free(b):
                    if not isinstance(b, int) or b >= 0:
                        v.wait_ge(row_in[U[0]], 24 * (b - U[0]) + 48)

                U = [0]
                for n in range(MAX_UNITS):
                    drain(("max", n), -1, n, n % 2)
                drain(("rows", 0), -1, MAX_UNITS, 0)

                def slot(b, u, last):
                    post = not isinstance(b, int) or b > 0
                    U[0] = u
                    wait_if(v, pv_done, 32 * b - 32)
                    v.tensor_copy(rvb[u][:, :, 0:RH * DH], RV[:, bass.ds(8 * b, 8), :]).then_inc(rv_ready, 1)
                    at = 0
                    for k in range(STEPS):
                        if k == SUM_AT and post:
                            v.wait_ge(esum_ready, b)
                            v.reciprocal(sm1[:, :], sm1[:, :]).then_inc(rsum_ready, 1)
                        for w in side_work(k, post, not last):
                            drain(w, b, side_base(b) + at, (u + 1 + at) % 2)
                            at += 1

                over(v, B, slot)
                for at, w in enumerate([("tokens", k) for k in range(8)] + [("back", 0), ("back", 1), ("wout", 0), ("wout", 1)]):
                    if at == 8:
                        v.wait_ge(esum_ready, B)
                        v.reciprocal(sm1[:, :], sm1[:, :]).then_inc(rsum_ready, 1)
                    drain(w, B, side_base(B) - SIDE1 + at, at % 2)

            @block.scalar
            def _(a):
                def exps(b, k):
                    for hp in range(2):
                        a.wait_ge(s_ready, 64 * b + 2 * k + hp + 1)
                        wait_if(a, pv_done, 32 * b + k - 1)
                        a.activation(P[k % 2][:, 2 * hp:2 * hp + 2, :], S[hp][:, :, :], ACT.Exp).then_inc(p_ready, 1)

                def save(b, g, post, last):
                    quad, half = divmod(g, 2)
                    cols = slice(half * CH, (half + 1) * CH)
                    a.wait_ge(pv_done, 32 * b + 8 * g + 8)
                    if g == 0 and post:
                        a.wait_ge(side_ready, side_at(b, 7, ("tokens", 7), following=not last))
                    a.copy(sums[:, 2 * quad, cols], pv_acc[0][:, :])
                    a.copy(sums[:, 2 * quad + 1, cols], pv_acc[1][:, :]).then_inc(grp_saved, 1)

                def softmax2(b):
                    a.wait_ge(sim_ready, b + 1)
                    a.activation(sim[:, :, 0], sm1[:, :], ACT.Relu, scale=-1.0).then_inc(far_ready, 1)
                    a.activation(sim[:, :, 1], sm1[:, :], ACT.Relu).then_inc(far_ready, 1)
                    a.wait_ge(far_ready, 2 * b + 2)
                    a.activation(sim[:, :, :], sim[:, :, :], ACT.Exp, scale=-SCALE).then_inc(e_ready, 1)

                def slot(b, u, last):
                    post = not isinstance(b, int) or b > 0
                    exps(b, 0)
                    for k in range(STEPS):
                        if k + 1 < STEPS:
                            exps(b, k + 1)
                        if k == EXP_AT and post:
                            softmax2(b - 1)
                        if k % 8 == 7:
                            save(b, k // 8, post, last)

                over(a, B, slot)
                softmax2(B - 1)


def phase_norm(nc, K, X, Y, tag):
    with Mem(nc, tag) as m:
        ln = LayerNorm(m, K, X)
        with nc.Block() as block:
            @block.sync
            def _(sp):
                over(sp, NCH, lambda n, u, last: ln.sync(sp, n, u))

            @block.gpsimd
            def _(g):
                over(g, NCH, lambda n, u, last: ln.gpsimd(g, n, u))

            @block.scalar
            def _(a):
                over(a, NCH, lambda n, u, last: ln.scalar(a, n, u))

            @block.tensor
            def _(pe):
                def step(n, u, last):
                    if not last:
                        ln.tensor_front(pe, n + 1, 1 - u)
                    ln.tensor_back(pe, n, u)

                ln.tensor_front(pe, 0, 0)
                over(pe, NCH, step)

            @block.vector
            def _(v):
                def step(n, u, last):
                    if not last:
                        ln.vector_stats(v, n + 1, 1 - u)
                    ln.vector_save(v, n, Y[:, bass.ds(n * CH, CH)])

                ln.vector_stats(v, 0, 0)
                over(v, NCH, step)



E6 = 6
NP11 = 11
F = 341
FT = 16
PARTITIONS_OF_6 = [(6,), (5, 1), (4, 2), (4, 1, 1), (3, 3), (3, 2, 1), (3, 1, 1, 1), (2, 2, 2), (2, 2, 1, 1),
                   (2, 1, 1, 1, 1), (1, 1, 1, 1, 1, 1)]


def partition_weights():
    import numpy as np
    w = np.zeros((NP11, E6), np.float32)
    for i, parts in enumerate(PARTITIONS_OF_6):
        for j, part in enumerate(parts):
            w[i, j] = part / 6
    return w


def phase_router(nc, K, D, Y, wcol, b2w):
    with Mem(nc, "rt") as m:
        rw = m.sb("rw", [C, NP11])
        pwx = m.sb("pwx", [NP11, FT * C])
        pw6 = m.sb("pw6", [NP11, E6])
        b2 = m.sb("b2", [E6, C])
        mean = m.sb("mean", [C, B])
        p = m.sb("p", [B, NP11])
        rev = m.sb("rev", [B, NP11])
        t1, oh1, oh2 = m.sb("t1", [B, NP11]), m.sb("oh1", [B, NP11]), m.sb("oh2", [B, NP11])
        cv = m.sb("cv", [B, 8])
        wT = m.sb("wT", [NP11, B])
        ew, ewt = m.sb("ew", [E6, B]), m.sb("ewt", [E6, B])
        wraw = m.sb("wraw", [C, FT, B])
        pl = m.ps("pl", [B, NP11])
        pt = m.ps("pt", [NP11, B])
        px = m.ps("px", [C, FT, B])
        p6 = m.ps("p6", [E6, B])
        pb = m.ps("pb", [C, B])
        w_in, vec, pe_s, act, rev_ready = (m.sem(x) for x in ("w_in", "vec", "pe", "act", "rev_ready"))
        mean_ready, max_ready, wt_ready, w11_ready, ew_ready = (
            m.sem(x) for x in ("mean_ready", "max_ready", "wt_ready", "w11_ready", "ew_ready"))
        NM, SUM, V1, V2, R1, S = (cv[:, i:i + 1] for i in range(6))
        with nc.Block() as block:
            @block.sync
            def _(sp):
                for dst, src in ((rw, "router_wT"), (pwx, "pwx"), (pw6, "pw6"), (b2, "ffn_b2")):
                    sp.dma_start(dst[:, :], D[src]).then_inc(w_in, 16)

            @block.gpsimd
            def _(g):
                g.iota(rev[:, :], pattern=[[-1, NP11]], base=NP11, channel_multiplier=0,
                       allow_small_or_imprecise_dtypes=True).then_inc(rev_ready, 1)

            @block.tensor
            def _(pe):
                pe.wait_ge(w_in, 64)
                pe.wait_ge(mean_ready, 1)
                pe.matmul(pl[:, :], mean[:, :], rw[:, :], start=True, stop=True).then_inc(pe_s, 1)
                pe.wait_ge(w11_ready, 1)
                pe.transpose(pt[:, :], t1[:, :], K["ident"][0:B, 0:B]).then_inc(pe_s, 1)
                pe.wait_ge(wt_ready, 1)
                for f in range(FT):
                    pe.matmul(px[:, f, :], pwx[:, f * C:(f + 1) * C], wT[:, :], start=True, stop=True)
                pe.matmul(p6[:, :], pw6[:, :], wT[:, :], start=True, stop=True).then_inc(pe_s, 1)
                pe.wait_ge(ew_ready, 1)
                pe.matmul(pb[:, :], b2[:, :], ew[:, :], start=True, stop=True).then_inc(pe_s, 1)

            @block.scalar
            def _(a):
                a.wait_ge(max_ready, 1)
                a.activation(p[:, :], pl[:, :], ACT.Exp, bias=NM, accum_out=SUM).then_inc(act, 1)

            @block.vector
            def _(v):
                step = Chain(v, vec)
                for b in range(0, B, 4):
                    last = v.reduce_sum(mean[:, b:b + 4], Y[:, b * N:(b + 4) * N].rearrange("c (b n) -> c b n", n=N), AX.X)
                    step(last)
                step(v.tensor_scalar(mean[:, :], mean[:, :], 1.0 / N, None, ALU.mult))
                v.sem_inc(mean_ready, 1)
                v.wait_ge(pe_s, 1)
                step(v.tensor_reduce(NM, pl[:, :], AX.X, ALU.max, negate=True))
                v.sem_inc(max_ready, 1)
                v.wait_ge(act, 1)
                v.wait_ge(rev_ready, 1)
                step(v.reciprocal(SUM, SUM))
                step(v.tensor_scalar(p[:, :], p[:, :], SUM, None, ALU.mult))
                for value, onehot in ((V1, oh1), (V2, oh2)):
                    step(v.reduce_max(value, p[:, :], AX.X))
                    step(v.scalar_tensor_tensor(t1[:, :], p[:, :], value, rev[:, :], ALU.is_equal, ALU.mult))
                    step(v.reduce_max(R1, t1[:, :], AX.X))
                    step(v.tensor_scalar(onehot[:, :], rev[:, :], R1, None, ALU.is_equal))
                    step(v.scalar_tensor_tensor(p[:, :], onehot[:, :], -2.0, p[:, :], ALU.mult, ALU.add))
                step(v.tensor_add(S, V1, V2))
                step(v.reciprocal(S, S))
                step(v.tensor_mul(V1, V1, S))
                step(v.tensor_mul(V2, V2, S))
                step(v.tensor_scalar(t1[:, :], oh1[:, :], V1, None, ALU.mult))
                step(v.scalar_tensor_tensor(t1[:, :], oh2[:, :], V2, t1[:, :], ALU.mult, ALU.add))
                v.sem_inc(w11_ready, 1)
                v.wait_ge(pe_s, 2)
                step(v.tensor_copy(wT[:, :], pt[:, :]))
                v.sem_inc(wt_ready, 1)
                v.wait_ge(pe_s, 3)
                step(v.tensor_copy(wraw[:, :, :], px[:, :, :]))
                step(v.scalar_tensor_tensor(wcol[:, :, :], wraw[:, :, :], 1e-6, wraw[:, :, :], ALU.is_gt, ALU.mult))
                step(v.tensor_copy(ewt[:, :], p6[:, :]))
                step(v.scalar_tensor_tensor(ew[:, :], ewt[:, :], 1e-6, ewt[:, :], ALU.is_gt, ALU.mult))
                v.sem_inc(ew_ready, 1)
                v.wait_ge(pe_s, 4)
                step(v.tensor_copy(b2w[:, :], pb[:, :]))


def phase_ffn(nc, K, D, X, Y, wcol, b2w):
    R = 4
    LEAD = 2
    with Mem(nc, "ff") as m:
        w1 = m.sb("w1", [C, FT, C])
        w2 = m.sb("w2", [C, FT, C])
        b1 = m.sb("b1", [C, FT])
        w2s = [m.sb(f"w2s{u}", [C, FT, C]) for u in range(2)]
        hs = [m.sb(f"hs{r}", [C, CH]) for r in range(R)]
        ph = [m.ps(f"ph{r}", [C, CH]) for r in range(R)]
        po = [m.ps(f"po{h}", [C, CH]) for h in range(2)]
        w_in, w2_ready, h_mm, h_ready, h_used, o_mm, x_ready = (
            m.sem(x) for x in ("w_in", "w2_ready", "h_mm", "h_ready", "h_used", "o_mm", "x_ready"))
        ITEMS = 2 * FT
        with nc.Block() as block:
            @block.sync
            def _(sp):
                sp.dma_start(w1[:, :, :], D["W1"]).then_inc(w_in, 16)
                sp.dma_start(w2[:, :, :], D["W2"]).then_inc(w_in, 16)
                sp.dma_start(b1[:, :], D["b1"]).then_inc(w_in, 16)

            @block.tensor
            def _(pe):
                pe.wait_ge(w_in, 48)

                def up(b, j):
                    wait_if(pe, h_ready, ITEMS * b + j - R + 1)
                    half, f = divmod(j, FT)
                    pe.matmul(ph[j % R][:, :], w1[:, f, :], Y[:, bass.ds(b * N + half * CH, CH)],
                              start=True, stop=True).then_inc(h_mm, 1)

                def batch(b, u, last):
                    pe.wait_ge(w2_ready, b + 1)
                    for j in range(ITEMS):
                        half, f = divmod(j, FT)
                        if j + LEAD < ITEMS:
                            up(b, j + LEAD)
                        elif not last:
                            up(b + 1, j + LEAD - ITEMS)
                        if f == 0:
                            wait_if(pe, x_ready, 2 * b + half - 1)
                        pe.wait_ge(h_ready, ITEMS * b + j + 1)
                        done = pe.matmul(po[half][:, :], w2s[u][:, f, :], hs[j % R][:, :],
                                         start=(f == 0), stop=(f == FT - 1)).then_inc(h_used, 1)

                for j in range(LEAD):
                    up(0, j)
                over_batches(pe, batch)

            @block.scalar
            def _(a):
                a.wait_ge(w_in, 48)

                def batch(b, u, last):
                    for j in range(ITEMS):
                        a.wait_ge(h_mm, ITEMS * b + j + 1)
                        wait_if(a, h_used, ITEMS * b + j - R + 1)
                        a.activation(hs[j % R][:, :], ph[j % R][:, :], ACT.Gelu,
                                     bias=b1[:, j % FT:j % FT + 1]).then_inc(h_ready, 1)

                over_batches(a, batch)

            @block.vector
            def _(v):
                v.wait_ge(w_in, 48)

                def scale(b, u):
                    wait_if(v, h_used, ITEMS * (b - 1))
                    v.tensor_tensor(w2s[u][:, :, :], w2[:, :, :],
                                    wcol[:, :, bass.ds(b, 1)].to_broadcast([C, FT, C]), ALU.mult).then_inc(w2_ready, 1)

                def batch(b, u, last):
                    for half in range(2):
                        v.wait_ge(h_used, ITEMS * b + FT * (half + 1))
                        xb = X[:, bass.ds(b * N + half * CH, CH)]
                        v.scalar_tensor_tensor(xb, po[half][:, :], b2w[:, bass.ds(b, 1)], xb, ALU.add, ALU.add)\
                         .then_inc(x_ready, 1)
                        if half == 0 and not last:
                            scale(b + 1, 1 - u)

                scale(0, 0)
                over_batches(v, batch)



G8 = 8
H4 = 4


def phase_gqa(nc, K, D, X, Y):
    GH = G8 * H4
    TL = N // C
    with Mem(nc, "gq") as m:
        wk = m.sb("wk", [C, G8, C])
        wqT = m.sb("wqT", [C, GH, C])
        wvT = m.sb("wvT", [C, G8, C])
        wo = m.sb("wo", [C, G8, C])
        bkT, bvT, bqT, bo = m.sb("bkT", [C, G8]), m.sb("bvT", [C, G8]), m.sb("bqT", [C, GH]), m.sb("bo", [C, 1])
        xsum = m.sb("xsum", [C, B])
        ksum = m.sb("ksum", [C, G8, B])
        bk_ = m.sb("bqk", [C, GH, B])
        sw = m.sb("sw", [C, B, GH])
        sb_ = m.sb("sbias", [C, B, GH])
        vo = m.sb("vo", [C, G8, C])
        bvo = m.sb("bvo", [C, G8])
        ys = [m.sb(f"ys{u}", [C, N]) for u in range(2)]
        sc = m.sb("sc", [C, TL, GH])
        red = m.sb("red", [C, TL * H4])
        wsum = m.sb("wsum", [C, G8])
        mix = m.sb("mix", [C, G8, C])
        A = [m.sb(f"A{u}", [C, C]) for u in range(2)]
        bias = [m.sb(f"bias{u}", [C, 1]) for u in range(2)]
        bt = m.sb("bt", [C, G8])
        pa = m.ps("pa", [C, CH])
        pc = m.ps("pc", [C, CH])
        pv = [m.ps(f"pv{h}", [C, 4, C]) for h in range(2)]
        psc = m.ps("psc", [C, TL, GH])
        pws = m.ps("pws", [C, TL, GH])
        po = [m.ps(f"po{h}", [C, CH]) for h in range(2)]
        w_in, vec, prep_mm, xs_ready, ks_ready, prep_done = (m.sem(x) for x in ("w_in", "vec", "prep_mm", "xs_ready", "ks_ready", "prep_done"))
        y_in = [m.sem("y_in0"), m.sem("y_in1")]
        s_mm, sub_ready, sub_ready2, e_ready, w_ready, ws_mm, a_ready, o_mm, x_ready, dstep = (
            m.sem(x) for x in ("s_mm", "biased", "below_max", "e_ready", "w_ready", "ws_mm", "a_ready", "o_mm", "x_ready", "dstep"))
        NW = 9

        def y_count(b, u):
            return (b // 2 + 1) * 16 if isinstance(b, int) else 8 * b + (16 - 8 * u)

        with nc.Block() as block:
            @block.sync
            def _(sp):
                for dst, src in ((wk, "Wk"), (wqT, "WqT"), (wvT, "WvT"), (wo, "Wo")):
                    sp.dma_start(dst[:, :, :], D[src]).then_inc(w_in, 16)
                for dst, src in ((bkT, "bkT"), (bvT, "bvT"), (bqT, "bqT"), (bo, "bo")):
                    sp.dma_start(dst[:, :], D[src]).then_inc(w_in, 16)

                def step(b, u, last):
                    wait_if(sp, s_mm, b - 1)
                    sp.dma_start(ys[u][:, :], Y[:, bass.ds(b * N, N)]).then_inc(y_in[u], 16)

                over(sp, B, step)

            @block.tensor
            def _(pe):
                pe.wait_ge(w_in, 128)
                pe.wait_ge(xs_ready, 1)
                for g in range(G8):
                    last = pe.matmul(pc[:, g * B:(g + 1) * B], wk[:, g, :], xsum[:, :], start=True, stop=True)
                last.then_inc(prep_mm, 1)
                for g in range(G8):
                    last = pe.matmul(pv[g // 4][:, g % 4, :], wvT[:, g, :], wo[:, g, :], start=True, stop=True)
                last.then_inc(prep_mm, 1)
                for g in range(G8):
                    last = pe.matmul(pws[:, 0, g:g + 1], wo[:, g, :], bvT[:, g:g + 1], start=True, stop=True)
                last.then_inc(prep_mm, 1)
                pe.wait_ge(ks_ready, 1)
                for i in range(GH):
                    last = pe.matmul(pa[:, i * B:(i + 1) * B], wqT[:, i, :], ksum[:, i // H4, :], start=True, stop=True)
                last.then_inc(prep_mm, 1)
                pe.wait_ge(ks_ready, 2)
                pe.matmul(pc[:, :], K["ones"][:, :], bk_[:, :, :].rearrange("p i b -> p (i b)"), start=True, stop=True).then_inc(prep_mm, 1)
                pe.wait_ge(prep_done, 1)

                def scores(b, u):
                    pe.wait_ge(y_in[u], y_count(b, u))
                    wait_if(pe, sub_ready, b)
                    for t in range(TL):
                        last = pe.matmul(psc[:, t, :], ys[u][:, t * C:(t + 1) * C], sw[:, bass.ds(b, 1), :].rearrange("p o g -> p (o g)"),
                                         start=True, stop=True)
                    last.then_inc(s_mm, 1)

                scores(0, 0)

                def step(b, u, last):
                    if not last:
                        scores(b + 1, 1 - u)
                    pe.wait_ge(w_ready, b + 1)
                    pe.matmul(pws[:, :, :], K["ones"][:, :], sc[:, :, :], start=True, stop=True).then_inc(ws_mm, 1)
                    pe.wait_ge(a_ready, b + 1)
                    for h in range(2):
                        wait_if(pe, x_ready, 2 * b - 1 + h)
                        pe.matmul(po[h][:, :], A[u][:, :], Y[:, bass.ds(b * N + h * CH, CH)], start=True, stop=True).then_inc(o_mm, 1)

                over(pe, B, step)

            @block.scalar
            def _(a):
                with a.Fori(0, B) as b:
                    a.wait_ge(sub_ready2, b + 1)
                    a.activation(sc[:, :, :], sc[:, :, :], ACT.Exp, scale=C ** -0.5).then_inc(e_ready, 1)

            @block.vector
            def _(v):
                step0 = Chain(v, vec)
                v.wait_ge(w_in, 128)
                for b in range(0, B, 4):
                    step0(v.reduce_sum(xsum[:, b:b + 4], Y[:, b * N:(b + 4) * N].rearrange("c (b n) -> c b n", n=N), AX.X))
                v.sem_inc(xs_ready, 1)
                step0(v.tensor_scalar(bkT[:, :], bkT[:, :], float(N), None, ALU.mult))
                v.wait_ge(prep_mm, 1)
                step0(v.tensor_tensor(ksum[:, :, :], pc[:, 0:G8 * B].rearrange("p (g b) -> p g b", b=B),
                                      bkT[:, :].rearrange("p (g o) -> p g o", o=1).to_broadcast([C, G8, B]), ALU.add))
                v.sem_inc(ks_ready, 1)
                for g in range(G8):
                    last = v.tensor_tensor(bk_[:, g * H4:(g + 1) * H4, :],
                                           ksum[:, g:g + 1, :].to_broadcast([C, H4, B]),
                                           bqT[:, g * H4:(g + 1) * H4].rearrange("p (g o) -> p g o", o=1).to_broadcast([C, H4, B]), ALU.mult)
                step0(last)
                v.sem_inc(ks_ready, 1)
                v.wait_ge(prep_mm, 3)
                for h in range(2):
                    step0(v.tensor_copy(vo[:, 4 * h:4 * h + 4, :], pv[h][:, :, :]))
                step0(v.tensor_copy(bvo[:, :], pws[:, 0, 0:G8]))
                v.wait_ge(prep_mm, 5)
                for dst, src in ((sw, pa), (sb_, pc)):
                    for h in range(H4):
                        step0(v.tensor_copy(dst[:, :, h * G8:(h + 1) * G8],
                                            src[:, :].rearrange("p (g h b) -> p h b g", h=H4, b=B)[:, h, :, :]))
                v.sem_inc(prep_done, 1)

                def softmax(b):
                    st = Chain(v, dstep, NW * b)
                    scv = sc[:, :, :].rearrange("p t (h g) -> p (t h) g", g=G8)
                    v.wait_ge(s_mm, b + 1)
                    wait_if(v, ws_mm, b)
                    v.tensor_tensor(sc[:, :, :], psc[:, :, :], sb_[:, bass.ds(b, 1), :].to_broadcast([C, TL, GH]), ALU.add)\
                     .then_inc(sub_ready, 1)
                    v.wait_ge(sub_ready, b + 1)
                    st(v.reduce_max(red[:, :], scv, AX.X))
                    v.tensor_tensor(scv, scv, red[:, :].rearrange("p (t o) -> p t o", o=1).to_broadcast([C, TL * H4, G8]),
                                    ALU.subtract).then_inc(sub_ready2, 1)
                    v.wait_ge(e_ready, b + 1)
                    st(v.reduce_sum(red[:, :], scv, AX.X))
                    st(v.reciprocal(red[:, :], red[:, :]))
                    v.tensor_tensor(scv, scv, red[:, :].rearrange("p (t o) -> p t o", o=1).to_broadcast([C, TL * H4, G8]),
                                    ALU.mult).then_inc(w_ready, 1)
                    return st

                def mixing(b, u, st):
                    v.wait_ge(ws_mm, b + 1)
                    st(v.reduce_sum(wsum[:, :], pws[:, :, :].rearrange("p t (h g) -> p g (t h)", g=G8), AX.X))
                    st(v.tensor_tensor(mix[:, :, :], vo[:, :, :], wsum[:, :].rearrange("p (g o) -> p g o", o=1).to_broadcast([C, G8, C]), ALU.mult))
                    st(v.tensor_mul(bt[:, :], bvo[:, :], wsum[:, :]))
                    wait_if(v, o_mm, 2 * b - 2)
                    st(v.reduce_sum(A[u][:, :], mix[:, :, :].rearrange("p g n -> p n g"), AX.X))
                    st(v.reduce_sum(bias[u][:, :], bt[:, :], AX.X))
                    st(v.tensor_add(bias[u][:, :], bias[u][:, :], bo[:, :]))
                    v.sem_inc(a_ready, 1)
                    assert st.n == NW

                def step(b, u, last):
                    mixing(b, u, softmax(b))
                    for h in range(2):
                        v.wait_ge(o_mm, 2 * b + h + 1)
                        xb = X[:, bass.ds(b * N + h * CH, CH)]
                        v.scalar_tensor_tensor(xb, po[h][:, :], bias[u][:, :], xb, ALU.add, ALU.add).then_inc(x_ready, 1)

                over(v, B, step)



E8 = 8
ITERS = 8
TOP = N // E8
NT = T // C
CLIP = 1e-10


def phase_route(nc, K, D, Y):
    with Mem(nc, "sk") as m:
        gw = m.sb("gw", [C, E8])
        ys = [m.sb(f"ys{u}", [C, N]) for u in range(2)]
        G = m.sb("G", [C, NT, E8])
        tmp = m.sb("tmp", [C, NT, E8])
        cg = m.sb("cg", [C, NT, E8])
        mask = m.sb("mask", [C, NT, E8], BF16)
        oneb = m.sb("oneb", [C, C], BF16)
        lower = m.sb("lower", [C, C], BF16)
        uu = m.sb("uu", [C, NT])
        ss = m.sb("ss", [C, NT])
        vv = m.sb("vv", [C, E8])
        part = m.sb("part", [C, E8])
        thr = m.sb("thr", [C, E8], mybir.dt.int32)
        cand = m.sb("cand", [C, E8], mybir.dt.int32)
        bit = m.sb("bit", [C, E8], mybir.dt.int32)
        cnt = m.sb("cnt", [C, E8])
        need = m.sb("need", [C, E8])
        tot = m.sb("tot", [C, NT, E8])
        cum = m.sb("cum", [C, E8, NT])
        zero = m.sb("zero", [C, NT])
        wT = m.sb("wT", [C, E8, C])
        pg = [m.ps(f"pg{u}", [C, N // C, E8]) for u in range(2)]
        pr = m.ps("pr", [C, E8])
        pcn = m.ps("pcn", [C, 16, E8])
        pp = [m.ps(f"pp{h}", [C, 64, E8]) for h in range(2)]
        pq = [m.ps(f"pq{h}", [C, 64, E8]) for h in range(2)]
        g_in, const_ready, pool = m.sem("g_in"), m.sem("const_ready"), m.sem("pool")
        y_in = [m.sem("y_in0"), m.sem("y_in1")]
        g_mm, g_saved, vec, pe_s, v_ready = (m.sem(x) for x in ("g_mm", "g_saved", "vec", "pe", "v_ready"))
        out_done, wt_ready = m.sem("out_done"), m.sem("wt_ready")
        bisect_mm, bisect_vec = m.sem("bisect_mm"), m.sem("bisect_vec")

        def bc_e(v8):
            return v8.rearrange("p (o e) -> p o e", o=1).to_broadcast([C, NT, E8])

        def bc_t(v):
            return v.rearrange("p (t o) -> p t o", o=1).to_broadcast([C, NT, E8])

        def y_count(b, u):
            return (b // 2 + 1) * 16 if isinstance(b, int) else 8 * b + (16 - 8 * u)

        BITS = 30
        with nc.Block() as block:
            @block.sync
            def _(sp):
                sp.dma_start(gw[:, :], D["gate_w"]).then_inc(g_in, 16)

                def step(b, u, last):
                    wait_if(sp, g_mm, b - 1)
                    sp.dma_start(ys[u][:, :], Y[:, bass.ds(b * N, N)]).then_inc(y_in[u], 16)

                over(sp, B, step)
                sp.wait_ge(wt_ready, 1)
                for t in range(16):
                    sp.dma_start(D["w"][:, :].rearrange("e (k t n) -> t e k n", t=16, n=C)[t],
                                 wT[E8 * t:E8 * t + E8, :, :]).then_inc(out_done, 16)
                sp.wait_ge(out_done, 16 * 16)

            @block.gpsimd
            def _(g):
                step = Chain(g, pool)
                step(g.memset(oneb[:, :], 1.0))
                step(g.memset(lower[:, :], 1.0))
                step(g.memset(zero[:, :], 0.0))
                step(g.affine_select(out=lower[:, :], in_=lower[:, :], pattern=[[1, C]], base=-1,
                                     channel_multiplier=-1, compare_op=ALU.is_ge, fill=0.0))
                g.sem_inc(const_ready, 1)

            @block.tensor
            def _(pe):
                pe.wait_ge(g_in, 16)
                pe.wait_ge(const_ready, 1)

                def step(b, u, last):
                    pe.wait_ge(y_in[u], y_count(b, u))
                    wait_if(pe, g_saved, b - 1)
                    for t in range(N // C):
                        done = pe.matmul(pg[u][:, t, :], ys[u][:, t * C:(t + 1) * C], gw[:, :], start=True, stop=True)
                    done.then_inc(g_mm, 1)

                over(pe, B, step)
                for i in range(ITERS):
                    pe.wait_ge(v_ready, i + 1)
                    pe.matmul(pr[:, :], K["ones"][:, :], part[:, :], start=True, stop=True).then_inc(pe_s, 1)
                with pe.Fori(0, BITS + 1) as i:
                    pe.wait_ge(bisect_vec, i + 1)
                    for c in range(8):
                        last = pe.matmul(pcn[:, :, :], oneb[:, :], mask[:, 16 * c:16 * c + 16, :], start=(c == 0), stop=(c == 7))
                    last.then_inc(bisect_mm, 1)
                pe.wait_ge(v_ready, ITERS + 1)
                for h in range(2):
                    pe.matmul(pp[h][:, :, :], lower[:, :], mask[:, 64 * h:64 * h + 64, :], start=True, stop=True)
                    last = pe.matmul(pq[h][:, :, :], oneb[:, :], mask[:, 64 * h:64 * h + 64, :], start=True, stop=True)
                last.then_inc(pe_s, 1)
                pe.wait_ge(v_ready, ITERS + 2)
                for c in range(8):
                    last = pe.transpose(pq[c // 4][:, :, :].rearrange("p t e -> p (t e)")[:, (c % 4) * C:(c % 4 + 1) * C],
                                        tmp[:, 16 * c:16 * c + 16, :].rearrange("p t e -> p (t e)"), K["ident"][:, :])
                last.then_inc(pe_s, 1)

            @block.vector
            def _(v):
                with v.Fori(0, B // 2) as i:
                    for u in range(2):
                        b = 2 * i + u
                        v.wait_ge(g_mm, b + 1)
                        v.tensor_scalar(G[:, bass.ds(8 * b, 8), :], pg[u][:, :, :], CLIP, None, ALU.max).then_inc(g_saved, 1)
                v.wait_ge(g_saved, B)
                step = Chain(v, vec)
                gt = G[:, :, :].rearrange("p t e -> p e t")
                for i in range(ITERS):
                    if i == 0:
                        step(v.reduce_sum(part[:, :], gt, AX.X))
                    else:
                        step(v.tensor_tensor(tmp[:, :, :], G[:, :, :], bc_t(uu[:, :]), ALU.mult))
                        step(v.reduce_sum(part[:, :], tmp[:, :, :].rearrange("p t e -> p e t"), AX.X))
                    v.sem_inc(v_ready, 1)
                    v.wait_ge(pe_s, i + 1)
                    step(v.reciprocal(vv[:, :], pr[:, :]))
                    step(v.tensor_tensor(tmp[:, :, :], G[:, :, :], bc_e(vv[:, :]), ALU.mult))
                    step(v.reduce_sum(ss[:, :], tmp[:, :, :], AX.X))
                    step(v.reciprocal(uu[:, :], ss[:, :]))
                step(v.tensor_tensor(cg[:, :, :], tmp[:, :, :], bc_t(uu[:, :]), ALU.mult))
                step(v.tensor_tensor(tmp[:, :, :], bc_t(ss[:, :]), tmp[:, :, :], ALU.subtract))
                step(v.tensor_tensor(tmp[:, :, :], tmp[:, :, :], bc_t(uu[:, :]), ALU.mult))
                step(v.tensor_scalar(tmp[:, :, :], tmp[:, :, :], -1.0, 1.0, ALU.mult, ALU.add))
                step(v.tensor_tensor(tmp[:, :, :], tmp[:, :, :], cg[:, :, :], ALU.subtract))
                step(v.scalar_tensor_tensor(tmp[:, :, :].rearrange("p t e -> p (t e)"), cg[:, :, :].rearrange("p t e -> p (t e)"), 0.5,
                                            tmp[:, :, :].rearrange("p t e -> p (t e)"), ALU.is_gt, ALU.mult))
                step(v.tensor_tensor(cg[:, :, :], cg[:, :, :], tmp[:, :, :], ALU.add))
                step(v.memset(thr[:, :], 0))
                for i in range(BITS):
                    step(v.tensor_single_scalar(cand[:, :], thr[:, :], 1 << (BITS - 1 - i), ALU.bitwise_or))
                    v.tensor_tensor(mask[:, :, :], cg[:, :, :], bc_e(cand[:, :].bitcast(F32)), ALU.is_ge).then_inc(bisect_vec, 1)
                    v.wait_ge(bisect_mm, i + 1)
                    step(v.reduce_sum(cnt[:, :], pcn[:, :, :].rearrange("p t e -> p e t"), AX.X))
                    step(v.tensor_scalar(bit[:, :], cnt[:, :], float(TOP), float(1 << (BITS - 1 - i)), ALU.is_ge, ALU.mult))
                    step(v.tensor_tensor(thr[:, :], thr[:, :], bit[:, :], ALU.bitwise_or))
                thf = thr[:, :].bitcast(F32)
                v.tensor_tensor(mask[:, :, :], cg[:, :, :], bc_e(thf), ALU.is_gt).then_inc(bisect_vec, 1)
                v.wait_ge(bisect_mm, BITS + 1)
                step(v.reduce_sum(cnt[:, :], pcn[:, :, :].rearrange("p t e -> p e t"), AX.X))
                step(v.tensor_scalar(need[:, :], cnt[:, :], -1.0, float(TOP), ALU.mult, ALU.add))
                step(v.tensor_copy(G[:, :, :], mask[:, :, :]))
                step(v.tensor_tensor(mask[:, :, :], cg[:, :, :], bc_e(thf), ALU.is_equal))
                v.sem_inc(v_ready, 1)
                v.wait_ge(pe_s, ITERS + 1)
                for h in range(2):
                    step(v.tensor_copy(tot[:, 64 * h:64 * h + 64, :], pq[h][:, :, :]))
                for e in range(E8):
                    step(v.tensor_tensor_scan(cum[:, e, :], tot[:, :, e], zero[:, :], 0.0, ALU.add, ALU.add))
                for h in range(2):
                    step(v.tensor_tensor(tot[:, 64 * h:64 * h + 64, :], pp[h][:, :, :], tot[:, 64 * h:64 * h + 64, :], ALU.subtract))
                step(v.tensor_tensor(tot[:, :, :], tot[:, :, :], cum[:, :, :].rearrange("p e t -> p t e"), ALU.add))
                step(v.tensor_tensor(tot[:, :, :], tot[:, :, :], bc_e(need[:, :]), ALU.is_lt))
                step(v.tensor_tensor(tot[:, :, :], tot[:, :, :], mask[:, :, :], ALU.mult))
                step(v.tensor_tensor(G[:, :, :], G[:, :, :], tot[:, :, :], ALU.add))
                step(v.reduce_sum(uu[:, :], G[:, :, :], AX.X))
                step(v.tensor_scalar(uu[:, :], uu[:, :], 1.0, None, ALU.add))
                step(v.reciprocal(uu[:, :], uu[:, :]))
                step(v.scalar_tensor_tensor(tmp[:, :, :].rearrange("p t e -> p (t e)"), cg[:, :, :].rearrange("p t e -> p (t e)"), 0.5,
                                            G[:, :, :].rearrange("p t e -> p (t e)"), ALU.is_gt, ALU.mult))
                step(v.tensor_tensor(tmp[:, :, :], tmp[:, :, :], bc_t(uu[:, :]), ALU.mult))
                v.sem_inc(v_ready, 1)
                v.wait_ge(pe_s, ITERS + 2)
                for h in range(2):
                    step(v.tensor_copy(wT[:, 4 * h:4 * h + 4, :], pq[h][:, :, :].rearrange("p t e -> p (t e)").rearrange("p (k n) -> p k n", n=C)))
                v.sem_inc(wt_ready, 1)


def phase_experts(nc, K, D, X, Y):
    R = 4
    with Mem(nc, "ex") as m:
        ew = m.sb("ew", [C, E8, C])
        wb = [m.sb(f"wb{u}", [C, E8, CH]) for u in range(2)]
        xm = [m.sb(f"xm{r}", [C, CH]) for r in range(R)]
        po = [m.ps(f"po{u}", [C, CH]) for u in range(2)]
        e_in = m.sem("e_in")
        w_in = [m.sem("w_in0"), m.sem("w_in1")]
        xm_ready, xm_used, x_ready = m.sem("xm_ready"), m.sem("xm_used"), m.sem("x_ready")
        with nc.Block() as block:
            @block.sync
            def _(sp):
                sp.dma_start(ew[:, :, :], D["experts"]).then_inc(e_in, 16)

                def step(n, u, last):
                    wait_if(sp, xm_ready, 8 * n - 8)
                    sp.dma_start(wb[u][:, :, :], D["w"][:, bass.ds(n * CH, CH)].partition_broadcast(C)).then_inc(w_in[u], 16)

                over(sp, NCH, step)

            @block.tensor
            def _(pe):
                pe.wait_ge(e_in, 16)

                def step(n, u, last):
                    wait_if(pe, x_ready, n - 1)
                    for e in range(E8):
                        pe.wait_ge(xm_ready, 8 * n + e + 1)
                        pe.matmul(po[u][:, :], ew[:, e, :], xm[e % R][:, :], start=(e == 0), stop=(e == E8 - 1)).then_inc(xm_used, 1)

                over(pe, NCH, step)

            @block.vector
            def _(v):
                def add(n, u):
                    v.wait_ge(xm_used, 8 * n + 8)
                    xb = X[:, bass.ds(n * CH, CH)]
                    v.tensor_tensor(xb, xb, po[u][:, :], ALU.add).then_inc(x_ready, 1)

                def step(n, u, last):
                    v.wait_ge(w_in[u], (n // 2 + 1) * 16 if isinstance(n, int) else 8 * n + (16 - 8 * u))
                    for e in range(E8):
                        wait_if(v, xm_used, 8 * n + e - R + 1)
                        v.tensor_tensor(xm[e % R][:, :], Y[:, bass.ds(n * CH, CH)], wb[u][:, e, :], ALU.mult).then_inc(xm_ready, 1)
                        if e == 3 and (not isinstance(n, int) or n > 0):
                            add(n - 1, 1 - u)

                over(v, NCH, step)
                add(NCH - 1, 1)


def phase_store(nc, D, X):
    with Mem(nc, "store") as m:
        stored = [m.sem(f"stored{q}") for q in range(4)]
        with nc.Block() as block:
            @block.sync
            def _(sp):
                for q in range(4):
                    sp.dma_start(D["out"][4 * q:4 * q + 4].rearrange("b c n -> c b n"),
                                 X[:, q * 4 * N:(q + 1) * 4 * N].rearrange("c (b n) -> c b n", n=N)).then_inc(stored[q], 16)
                for q in range(4):
                    sp.wait_ge(stored[q], 16)


def build(nc, D):
    with ExitStack() as ctx:
        def sb(name, shape, dt=F32):
            return ctx.enter_context(nc.sbuf_tensor(name, shape, dt))

        K = {"ident": sb("ident", [C, C]), "ones": sb("ones", [C, C]),
             "neghalf": sb("neghalf", [C, C]), "mask8": sb("mask8", [C, C]),
             "eps": sb("eps", [C, 4]), "negone": sb("negone", [C, 4]),
             "stats": sb("bnstats", [C, NCH, 6])}
        X = sb("X", [C, T])
        D["proj"] = nc.dram_tensor("proj", [C, T], F32).ap()
        D["qk"] = nc.dram_tensor("qk", [2, 3, C, T], BF16).ap()
        D["w"] = nc.dram_tensor("w", [E8, T], F32).ap()
        D["u"] = nc.dram_tensor("u", [C, T // C, C], F32).ap()
        phase_constants(nc, K)
        phase_conv(nc, K, D, X)
        phase_linatt(nc, K, D, X)
        phase_linatt_norm(nc, K, D, X)
        with Mem(nc, "attn") as m:
            K["rv"] = m.sb("rv", [C, T // C, RH * DH])
            phase_attn_prep(nc, K, D, X)
            phase_attn(nc, K, D, X)
        with Mem(nc, "ffn") as m:
            Y = m.sb("Y", [C, T])
            wcol, b2w = m.sb("wcol", [C, FT, B]), m.sb("b2w", [C, B])
            phase_norm(nc, K, X, Y, "n2")
            phase_router(nc, K, D, Y, wcol, b2w)
            phase_ffn(nc, K, D, X, Y, wcol, b2w)
        with Mem(nc, "gqa") as m:
            Y = m.sb("Y", [C, T])
            phase_norm(nc, K, X, Y, "n3")
            phase_gqa(nc, K, D, X, Y)
        with Mem(nc, "moe") as m:
            Y = m.sb("Y", [C, T])
            phase_norm(nc, K, X, Y, "n4")
            phase_route(nc, K, D, Y)
            phase_experts(nc, K, D, X, Y)
        phase_store(nc, D, X)


def layout(inputs):
    import numpy as np
    x = {k: np.asarray(v) for k, v in inputs.items()}
    w = x["L0_conv_conv_w"]
    out = {"x": x["x"].reshape(B, C, N),
           "conv_w": w.reshape(C, 72),
           "conv_wt": np.tile(w.reshape(C, 8, 9).transpose(1, 2, 0), (16, 1, 1))}
    for k in ("bn1_gamma", "bn1_beta", "bn2_gamma", "bn2_beta", "prelu_a"):
        out["L0_conv_" + k] = x["L0_conv_" + k]
    out["w_qkvT"] = x["L1_conv_w_qkv"].reshape(16, 3, 8, C).transpose(3, 1, 0, 2).reshape(C, 3, C)
    out["w_projT"] = x["L1_conv_w_proj"].reshape(C, 2, C).transpose(2, 1, 0)
    out["w_pwT"] = np.tile(x["L1_conv_w_pw"].reshape(4, 4, 3, 8, 8).transpose(4, 2, 0, 1, 3).reshape(8, 3, 4, 32), (16, 1, 1, 1))
    out["w_taps"] = tap_weights(x["L1_conv_w_dw"])
    out["w_qtaps"] = x["L1_conv_w_dw"].reshape(16, PARTS, HD, TAPS)[:, 0].reshape(C, TAPS)
    for k in ("bn_gamma", "bn_beta"):
        out["L1_conv_" + k] = x["L1_conv_" + k]
    for k in ("wq_s", "wk_s", "wv_r", "w_out"):
        out[k] = x["L2_attn_" + k]
    out["wq_rT"] = x["L2_attn_wq_r"].T
    out["wk_retT"] = np.tile(x["L2_attn_wk_ret"].T, (8, 8))
    out["router_wT"] = x["L2_ffn_router_w"].T
    out["pw6"] = partition_weights()
    pad = FT * C - E6 * F
    out["pwx"] = np.pad(np.repeat(partition_weights(), F, axis=1), ((0, 0), (0, pad)))
    out["ffn_b2"] = x["L2_ffn_b2"]
    out["W1"] = np.pad(x["L2_ffn_W1"].transpose(1, 0, 2).reshape(C, E6 * F), ((0, 0), (0, pad))).reshape(C, FT, C)
    out["b1"] = np.pad(x["L2_ffn_b1"].reshape(-1), (0, pad)).reshape(FT, C).T
    out["W2"] = np.pad(x["L2_ffn_W2"].reshape(E6 * F, C), ((0, pad), (0, 0))).reshape(FT, C, C).transpose(1, 0, 2)
    out["Wk"] = x["L3_attn_Wk"].reshape(C, G8, C)
    out["WqT"] = x["L3_attn_Wq"].reshape(C, G8 * H4, C).transpose(2, 1, 0)
    out["WvT"] = x["L3_attn_Wv"].reshape(C, G8, C).transpose(2, 1, 0)
    out["Wo"] = x["L3_attn_Wo"].reshape(G8, C, C).transpose(1, 0, 2)
    out["bkT"] = x["L3_attn_bk"].reshape(G8, C).T
    out["bvT"] = x["L3_attn_bv"].reshape(G8, C).T
    out["bqT"] = x["L3_attn_bq"].reshape(G8 * H4, C).T
    out["bo"] = x["L3_attn_bo"].reshape(C, 1)
    out["gate_w"] = x["L3_ffn_gate_w"][0]
    out["experts"] = x["L3_ffn_experts"].transpose(1, 0, 2)
    return {k: np.ascontiguousarray(v) for k, v in out.items()}


def kernel(**inputs):
    import concourse.bacc as _bacc
    from concourse.bass_utils import run_bass_kernel_spmd as _run

    nc = _bacc.Bacc("TRN2", target_bir_lowering=False, num_devices=1)
    data = layout(inputs)
    arrays, D = {}, {}
    for name, a in data.items():
        arrays[f"in_{name}_dram"] = a
        D[name] = nc.dram_tensor(f"in_{name}_dram", a.shape, mybir.dt.from_np(a.dtype), kind="ExternalInput").ap()
    D["out"] = nc.dram_tensor("out_0_dram", [B, C, N], F32, kind="ExternalOutput").ap()
    build(nc, D)
    r = _run(nc, [arrays], core_ids=[0])
    return r.results[0]["out_0_dram"].reshape(B, C, HW, HW)
```

```python
from contextlib import ExitStack

import concourse.bass as bass
from concourse import mybir

F32 = mybir.dt.float32
BF16 = mybir.dt.bfloat16
ALU = mybir.AluOpType
ACT = mybir.ActivationFunctionType
AX = mybir.AxisListType

C = 128
B = 16
HW = 32
N = HW * HW
T = B * N
CH = 512
NCH = T // CH
EPS = 1e-5


class Chain:

    def __init__(self, eng, sem, base=0):
        self.eng, self.sem, self.base, self.n = eng, sem, base, 0

    def __call__(self, ins):
        self.n += 1
        ins.then_inc(self.sem, 1)
        self.eng.wait_ge(self.sem, self.base + self.n)


class Mem:

    def __init__(self, nc, tag):
        self.nc, self.tag, self.ctx, self.sems = nc, tag, ExitStack(), []

    def __enter__(self):
        return self

    def __exit__(self, *e):
        if self.sems:
            self.nc.clear_and_free_semaphores(self.sems)
            self.nc.all_engine_barrier()
        return self.ctx.__exit__(*e)

    def sb(self, name, shape, dt=F32):
        return self.ctx.enter_context(self.nc.sbuf_tensor(f"{self.tag}_{name}", shape, dt))

    def ps(self, name, shape, dt=F32):
        return self.ctx.enter_context(self.nc.psum_tensor(f"{self.tag}_{name}", shape, dt))

    def sem(self, name):
        self.sems.append(self.nc.alloc_semaphore(f"{self.tag}_{name}"))
        return self.sems[-1]

    def block(self):
        return self.ctx.enter_context(self.nc.Block())


def col(v):
    return v.rearrange("(p o) -> p o", o=1)


def block_mask(g, out, k):
    cols = out.shape[1]
    view = out.rearrange("p (b k) -> p b k", k=k)
    keep = dict(compare_op=ALU.is_ge, fill=0.0)
    return (lambda: g.affine_select(out=view, in_=view, pattern=[[-k, cols // k], [0, k]],
                                    base=0, channel_multiplier=1, **keep),
            lambda: g.affine_select(out=view, in_=view, pattern=[[k, cols // k], [0, k]],
                                    base=k - 1, channel_multiplier=-1, **keep))


def phase_constants(nc, K):
    with Mem(nc, "const") as m:
        s = m.sem("step")
        with nc.Block() as block:
            @block.gpsimd
            def _(g):
                step = Chain(g, s)
                step(g.memset(K["ident"][:, :], 1.0))
                step(g.memset(K["ones"][:, :], 1.0))
                step(g.memset(K["neghalf"][:, :], -0.5))
                step(g.memset(K["eps"][:, :], EPS))
                step(g.memset(K["negone"][:, :], -1.0))
                step(g.memset(K["mask8"][:, :], 1.0))
                for one in block_mask(g, K["ident"][:, :], 1):
                    step(one())
                for one in block_mask(g, K["mask8"][:, :], 8):
                    step(one())


def rsqrt_eps(g, step, K, out, var, eps):
    n = out.shape[-1]
    step(g.tensor_scalar(out, var, float(eps), None, ALU.add))
    step(g.tensor_tensor(out, out, K["neghalf"][:, 0:n], ALU.pow))


def phase_conv(nc, K, D, X):
    P = HW + 2
    TAPS = 9
    CIN = 8
    NW = CIN * TAPS
    with Mem(nc, "conv") as m:
        Y = m.sb("Y", [C, T])
        stats = K["stats"]
        mv = m.sb("mv", [C, B, 2])
        gmask = m.sb("gmask", [C, C])
        sm = m.sb("small", [C, 20, B])
        cv = m.sb("colv", [C, 16])
        wrow = m.sb("wrow", [C, NW])
        wtmp = m.sb("wtmp", [C, NW])
        wtap = m.sb("wtap", [C, TAPS, C])
        wsig = m.sb("wsig", [C, TAPS, C], BF16)
        par = m.sb("par", [C, 5])
        img = [m.sb(f"img{u}", [C, P, P], BF16) for u in range(2)]
        pg = m.ps("pg", [C, 2, B])
        acc = [m.ps(f"acc{u}", [C, CH]) for u in range(2)]
        x_in = [m.sem(f"x_in{q}") for q in range(4)]
        par_in = m.sem("par_in")
        pool = m.sem("pool")
        vec = m.sem("vec")
        act = m.sem("act")
        pe_s = m.sem("pe")
        coef1_ready = m.sem("coef1_ready")
        mean_ready, dev_ready, v1_ready, v2_ready = (m.sem(x) for x in ("mean_ready", "dev_ready", "v1_ready", "v2_ready"))
        rg_ready, s1_ready, s2_ready, sw_ready = (m.sem(x) for x in ("rg_ready", "s1_ready", "s2_ready", "sw_ready"))
        wvar_ready = m.sem("wvar_ready")
        mask_ready = m.sem("mask_ready")
        img_ready = m.sem("img_ready")
        acc_ready, stat_done, acc_saved = m.sem("acc_ready"), m.sem("stat_done"), m.sem("acc_saved")
        wsig_ready = m.sem("wsig_ready")
        border_ready = m.sem("border_ready")
        coef2_ready = m.sem("coef2_ready")
        lin_ready, sum_ready, negpart_ready = m.sem("lin_ready"), m.sem("sum_ready"), m.sem("negpart_ready")
        res_ready = m.sem("res_ready")
        negpart = [m.sb(f"negpart{u}", [C, N]) for u in range(2)]
        G1, B1v, G2, B2v, PA = (par[:, i:i + 1] for i in range(5))
        MEAN, VAR = mv[:, :, 0], mv[:, :, 1]
        MG, VG, DEV, T0, RG, RDEV, RV, C0, A1, BB1, T2, T1 = (sm[:, i, :] for i in range(12))
        M1, V1, S1, MC, VC, S2, SW, WM, WV, WR, V2, T2C, TC, ONEMA = (cv[:, i:i + 1] for i in range(14))
        csum = m.sb("csum", [C, 2])

        with nc.Block() as block:
            @block.sync
            def _(sp):
                for q in range(4):
                    sp.dma_start(X[:, q * 4 * N:(q + 1) * 4 * N].rearrange("c (b n) -> c b n", n=N),
                                 D["x"][4 * q:4 * q + 4].rearrange("b c n -> c b n")).then_inc(x_in[q], 16)

            @block.gpsimd
            def _(g):
                for i, name in enumerate(("bn1_gamma", "bn1_beta", "bn2_gamma", "bn2_beta", "prelu_a")):
                    g.dma_start(par[:, i:i + 1], col(D["L0_conv_" + name])).then_inc(par_in, 16)
                g.dma_start(wrow[:, :], D["conv_w"]).then_inc(par_in, 16)
                g.dma_start(wtap[:, :, :], D["conv_wt"]).then_inc(par_in, 16)
                step = Chain(g, pool)
                step(g.memset(gmask[:, :], 0.25))
                for one in block_mask(g, gmask[:, :], 4):
                    last = one()
                    step(last)
                g.sem_inc(mask_ready, 1)
                g.memset(img[0][:, :, :], 0.0).then_inc(border_ready, 1)
                g.memset(img[1][:, :, :], 0.0).then_inc(border_ready, 1)
                g.wait_ge(dev_ready, 2)
                rsqrt_eps(g, step, K, RG, VG, EPS)
                g.sem_inc(rg_ready, 1)
                g.wait_ge(v1_ready, 1)
                rsqrt_eps(g, step, K, S1, V1, EPS)
                g.sem_inc(s1_ready, 1)
                g.wait_ge(wvar_ready, 1)
                rsqrt_eps(g, step, K, WR, WV, 0.0)
                g.sem_inc(sw_ready, 1)
                g.wait_ge(v2_ready, 1)
                rsqrt_eps(g, step, K, S2, V2, EPS)
                g.sem_inc(s2_ready, 1)

            @block.tensor
            def _(pe):
                pe.wait_ge(mask_ready, 1)
                pe.wait_ge(mean_ready, 1)
                pe.matmul(pg[:, 0, :], gmask[:, :], T1, start=True, stop=True).then_inc(pe_s, 1)
                pe.wait_ge(dev_ready, 1)
                pe.matmul(pg[:, 1, :], gmask[:, :], T0, start=True, stop=True).then_inc(pe_s, 1)
                pe.wait_ge(wsig_ready, 1)

                with pe.Fori(0, B // 2) as i:
                    for u in range(2):
                        pe.wait_ge(img_ready, 2 * i + u + 1)
                        for h in range(2):
                            pe.wait_ge(acc_saved, 4 * i + 2 * u + h - 1 + 2)
                            for t in range(TAPS):
                                dy, dx = divmod(t, 3)
                                last = pe.matmul(acc[h][:, :], wsig[:, t, :],
                                                 img[u][:, 16 * h + dy:16 * h + dy + 16, dx:dx + HW],
                                                 start=(t == 0), stop=(t == TAPS - 1))
                            last.then_inc(acc_ready, 1)

            @block.vector
            def _(v):
                step = Chain(v, vec)
                for q in range(4):
                    v.wait_ge(x_in[q], 16)
                    for b in range(4 * q, 4 * q + 4):
                        for h in range(2):
                            last = v.bn_stats(stats[:, 2 * b + h, :], X[:, b * N + h * CH:b * N + (h + 1) * CH])
                        step(last)
                        step(v.bn_aggr(mv[:, b, :], stats[:, 2 * b:2 * b + 2, :]))
                step(v.tensor_copy(T1, MEAN))
                v.sem_inc(mean_ready, 1)
                v.wait_ge(pe_s, 1)
                step(v.tensor_copy(MG, pg[:, 0, :]))
                step(v.tensor_sub(DEV, MEAN, MG))
                step(v.tensor_mul(T0, DEV, DEV))
                step(v.tensor_add(T0, T0, VAR))
                v.sem_inc(dev_ready, 1)
                v.wait_ge(pe_s, 2)
                step(v.tensor_copy(VG, pg[:, 1, :]))
                v.sem_inc(dev_ready, 1)
                v.wait_ge(rg_ready, 1)
                v.wait_ge(par_in, 7 * 16)
                step(v.tensor_mul(RDEV, RG, DEV))
                step(v.tensor_mul(C0, RG, MG))
                step(v.tensor_scalar(C0, C0, -1.0, None, ALU.mult))
                step(v.reduce_sum(M1, RDEV, AX.X))
                step(v.tensor_scalar(M1, M1, 1.0 / B, None, ALU.mult))
                step(v.tensor_scalar(RDEV, RDEV, M1, None, ALU.subtract))
                step(v.tensor_mul(RDEV, RDEV, RDEV))
                step(v.tensor_mul(RV, RG, RG))
                step(v.tensor_mul(RV, RV, VAR))
                step(v.tensor_add(RV, RV, RDEV))
                step(v.reduce_sum(V1, RV, AX.X))
                step(v.tensor_scalar(V1, V1, 1.0 / B, None, ALU.mult))
                v.sem_inc(v1_ready, 1)
                v.wait_ge(s1_ready, 1)
                step(v.tensor_mul(S1, S1, G1))
                step(v.tensor_scalar(A1, RG, S1, None, ALU.mult))
                step(v.tensor_scalar(BB1, C0, M1, S1, ALU.subtract, ALU.mult))
                step(v.tensor_scalar(BB1, BB1, B1v, None, ALU.add))
                v.sem_inc(coef1_ready, 1)
                v.wait_ge(act, 1)
                v.tensor_tensor(wsig[:, :, :], wtap[:, :, :],
                                K["mask8"][:, :].rearrange("p (o c) -> p o c", o=1).to_broadcast([C, TAPS, C]),
                                ALU.mult).then_inc(wsig_ready, 1)
                step(v.reduce_sum(WM, wrow[:, :], AX.X))
                step(v.tensor_scalar(WM, WM, 1.0 / NW, None, ALU.mult))
                step(v.tensor_scalar(wrow[:, :], wrow[:, :], WM, None, ALU.subtract))
                step(v.reduce_sum(WM, wrow[:, :], AX.X))
                step(v.tensor_scalar(WM, WM, 1.0 / NW, None, ALU.mult))
                step(v.tensor_scalar(wtmp[:, :], wrow[:, :], WM, None, ALU.subtract))
                step(v.tensor_mul(wtmp[:, :], wtmp[:, :], wtmp[:, :]))
                step(v.reduce_sum(WV, wtmp[:, :], AX.X))
                step(v.tensor_scalar(WV, WV, 1.0 / (NW - 1), None, ALU.mult))
                v.sem_inc(wvar_ready, 1)
                step(v.tensor_reduce(SW, wrow[:, :], AX.X, ALU.add, apply_absolute_value=True))
                step(v.tensor_scalar(SW, SW, 1.0 / NW, None, ALU.mult))
                v.wait_ge(sw_ready, 1)
                step(v.tensor_mul(SW, SW, WR))
                with v.Fori(0, NCH // 2) as i:
                    for h in range(2):
                        v.wait_ge(acc_saved, 2 * i + h + 1 + 2)
                        v.bn_stats(stats[:, bass.ds(2 * i + h, 1), :],
                                   Y[:, bass.ds((2 * i + h) * CH, CH)]).then_inc(stat_done, 1)
                v.wait_ge(stat_done, NCH)
                step(v.bn_aggr(csum[:, :], stats[:, :, :]))
                step(v.tensor_mul(V2, csum[:, 1:2], SW))
                step(v.tensor_mul(V2, V2, SW))
                v.sem_inc(v2_ready, 1)
                v.wait_ge(s2_ready, 1)
                step(v.tensor_mul(S2, S2, SW))
                step(v.tensor_mul(S2, S2, G2))
                step(v.tensor_mul(TC, csum[:, 0:1], S2))
                step(v.tensor_sub(T2C, B2v, TC))
                step(v.tensor_scalar(ONEMA, PA, -1.0, 1.0, ALU.mult, ALU.add))
                step(v.tensor_scalar(T2, C0, T2C, None, ALU.add))
                v.sem_inc(coef2_ready, 1)
                with v.Fori(0, B // 2) as i:
                    for u in range(2):
                        b = 2 * i + u
                        xb, yb = X[:, bass.ds(b * N, N)], Y[:, bass.ds(b * N, N)]
                        v.wait_ge(lin_ready, b + 1)
                        v.scalar_tensor_tensor(yb, xb, sm[:, 4, bass.ds(b, 1)], yb, ALU.mult, ALU.add)\
                         .then_inc(sum_ready, 1)
                        v.wait_ge(sum_ready, 2 * b + 1)
                        v.tensor_add(xb, xb, yb).then_inc(sum_ready, 1)
                        v.wait_ge(sum_ready, 2 * b + 2)
                        v.wait_ge(negpart_ready, b + 1)
                        v.scalar_tensor_tensor(xb, negpart[u][:, :], ONEMA, xb, ALU.mult, ALU.add)\
                         .then_inc(res_ready, 1)

            @block.scalar
            def _(a):
                a.wait_ge(par_in, 7 * 16)
                a.activation(wtap[:, :, :], wtap[:, :, :], ACT.Sign).then_inc(act, 1)
                a.wait_ge(coef1_ready, 1)
                a.wait_ge(border_ready, 2)
                a.sem_inc(acc_saved, 2)

                def signs(b, u):
                    a.activation(img[u][:, 1:HW + 1, 1:HW + 1],
                                 X[:, bass.ds(b * N, N)].rearrange("c (y x) -> c y x", x=HW), ACT.Sign,
                                 bias=sm[:, 9, bass.ds(b, 1)], scale=sm[:, 8, bass.ds(b, 1)]).then_inc(img_ready, 1)

                def save(b, h):
                    a.wait_ge(acc_ready, 2 * b + h + 1)
                    a.copy(Y[:, bass.ds(b * N + h * CH, CH)], acc[h][:, :]).then_inc(acc_saved, 1)

                signs(0, 0)
                signs(1, 1)
                with a.Fori(0, B // 2 - 1) as i:
                    for u in range(2):
                        save(2 * i + u, 0)
                        save(2 * i + u, 1)
                        signs(2 * i + u + 2, u)
                for b in (B - 2, B - 1):
                    save(b, 0)
                    save(b, 1)
                a.wait_ge(coef2_ready, 1)

                def affine(b):
                    yb = Y[:, bass.ds(b * N, N)]
                    a.activation(yb, yb, ACT.Identity, bias=sm[:, 10, bass.ds(b, 1)], scale=S2).then_inc(lin_ready, 1)

                def negative_part(b, u):
                    a.wait_ge(sum_ready, 2 * b + 1)
                    a.activation(negpart[u][:, :], Y[:, bass.ds(b * N, N)], ACT.Relu, scale=-1.0)\
                     .then_inc(negpart_ready, 1)

                affine(0)
                affine(1)
                for b in (0, 1):
                    negative_part(b, b)
                    affine(b + 2)
                with a.Fori(1, B // 2 - 1) as i:
                    for u in range(2):
                        a.wait_ge(res_ready, 2 * i + u - 1)
                        negative_part(2 * i + u, u)
                        affine(2 * i + u + 2)
                for b in (B - 2, B - 1):
                    a.wait_ge(res_ready, b - 1)
                    negative_part(b, b % 2)



HD = 8
PARTS = 3
SIDE = 36
PATTERN = ((0, 0), (0, 1), (0, 3), (1, 3))
PLACES = ((0, 1), (0, 0), (1, -1), (1, 1), (2, 0), (3, -1), (3, 1), (4, 0))
NG = len(PLACES)
SHIFTS = tuple(SIDE * y + x for y, x in PATTERN)
MARGIN = 1
REP = SIDE * SIDE + 2
PAD = MARGIN + REP + max(SHIFTS) + 2
EPS_ATT = 1e-15


def tap_weights(w_dw):
    import numpy as np
    w = w_dw.reshape(16, PARTS, HD, 5, 5).transpose(1, 0, 2, 3, 4).reshape(PARTS, 4, 32, 5, 5)
    w = w[1:]
    out = np.zeros((4, 32, 2, 4, NG), w.dtype)
    seen = set()
    for g, (gy, gx) in enumerate(PLACES):
        for t, (py, px) in enumerate(PATTERN):
            y, x = gy + py, gx + px
            if 0 <= y < 5 and 0 <= x < 5 and (y, x) not in seen:
                seen.add((y, x))
                out[t, :, :, :, g] = w[:, :, :, y, x].transpose(2, 0, 1)
    assert len(seen) == 25
    return out.reshape(C, 2, 4, NG)


def wait_if(eng, sem, value):
    if not isinstance(value, int) or value > 0:
        eng.wait_ge(sem, value)


def over_batches(eng, batch):
    batch(0, 0, 0)
    batch(1, 1, 0)
    with eng.Fori(1, B // 2 - 1) as i:
        for u in range(2):
            batch(2 * i + u, u, 0)
    batch(B - 2, 0, 0)
    batch(B - 1, 1, 1)


SLOT = {0: [("tp", "agg", 0)], 1: [("tp", "agg", 1)], 2: [("tp", "agg", 2)], 3: [("tp", "agg", 3)],
        5: [("vk", "agg")], 7: [("den",), ("nb", 0)],
        8: [("tp", "base", 0)], 9: [("tp", "base", 1)], 12: [("tp", "base", 2)], 13: [("tp", "base", 3)],
        14: [("rb", 0)], 17: [("nb", 1), ("rb", 1)], 19: [("nb", 2)], 20: [("y", 0), ("rb", 2)],
        23: [("nb", 3), ("rb", 3)], 24: [("tp", "base", 4)], 25: [("tp", "base", 5)], 26: [("y", 1)],
        28: [("vk", "base")]}
BASE_STEPS = [s for g in sorted(SLOT) for s in SLOT[g] if "base" in s]
OUTPUTS = [s for g in sorted(SLOT) for s in SLOT[g] if "base" not in s]
TAPS = 25
EARLY = 4
BUSY = (1, 3, 7, 8, 9, 13, 17, 23, 28, 30, 31)
TAP_AFTER = [g for g in range(4 * NG) if g not in BUSY]
assert EARLY + len(TAP_AFTER) == TAPS


def slot_work(first, last):
    for g in range(4 * NG):
        yield g, [s for s in SLOT.get(g, ()) if not (last if "base" in s else first)]


def phase_linatt(nc, K, D, X):
    with Mem(nc, "la") as m:
        wqkv = m.sb("wqkv", [C, PARTS, C])
        wproj = m.sb("wproj", [C, 2, C])
        pwt = m.sb("pwt", [C, PARTS, 4, 32])
        dwt = m.sb("dwt", [C, 2, 4, NG])
        taps = m.sb("taps", [C, TAPS])
        wpq = m.sb("wpq", [C, C])
        dwq = m.sb("dwq", [C, N])
        mask32 = m.sb("mask32", [C, 32])
        wagg = m.sb("wagg", [C, 2, 4, NG, 32])
        densel = m.sb("densel", [C, 2, 32])
        spread = m.sb("spread", [64, 2, C])
        pad = [m.sb(f"pad{u}", [C, PARTS, PAD]) for u in range(2)]
        rep = m.sb("rep", [C, 2, 4, REP])
        agg = m.sb("agg", [C, 2, N])
        q_base = [m.sb(f"qb{u}", [C, N]) for u in range(2)]
        q_agg = m.sb("qa", [C, N])
        kT = m.sb("kT", [C, 9, C])
        vT = m.sb("vT", [C, 9, C + 2])
        num_w = [m.sb(f"nw{u}", [C, C]) for u in range(3)]
        den_w = [m.sb(f"dw{u}", [C, 32]) for u in range(3)]
        rec = m.sb("rec", [64, CH])
        recs = [m.sb(f"recs{u}", [C, CH]) for u in range(2)]
        o = [m.sb(f"o{u}", [C, CH]) for u in range(2)]
        y = [m.sb(f"y{u}", [C, CH]) for u in range(2)]
        stats = K["stats"]
        acc = [m.ps(f"acc{u}", [C, CH]) for u in range(2)]
        tp = [m.ps(f"tp{u}", [C, 4, C]) for u in range(2)]
        vkp = m.ps("vkp", [C, CH])
        nb = m.ps("nb", [C, CH])
        rb = m.ps("rb", [C, CH])
        dp = m.ps("dp", [C, CH])
        w_in = m.sem("w_in")
        pool, vec = m.sem("pool"), m.sem("vec")
        const_ready, pad_zero, wagg_ready = m.sem("const_ready"), m.sem("pad_zero"), m.sem("wagg_ready")
        acc_ready, acc_saved = m.sem("acc_ready"), m.sem("acc_saved")
        rep_in = {p: m.sem(f"rep_in{p}") for p in (1, 2)}
        tap_done = m.sem("tap_done")
        tp_ready, tp_saved = m.sem("tp_ready"), m.sem("tp_saved")
        vk_ready, vk_saved = m.sem("vk_ready"), m.sem("vk_saved")
        q_ready = m.sem("q_ready")
        den_ready, den_read, rec_ready = m.sem("den_ready"), m.sem("den_read"), m.sem("rec_ready")
        nb_ready, rb_ready, recs_ready, o_ready = (m.sem(x) for x in ("nb_ready", "rb_ready", "recs_ready", "o_ready"))
        y_mm, y_saved, y_stat = m.sem("y_mm"), m.sem("y_saved"), m.sem("y_stat")
        y_out = [m.sem("y_out0"), m.sem("y_out1")]

        def window(u, p, dy, dx, rows=HW):
            at = MARGIN + dy * SIDE + dx
            return pad[u][:, p, at:at + rows * SIDE].rearrange("c (y x) -> c y x", x=SIDE)[:, :, 0:HW]

        def interior(u, p, row, rows):
            return window(u, p, 2 + row, 2, rows)

        def fills(tiles):
            return [(p, lo, min(lo + 4, tiles)) for p in (1, 2) for lo in range(0, tiles, 4)]

        ROW0 = MARGIN + 2 * SIDE

        def acc_project(b):
            return 12 * b - 6 if not isinstance(b, int) or b else 0

        def acc_aggregate(b, last):
            return 12 * b + (6 if last else 12)

        def tp_base(b):
            return 10 * b - 4 if not isinstance(b, int) or b else 0

        def tp_aggregate(b, last):
            return 10 * b + (6 if last else 12)

        def vk_base(b):
            return 2 * b - 1 if not isinstance(b, int) or b else 0

        def vk_aggregate(b, last):
            return 2 * b + (1 if last else 2)

        with nc.Block() as block:
            @block.sync
            def _(sp):
                sp.dma_start(wqkv[:, :, :], D["w_qkvT"]).then_inc(w_in, 16)
                sp.dma_start(wproj[:, :, :], D["w_projT"]).then_inc(w_in, 16)
                sp.dma_start(pwt[:, :, :, :], D["w_pwT"]).then_inc(w_in, 16)
                sp.dma_start(dwt[:, :, :, :], D["w_taps"]).then_inc(w_in, 16)
                sp.dma_start(taps[:, :], D["w_qtaps"]).then_inc(w_in, 16)

                def replicate(b, u):
                    for p in (1, 2):
                        sp.wait_ge(acc_saved, 12 * b + 2 * p if not isinstance(b, int) or b else 2 * p + 2)
                        for j in range(4):
                            for t in range(4):
                                sp.dma_start(rep[32 * t:32 * t + 32, p - 1, j, :],
                                             pad[u][32 * j:32 * j + 32, p, SHIFTS[t]:SHIFTS[t] + REP]).then_inc(rep_in[p], 16)

                over_batches(sp, lambda b, u, last: replicate(b, u))

            @block.gpsimd
            def _(g):
                step = Chain(g, pool)
                g.memset(pad[0][:, :, :], 0.0).then_inc(pad_zero, 1)
                g.memset(pad[1][:, :, :], 0.0).then_inc(pad_zero, 1)
                step(g.memset(vT[:, :, :], 1.0))
                step(g.memset(spread[:, :, :], 1.0))
                for q in range(2):
                    for s in range(2):
                        v = spread[32 * q:32 * q + 32, s, :].rearrange("p (b k) -> p b k", k=HD)
                        for sign in (1, -1):
                            step(g.affine_select(out=v, in_=v, pattern=[[-sign, 16], [0, HD]], base=-16 * s * sign,
                                                 channel_multiplier=sign, compare_op=ALU.is_ge, fill=0.0))
                g.sem_inc(const_ready, 1)
                with g.Fori(0, B) as b:
                    for h in range(2):
                        g.wait_ge(y_saved, 2 * b + h + 1)
                        g.dma_start(D["proj"][:, bass.ds(b * N + h * CH, CH)], y[h][:, :]).then_inc(y_out[h], 16)
                g.wait_ge(y_out[0], 16 * B)
                g.wait_ge(y_out[1], 16 * B)

            @block.tensor
            def _(pe):
                pe.wait_ge(w_in, 80)
                pe.wait_ge(wagg_ready, 1)
                pe.wait_ge(const_ready, 1)

                def project(b):
                    n = acc_project(b)
                    for c in range(6):
                        p, h = divmod(c, 2)
                        wait_if(pe, acc_saved, n + c - 1)
                        pe.matmul(acc[h][:, :], wqkv[:, p, :], X[:, bass.ds(b * N + h * CH, CH)],
                                  start=True, stop=True).then_inc(acc_ready, 1)

                def group(b, n, i):
                    c, g = divmod(i, NG)
                    p, h = c // 2 + 1, c % 2
                    if g == 0:
                        pe.wait_ge(rep_in[p], 256 * b + 256)
                        wait_if(pe, acc_saved, n + c - 1)
                    gy, gx = PLACES[g]
                    at = MARGIN + (gy + 16 * h) * SIDE + gx
                    for j in range(4):
                        view = rep[:, p - 1, j, at:at + 16 * SIDE].rearrange("c (y x) -> c y x", x=SIDE)
                        last = pe.matmul(acc[h][32 * j:32 * j + 32, :], wagg[:, p - 1, j, g, :],
                                         view[:, :, 0:HW], start=(g == 0), stop=(g == NG - 1))
                    if g == NG - 1:
                        last.then_inc(acc_ready, 1)

                def queries(b, n):
                    pe.wait_ge(tap_done, TAPS * b + TAPS)
                    for h in range(2):
                        wait_if(pe, acc_saved, n + 4 + h - 1)
                        pe.matmul(acc[h][:, :], wpq[:, :], dwq[:, h * CH:(h + 1) * CH], start=True, stop=True)\
                          .then_inc(acc_ready, 1)

                def work(step, b, u, last):
                    kind = step[0]
                    base = "base" in step
                    if kind == "tp":
                        c = step[2]
                        p, lo, hi = fills(9 if base else 8)[c]
                        n = tp_base(b) if base else tp_aggregate(b, last)
                        if c == 0:
                            pe.wait_ge(acc_saved, (acc_project(b) if base else acc_aggregate(b, last)) + 6)
                        wait_if(pe, tp_saved, n + c - 1)
                        for r in range(lo, hi):
                            source = pad[u][:, p, ROW0 + r * C:ROW0 + (r + 1) * C] if base else agg[:, p - 1, r * C:(r + 1) * C]
                            done = pe.transpose(tp[c % 2][:, r - lo, :], source, K["ident"][:, :])
                        done.then_inc(tp_ready, 1)
                    elif kind == "vk":
                        tiles = 9 if base else 8
                        n, k = (tp_base(b), vk_base(b)) if base else (tp_aggregate(b, last), vk_aggregate(b, last))
                        pe.wait_ge(tp_saved, n + len(fills(tiles)))
                        wait_if(pe, vk_saved, k)
                        for r in range(tiles):
                            done = pe.matmul(vkp[:, 0:C + 1], kT[:, r, :], vT[:, r, 0:C + 1],
                                             start=(r == 0), stop=(r == tiles - 1))
                        done.then_inc(vk_ready, 1)
                    elif kind == "den":
                        pe.wait_ge(vk_saved, vk_aggregate(b, last) + 1)
                        wait_if(pe, y_saved, 2 * b)
                        pe.wait_ge(q_ready, b + 1)
                        for h in range(2):
                            cols = slice(h * CH, (h + 1) * CH)
                            pe.matmul(dp[32 * h:32 * h + 32, :], den_w[u][:, :], q_base[u][:, cols], start=True, stop=False)
                            done = pe.matmul(dp[32 * h:32 * h + 32, :], den_w[2][:, :], q_agg[:, cols], start=False, stop=True)
                        done.then_inc(den_ready, 1)
                    elif kind == "nb":
                        h, s = divmod(step[1], 2)
                        wait_if(pe, o_ready, 4 * b + 2 * h + s)
                        pe.matmul(nb[:, :], num_w[u if s == 0 else 2][:, :],
                                  (q_base[u] if s == 0 else q_agg)[:, h * CH:(h + 1) * CH],
                                  start=True, stop=True).then_inc(nb_ready, 1)
                    elif kind == "rb":
                        h, s = divmod(step[1], 2)
                        pe.wait_ge(rec_ready, b + 1)
                        wait_if(pe, recs_ready, 4 * b + 2 * h + s)
                        pe.matmul(rb[:, :], spread[32 * h:32 * h + 32, s, :], rec[32 * h:32 * h + 32, :],
                                  start=True, stop=True).then_inc(rb_ready, 1)
                    else:
                        h = step[1]
                        pe.wait_ge(o_ready, 4 * b + 2 * h + 2)
                        if h == 1:
                            pe.wait_ge(y_saved, 2 * b + 1)
                        pe.matmul(dp[:, :], wproj[:, 0, :], o[0][:, :], start=True, stop=False)
                        pe.matmul(dp[:, :], wproj[:, 1, :], o[1][:, :], start=False, stop=True).then_inc(y_mm, 1)

                project(0)
                for step in BASE_STEPS:
                    work(step, 0, 0, False)

                def batch(b, u, last):
                    if not last:
                        project(b + 1)
                    n = acc_aggregate(b, last)
                    for i, steps in slot_work(isinstance(b, int) and b == 0, last):
                        group(b, n, i)
                        for step in steps:
                            work(step, b + 1 if "base" in step else b - 1, 1 - u, False)
                    queries(b, n)

                over_batches(pe, batch)
                for step in OUTPUTS:
                    work(step, B - 1, 1, True)

            @block.vector
            def _(v):
                step = Chain(v, vec)
                v.wait_ge(w_in, 80)
                step(v.reduce_sum(mask32[:, :], K["mask8"][:, :].rearrange("p (t c) -> p c t", t=4), AX.X))
                step(v.tensor_tensor(wpq[:, :], pwt[:, 0, :, :].rearrange("p j c -> p (j c)"), K["mask8"][:, :], ALU.mult))
                step(v.tensor_tensor(pwt[:, :, :, :].rearrange("p a j c -> p (a j) c"),
                                     pwt[:, :, :, :].rearrange("p a j c -> p (a j) c"),
                                     mask32[:, :].rearrange("p (o c) -> p o c", o=1).to_broadcast([C, PARTS * 4, 32]), ALU.mult))
                for p in range(2):
                    step(v.tensor_tensor(wagg[:, p, :, :, :],
                                         pwt[:, p + 1, :, :].rearrange("p j (o c) -> p j o c", o=1).to_broadcast([C, 4, NG, 32]),
                                         dwt[:, p, :, :].rearrange("p j (g o) -> p j g o", o=1).to_broadcast([C, 4, NG, 32]),
                                         ALU.mult))
                v.sem_inc(wagg_ready, 1)
                step(v.memset(densel[:, :, :], 0.0))
                for s in range(2):
                    step(v.tensor_copy(densel[:, s, 16 * s:16 * s + 16], K["mask8"][:, 0:C:HD]))
                v.wait_ge(const_ready, 1)

                def work(step, b, u, last):
                    kind = step[0]
                    base = "base" in step
                    if kind == "tp":
                        c = step[2]
                        p, lo, hi = fills(9 if base else 8)[c]
                        n = tp_base(b) if base else tp_aggregate(b, last)
                        v.wait_ge(tp_ready, n + c + 1)
                        if p == 1:
                            v.tensor_scalar(kT[:, lo:hi, :], tp[c % 2][:, 0:hi - lo, :], 0.0, None, ALU.max)\
                             .then_inc(tp_saved, 1)
                        else:
                            v.tensor_copy(vT[:, lo:hi, 0:C], tp[c % 2][:, 0:hi - lo, :]).then_inc(tp_saved, 1)
                    elif kind == "vk":
                        w, s = (u, 0) if base else (2, 1)
                        v.wait_ge(vk_ready, (vk_base(b) if base else vk_aggregate(b, last)) + 1)
                        if base:
                            v.tensor_scalar(q_base[u][:, :].rearrange("c (y x) -> c y x", x=HW), interior(u, 0, 0, HW),
                                            0.0, None, ALU.max).then_inc(q_ready, 1)
                        v.tensor_tensor(num_w[w][:, :], vkp[:, 0:C], K["mask8"][:, :], ALU.mult)
                        v.tensor_scalar(den_w[w][:, :], densel[:, s, :], vkp[:, C:C + 1], None, ALU.mult).then_inc(vk_saved, 1)
                    elif kind == "den":
                        v.wait_ge(den_ready, b + 1)
                        v.tensor_scalar(rec[:, :], dp[0:64, :], EPS_ATT, None, ALU.add).then_inc(den_read, 1)
                        v.wait_ge(den_read, b + 1)
                        v.reciprocal(rec[:, :], rec[:, :]).then_inc(rec_ready, 1)
                    elif kind == "rb":
                        h, s = divmod(step[1], 2)
                        k = 4 * b + 2 * h + s
                        v.wait_ge(nb_ready, k + 1)
                        v.wait_ge(recs_ready, k + 1)
                        wait_if(v, y_mm, 2 * b + h)
                        v.tensor_tensor(o[s][:, :], nb[:, :], recs[s][:, :], ALU.mult).then_inc(o_ready, 1)

                def tap(b, u, t):
                    image = window(u, 0, *divmod(t, 5))
                    out = dwq[:, :].rearrange("c (y x) -> c y x", x=HW)
                    if t == 0:
                        wait_if(v, acc_ready, 12 * b + 6)
                        v.tensor_scalar(out, image, taps[:, 0:1], None, ALU.mult).then_inc(tap_done, 1)
                    else:
                        v.wait_ge(tap_done, TAPS * b + t)
                        v.scalar_tensor_tensor(out, image, taps[:, t:t + 1], out, ALU.mult, ALU.add).then_inc(tap_done, 1)

                def statistics(b):
                    for h in range(2):
                        v.wait_ge(y_saved, 2 * b + h + 1)
                        v.bn_stats(stats[:, bass.ds(2 * b + h, 1), :], y[h][:, :]).then_inc(y_stat, 1)

                for step in BASE_STEPS:
                    work(step, 0, 0, False)

                def batch(b, u, last):
                    first = isinstance(b, int) and b == 0
                    for t in range(EARLY):
                        tap(b, u, t)
                    for i, steps in slot_work(first, last):
                        if i in TAP_AFTER:
                            tap(b, u, EARLY + TAP_AFTER.index(i))
                        for step in steps:
                            work(step, b + 1 if "base" in step else b - 1, 1 - u, False)
                    if not first:
                        statistics(b - 1)

                over_batches(v, batch)
                for step in OUTPUTS:
                    work(step, B - 1, 1, True)
                statistics(B - 1)

            @block.scalar
            def _(a):
                a.wait_ge(pad_zero, 2)

                def project(b, u):
                    n = acc_project(b)
                    for c in range(6):
                        p, h = divmod(c, 2)
                        if h == 0 and (not isinstance(b, int) or b >= 2):
                            if p == 0:
                                a.wait_ge(tap_done, TAPS * (b - 1))
                            else:
                                a.wait_ge(rep_in[p], 256 * (b - 1))
                                a.wait_ge(tp_ready, tp_base(b - 2) + 3 * p)
                        a.wait_ge(acc_ready, n + c + 1)
                        a.copy(interior(u, p, 16 * h, 16), acc[h][:, :].rearrange("c (y x) -> c y x", x=HW)).then_inc(acc_saved, 1)

                def chunk(b, c, last):
                    a.wait_ge(acc_ready, acc_aggregate(b, last) + c + 1)
                    part, h = c // 2, c % 2
                    cols = slice(h * CH, (h + 1) * CH)
                    if part == 2:
                        a.activation(q_agg[:, cols], acc[h][:, :], ACT.Relu).then_inc(acc_saved, 1)
                    else:
                        if h == 0:
                            wait_if(a, tp_ready, tp_aggregate(b - 1, False) + 2 * part + 2 if not isinstance(b, int) or b else 0)
                        a.copy(agg[:, part, cols], acc[h][:, :]).then_inc(acc_saved, 1)

                def work(step, b):
                    if step[0] == "rb":
                        h, s = divmod(step[1], 2)
                        k = 4 * b + 2 * h + s
                        a.wait_ge(rb_ready, k + 1)
                        wait_if(a, o_ready, k - 1)
                        a.copy(recs[s][:, :], rb[:, :]).then_inc(recs_ready, 1)
                    elif step[0] == "y":
                        h = step[1]
                        a.wait_ge(y_mm, 2 * b + h + 1)
                        wait_if(a, y_stat, 2 * b + h - 1)
                        wait_if(a, y_out[h], 16 * b)
                        a.copy(y[h][:, :], dp[:, :]).then_inc(y_saved, 1)

                project(0, 0)

                def batch(b, u, last):
                    if not last:
                        project(b + 1, 1 - u)
                    for i, steps in slot_work(isinstance(b, int) and b == 0, last):
                        if i % NG == NG - 1:
                            chunk(b, i // NG, last)
                        for step in steps:
                            work(step, b - 1)
                    for c in (4, 5):
                        chunk(b, c, last)

                over_batches(a, batch)
                for step in OUTPUTS:
                    work(step, B - 1)


def phase_linatt_norm(nc, K, D, X):
    with Mem(nc, "lan") as m:
        y = [m.sb(f"y{u}", [C, 2 * N]) for u in range(2)]
        par = m.sb("par", [C, 2])
        mv = m.sb("mv", [C, 2])
        cv = m.sb("cv", [C, 4])
        S, T0, V = (cv[:, i:i + 1] for i in range(3))
        par_in, var_ready, s_ready, coef_ready = (m.sem(x) for x in ("par_in", "var_ready", "s_ready", "coef_ready"))
        y_in = [m.sem("y_in0"), m.sem("y_in1")]
        lin_ready, sum_ready = m.sem("lin_ready"), m.sem("sum_ready")
        pool, vec = m.sem("pool"), m.sem("vec")
        W = 2 * N
        NT = T // W
        with nc.Block() as block:
            @block.sync
            def _(sp):
                def load(k, u):
                    sp.dma_start(y[u][:, :], D["proj"][:, bass.ds(k * W, W)]).then_inc(y_in[u], 16)

                load(0, 0)
                load(1, 1)
                with sp.Fori(1, NT // 2) as i:
                    for u in range(2):
                        sp.wait_ge(sum_ready, 2 * i + u - 1)
                        load(2 * i + u, u)

            @block.gpsimd
            def _(g):
                for i, name in enumerate(("bn_gamma", "bn_beta")):
                    g.dma_start(par[:, i:i + 1], col(D["L1_conv_" + name])).then_inc(par_in, 16)
                g.wait_ge(var_ready, 1)
                step = Chain(g, pool)
                rsqrt_eps(g, step, K, S, mv[:, 1:2], EPS)
                g.sem_inc(s_ready, 1)

            @block.vector
            def _(v):
                step = Chain(v, vec)
                step(v.bn_aggr(mv[:, :], K["stats"][:, :, :]))
                v.sem_inc(var_ready, 1)
                v.wait_ge(s_ready, 1)
                v.wait_ge(par_in, 32)
                step(v.tensor_mul(S, S, par[:, 0:1]))
                step(v.tensor_mul(T0, S, mv[:, 0:1]))
                step(v.tensor_sub(T0, par[:, 1:2], T0))
                v.sem_inc(coef_ready, 1)
                with v.Fori(0, NT // 2) as i:
                    for u in range(2):
                        v.wait_ge(lin_ready, 2 * i + u + 1)
                        xb = X[:, bass.ds((2 * i + u) * W, W)]
                        v.tensor_add(xb, xb, y[u][:, :]).then_inc(sum_ready, 1)

            @block.scalar
            def _(a):
                a.wait_ge(coef_ready, 1)
                with a.Fori(0, NT // 2) as i:
                    for u in range(2):
                        a.wait_ge(y_in[u], 16 * i + 16)
                        a.activation(y[u][:, :], y[u][:, :], ACT.Identity, bias=T0, scale=S).then_inc(lin_ready, 1)



def over(eng, total, step, r=2, peel=1):
    for n in range(r * peel):
        step(n, n % r, False)
    with eng.Fori(peel, total // r - 1) as i:
        for u in range(r):
            step(r * i + u, u, False)
    for n in range(total - r, total):
        step(n, n % r, n == total - 1)


def ahead(n, r=2):
    return not isinstance(n, int) or n + r < NCH


class LayerNorm:

    def __init__(self, m, K, X, r=2):
        self.K, self.X, self.r = K, X, r
        self.xs = [m.sb(f"ln_xs{u}", [C, CH]) for u in range(r)]
        self.xt = [m.sb(f"ln_xt{u}", [C, 4, C]) for u in range(r)]
        self.st = [m.sb(f"ln_st{u}", [C, 4, 6]) for u in range(r)]
        self.mv = [m.sb(f"ln_mv{u}", [C, 4, 2]) for u in range(r)]
        self.ab = [m.sb(f"ln_ab{u}", [C, 2, 4]) for u in range(r)]
        self.front = [m.ps(f"ln_front{u}", [C, 4, C]) for u in range(r)]
        self.back = m.ps("ln_back", [C, CH])
        self.staged = [m.sem(f"ln_staged{u}") for u in range(r)]
        self.front_ready, self.stat, self.mv_ready, self.gp, self.ab_ready, self.xt_ready, self.back_ready, self.saved = (
            m.sem("ln_" + x) for x in ("front_ready", "stat", "mv_ready", "gp", "ab_ready", "xt_ready", "back_ready", "saved"))

    def sync(self, sp, n, u):
        wait_if(sp, self.front_ready, n - self.r + 1)
        sp.dma_start(self.xs[u][:, :], self.X[:, bass.ds(n * CH, CH)]).then_inc(self.staged[u], 16)

    def tensor_front(self, pe, n, u):
        pe.wait_ge(self.staged[u], (16 // self.r) * (n - u) + 16)
        wait_if(pe, self.xt_ready, n - self.r + 1)
        for r in range(4):
            last = pe.transpose(self.front[u][:, r, :], self.xs[u][:, r * C:(r + 1) * C], self.K["ident"][:, :])
        last.then_inc(self.front_ready, 1)

    def tensor_back(self, pe, n, u):
        pe.wait_ge(self.xt_ready, n + 1)
        wait_if(pe, self.saved, n)
        for r in range(4):
            last = pe.transpose(self.back[:, r * C:(r + 1) * C], self.xt[u][:, r, :], self.K["ident"][:, :])
        last.then_inc(self.back_ready, 1)

    def vector_stats(self, v, n, u):
        v.wait_ge(self.front_ready, n + 1)
        for r in range(4):
            last = v.bn_stats(self.st[u][:, r, :], self.front[u][:, r, :])
        last.then_inc(self.stat, 1)
        v.wait_ge(self.stat, 1)
        v.wait_ge(self.stat, n + 1)
        wait_if(v, self.ab_ready, n - self.r + 1)
        for r in range(4):
            last = v.bn_aggr(self.mv[u][:, r, :], self.st[u][:, r, :])
        last.then_inc(self.mv_ready, 1)

    def gpsimd(self, g, n, u):
        g.wait_ge(self.mv_ready, n + 1)
        wait_if(g, self.xt_ready, n - self.r + 1)
        rstd, shift = self.ab[u][:, 0, :], self.ab[u][:, 1, :]
        g.tensor_tensor(rstd, self.mv[u][:, :, 1], self.K["eps"][:, :], ALU.add).then_inc(self.gp, 1)
        g.wait_ge(self.gp, 3 * n + 1)
        g.tensor_tensor(rstd, rstd, self.K["neghalf"][:, 0:4], ALU.pow).then_inc(self.gp, 1)
        g.wait_ge(self.gp, 3 * n + 2)
        g.tensor_tensor(shift, self.mv[u][:, :, 0], rstd, ALU.mult).then_inc(self.gp, 1)
        g.wait_ge(self.gp, 3 * n + 3)
        g.tensor_tensor(shift, shift, self.K["negone"][:, :], ALU.mult).then_inc(self.ab_ready, 1)

    def scalar(self, a, n, u, used=None):
        a.wait_ge(self.ab_ready, n + 1)
        wait_if(a, self.back_ready, n - self.r + 1)
        if used is not None:
            used(n, u)
        for r in range(4):
            last = a.activation(self.xt[u][:, r, :], self.front[u][:, r, :], ACT.Identity,
                                bias=self.ab[u][:, 1, r:r + 1], scale=self.ab[u][:, 0, r:r + 1])
        last.then_inc(self.xt_ready, 1)

    def vector_save(self, v, n, out):
        v.wait_ge(self.back_ready, n + 1)
        v.tensor_copy(out, self.back[:, :]).then_inc(self.saved, 1)



SH = 8
DH = 16
RH = 2
Q_TERMS = (0, 0, 1, 0, 2, 1)
K_TERMS = (0, 1, 0, 2, 0, 1)
KQ = DH * len(Q_TERMS)
KM = KQ + 3
SCALE = DH ** -0.5


def phase_attn_prep(nc, K, D, X):
    RVW = RH * DH
    R = 4
    with Mem(nc, "ap") as m:
        ln = LayerNorm(m, K, X)
        wq, wk = m.sb("wq", [C, C]), m.sb("wk", [C, C])
        wqr, wkr = m.sb("wqr", [C, C]), m.sb("wkr", [C, C])
        mask16 = m.sb("mask16", [C, C])
        wuv = m.sb("wuv", [C, C + RVW])
        xc = [m.sb(f"xc{u}", [C, CH]) for u in range(2)]
        part = [m.sb(f"part{w}", [C, 2, 3, CH], BF16) for w in range(R)]
        left = [[m.sb(f"left{w}{z}", [C, CH]) for z in range(2)] for w in range(R)]
        us = [m.sb(f"us{w}", [C, 4, C]) for w in range(R)]
        pz = [m.ps(f"pz{z}", [C, CH]) for z in range(2)]
        puv = [m.ps(f"puv{h}", [C, 2, C + RVW]) for h in range(2)]
        pw = m.ps("pw", [C, C])
        w_in, pool, m_ready, w_ready, wu_mm = (m.sem(x) for x in ("w_in", "pool", "m_ready", "w_ready", "wu_mm"))
        vec = m.sem("vec")
        z_ready, uv_ready, high, left1, mid, low = (m.sem(x) for x in ("z_ready", "uv_ready", "high", "left1", "mid", "low"))
        uv_saved = m.sem("uv_saved")
        z_out = [m.sem(f"z_out{w}") for w in range(R)]
        u_out = [m.sem(f"u_out{w}") for w in range(R)]
        RV = K["rv"]

        with nc.Block() as block:
            @block.sync
            def _(sp):
                for dst, src in ((wq, "wq_s"), (wk, "wk_s"), (wqr, "wq_rT"), (wkr, "wk_retT")):
                    sp.dma_start(dst[:, :], D[src]).then_inc(w_in, 16)
                sp.dma_start(wuv[:, C:C + RVW], D["wv_r"]).then_inc(w_in, 16)

                def store(k, w, last):
                    sp.wait_ge(low, 2 * k + 2)
                    sp.dma_start(D["qk"][:, :, :, bass.ds(k * CH, CH)].rearrange("z t c n -> c (z t) n"),
                                 part[w][:, :, :, :].rearrange("c z t n -> c (z t) n")).then_inc(z_out[w], 16)
                    sp.wait_ge(uv_saved, 2 * k + 2)
                    sp.dma_start(D["u"][:, bass.ds(4 * k, 4), :], us[w][:, :, :]).then_inc(u_out[w], 16)

                over(sp, NCH, store, R)
                for w in range(R):
                    sp.wait_ge(z_out[w], 16 * NCH // R)
                    sp.wait_ge(u_out[w], 16 * NCH // R)

            @block.gpsimd
            def _(g):
                step = Chain(g, pool)
                step(g.memset(mask16[:, :], 1.0))
                for one in block_mask(g, mask16[:, :], DH):
                    step(one())
                g.sem_inc(m_ready, 1)

                def lows(n, w):
                    for z in range(2):
                        g.wait_ge(mid, 2 * n + z + 1)
                        g.tensor_tensor(part[w][:, z, 2, :], left[w][z][:, :], part[w][:, z, 1, :], ALU.subtract).then_inc(low, 1)

                def step(n, w, last):
                    ln.gpsimd(g, n, w % 2)
                    if not isinstance(n, int) or n > 1:
                        lows(n - 2, (w - 2) % R)

                over(g, NCH, step, R)
                lows(NCH - 2, R - 2)
                lows(NCH - 1, R - 1)

            @block.tensor
            def _(pe):
                pe.wait_ge(w_ready, 1)
                pe.matmul(pw[:, :], wqr[:, :], wkr[:, :], start=True, stop=True).then_inc(wu_mm, 1)
                pe.wait_ge(w_ready, 2)
                pe.wait_ge(w_in, 80)

                def step(n, u, last):
                    ln.tensor_back(pe, n, u)
                    if ahead(n):
                        ln.tensor_front(pe, n + 2, u)
                    pe.wait_ge(ln.saved, n + 1)
                    for z, w in enumerate((wq, wk)):
                        wait_if(pe, left1, 2 * n - 1 + z)
                        pe.matmul(pz[z][:, :], w[:, :], xc[u][:, :], start=True, stop=True).then_inc(z_ready, 1)
                    for h in range(2):
                        wait_if(pe, uv_saved, 2 * n - 1 + h)
                        for r in range(2):
                            k = 2 * h + r
                            done = pe.matmul(puv[h][:, r, :], xc[u][:, k * C:(k + 1) * C], wuv[:, :], start=True, stop=True)
                        done.then_inc(uv_ready, 1)

                for n in range(2):
                    ln.tensor_front(pe, n, n)
                over(pe, NCH, step)

            @block.vector
            def _(v):
                step = Chain(v, vec)
                v.wait_ge(w_in, 80)
                v.wait_ge(m_ready, 1)
                step(v.tensor_mul(wkr[:, :], wkr[:, :], mask16[:, :]))
                v.sem_inc(w_ready, 1)
                v.wait_ge(wu_mm, 1)
                v.tensor_copy(wuv[:, 0:C], pw[:, :]).then_inc(w_ready, 1)

                def step(n, w, last):
                    u = w % 2
                    wait_if(v, uv_ready, 2 * n - 2)
                    ln.vector_save(v, n, xc[u][:, :])
                    if not isinstance(n, int) or n > 0:
                        results(n - 1, (w - 1) % R)
                    if ahead(n):
                        ln.vector_stats(v, n + 2, u)

                def results(n, w):
                    for z in range(2):
                        v.wait_ge(high, 2 * n + z + 1)
                        wait_if(v, low, 2 * (n - R) + z + 1)
                        v.scalar_tensor_tensor(left[w][z][:, :], pz[z][:, :], SCALE if z == 0 else 1.0,
                                               part[w][:, z, 0, :], ALU.mult, ALU.subtract).then_inc(left1, 1)
                    for h in range(2):
                        v.wait_ge(uv_ready, 2 * n + h + 1)
                        wait_if(v, u_out[w], 16 // R * (n - w))
                        v.tensor_copy(us[w][:, 2 * h:2 * h + 2, :], puv[h][:, :, 0:C])
                        v.tensor_copy(RV[:, bass.ds(4 * n + 2 * h, 2), :], puv[h][:, :, C:C + RVW]).then_inc(uv_saved, 1)

                for n in range(2):
                    ln.vector_stats(v, n, n)
                over(v, NCH, step, R, 2)
                results(NCH - 1, R - 1)

            @block.scalar
            def _(a):
                def step(n, w, last):
                    if not isinstance(n, int) or n > 0:
                        mids(n - 1, (w - 1) % R)
                    if not last:
                        ln.scalar(a, n + 1, (w + 1) % 2)
                    if ahead(n, 3):
                        ln.sync(a, n + 3, (w + 1) % 2)
                    for z in range(2):
                        a.wait_ge(z_ready, 2 * n + z + 1)
                        wait_if(a, z_out[w], 16 // R * (n - w))
                        a.activation(part[w][:, z, 0, :], pz[z][:, :], ACT.Copy, scale=SCALE if z == 0 else 1.0).then_inc(high, 1)

                def mids(n, w):
                    for z in range(2):
                        a.wait_ge(left1, 2 * n + z + 1)
                        a.copy(part[w][:, z, 1, :], left[w][z][:, :]).then_inc(mid, 1)

                for n in range(2):
                    ln.sync(a, n, n)
                ln.scalar(a, 0, 0)
                ln.sync(a, 2, 0)
                over(a, NCH, step, R)
                mids(NCH - 1, R - 1)


STEPS = 32
MAX_UNITS = 128
VW = 2 * RH * DH
FIRST_MAX = 3
LAST_MAX = STEPS - 4
PER_STEP = -(-MAX_UNITS // (LAST_MAX + 1 - FIRST_MAX))
EXP_AT, SUM_AT, OUT_AT, WOUT_AT = 13, 15, 19, 22


def side_work(k, post, following):
    work = []
    if post:
        if k < 8:
            work.append(("tokens", k))
        if k == OUT_AT:
            work += [("back", 0), ("back", 1)]
        if k == WOUT_AT:
            work += [("wout", 0), ("wout", 1)]
    if following and k >= FIRST_MAX:
        first = (k - FIRST_MAX) * PER_STEP
        work += [("max", n) for n in range(first, min(first + PER_STEP, MAX_UNITS))]
        if k == LAST_MAX + 1:
            work.append(("rows", 0))
    return work


def phase_attn(nc, K, D, X):
    SIDE1 = MAX_UNITS + 1
    SIDE2 = SIDE1 + 12
    with Mem(nc, "at") as m:
        qo = [m.sb(f"qo{u}", [KM, SH, N], BF16) for u in range(2)]
        ko = [m.sb(f"ko{u}", [KM, SH, N], BF16) for u in range(2)]
        P = [m.sb(f"P{u}", [C, 4, CH]) for u in range(2)]
        sums = m.sb("sums", [C, 4, N])
        numT = m.sb("numT", [C, 8, 2 * C])
        prod = m.sb("prod", [C, 8, 2 * C])
        ub = m.sb("ub", [C, 8, C])
        oc = prod[:, :, :].rearrange("p i n -> p (i n)")[:, 0:N]
        wout = m.sb("wout", [C, C])
        recT = m.sb("recT", [C, 64])
        sim = m.sb("sim", [C, 64, 2])
        sm1 = m.sb("sm1", [C, 64])
        mx = m.sb("mx", [C, SH * 8, 2])
        negmax = m.sb("negmax", [C, SH * 8])
        rvb = [m.sb(f"rvb{u}", [C, 8, VW]) for u in range(2)]
        mleft = m.sb("mleft", [64, C])
        mrow = m.sb("mrow", [64, 3, C], BF16)
        RV = K["rv"]
        side = [m.ps(f"side{u}", [C, CH]) for u in range(2)]
        S = [m.ps(f"S{u}", [C, 2, CH]) for u in range(2)]
        pv_acc = [m.ps(f"pv{h}", [C, CH]) for h in range(2)]
        w_in, const_ready = m.sem("w_in"), m.sem("const_ready")
        op_in, row_in = [m.sem("op_in0"), m.sem("op_in1")], [m.sem("row_in0"), m.sem("row_in1")]
        u_in, rv_ready = m.sem("u_in"), m.sem("rv_ready")
        side_ready, side_saved = m.sem("side_ready"), m.sem("side_saved")
        s_ready, p_ready, pv_done, grp_saved = (m.sem(x) for x in ("s_ready", "p_ready", "pv_done", "grp_saved"))
        row_step, row_ready = m.sem("row_step"), m.sem("row_ready")
        far_ready = m.sem("far_ready")
        post_step, sim_ready, e_ready, esum_ready, rsum_ready, out_ready = (
            m.sem(x) for x in ("post_step", "sim_ready", "e_ready", "esum_ready", "rsum_ready", "out_ready"))

        def side_base(b):
            return SIDE2 * b + 2 * SIDE1 - SIDE2 if not isinstance(b, int) or b else SIDE1

        def side_at(b, k, what, post=True, following=True):
            n = 0
            for j in range(STEPS):
                for w in side_work(j, post, following):
                    n += 1
                    if j == k and w == what:
                        return side_base(b) + n
            raise ValueError(what)

        with nc.Block() as block:
            @block.sync
            def _(sp):
                sp.dma_start(wout[:, :], D["w_out"]).then_inc(w_in, 16)

                def load(b, u):
                    for z, (dst, terms) in enumerate(((qo[u], Q_TERMS), (ko[u], K_TERMS))):
                        for i, t in enumerate(terms):
                            sp.dma_start(dst[DH * i:DH * i + DH, :, :],
                                         D["qk"][z, t, :, bass.ds(b * N, N)].rearrange("(s d) n -> d s n", d=DH))\
                              .then_inc(op_in[u], 16)

                def rows(b, u):
                    sp.wait_ge(row_ready, b + 1)
                    for t in range(3):
                        sp.dma_start(qo[u][KQ + t:KQ + t + 1, :, :], mrow[:, t, :]).then_inc(row_in[u], 16)

                load(0, 0)
                load(1, 1)
                rows(0, 0)

                def slot(b, u, last):
                    if not isinstance(b, int) or b:
                        sp.wait_ge(side_ready, side_at(b, OUT_AT, ("back", 1), following=not last))
                    sp.dma_start(ub[:, :, :], D["u"][:, bass.ds(8 * b, 8), :]).then_inc(u_in, 16)
                    if not last:
                        rows(b + 1, 1 - u)
                    if not isinstance(b, int) or b < B - 2:
                        sp.wait_ge(s_ready, 64 * b + 64)
                        load(b + 2, u)

                over(sp, B, slot)

            @block.gpsimd
            def _(g):
                for u in range(2):
                    g.memset(rvb[u][:, :, RH * DH:VW], 1.0).then_inc(const_ready, 1)
                for u in range(2):
                    g.wait_ge(const_ready, u + 2)
                    g.memset(ko[u][KQ:KM, :, :], 1.0).then_inc(const_ready, 1)

                def retrieve(b, tokens):
                    step = Chain(g, post_step, 11 * b)
                    g.wait_ge(side_saved, tokens)
                    g.wait_ge(u_in, 16 * b + 16)
                    heads = prod[:, :, :].rearrange("p i (s d) -> p (i s) d", d=DH)
                    nv = numT[:, :, :].rearrange("p i (s r d) -> p (i s) r d", r=RH, d=DH)
                    pv = prod[:, :, :].rearrange("p i (s r d) -> p (i s) r d", r=RH, d=DH)
                    step(g.tensor_tensor(pv, nv, ub[:, :, :].rearrange("p i (s o d) -> p (i s) o d", o=1, d=DH)
                                         .to_broadcast([C, 64, RH, DH]), ALU.mult))
                    for w in (8, 4, 2):
                        step(g.tensor_tensor(heads[:, :, 0:w], heads[:, :, 0:w], heads[:, :, w:2 * w], ALU.add))
                    step(g.tensor_tensor(sim[:, :, :].rearrange("p s r -> p (s r)"), heads[:, :, 0], heads[:, :, 1], ALU.add))
                    step(g.tensor_tensor(sim[:, :, :], sim[:, :, :],
                                         recT[:, :].rearrange("p (s o) -> p s o", o=1).to_broadcast([C, 64, 2]), ALU.mult))
                    step(g.tensor_tensor(sm1[:, :], sim[:, :, 0], sim[:, :, 1], ALU.subtract))
                    g.sem_inc(sim_ready, 1)
                    g.wait_ge(e_ready, b + 1)
                    g.tensor_tensor(sm1[:, :], sim[:, :, 0], sim[:, :, 1], ALU.add).then_inc(esum_ready, 1)
                    g.wait_ge(rsum_ready, b + 1)
                    step(g.tensor_tensor(sm1[:, :], sm1[:, :], recT[:, :], ALU.mult))
                    step(g.tensor_tensor(sim[:, :, :], sim[:, :, :],
                                         sm1[:, :].rearrange("p (s o) -> p s o", o=1).to_broadcast([C, 64, 2]), ALU.mult))
                    step(g.tensor_tensor(heads, numT[:, :, :].rearrange("p i (s d) -> p (i s) d", d=DH),
                                         sim[:, :, :].rearrange("p s (r o) -> p (s r) o", o=1).to_broadcast([C, 128, DH]),
                                         ALU.mult))
                    step(g.tensor_tensor(ub[:, :, :].rearrange("p i (s d) -> p (i s) d", d=DH),
                                         pv[:, :, 0, :], pv[:, :, 1, :], ALU.add))
                    assert step.n == 11
                    g.sem_inc(out_ready, 1)

                with g.Fori(1, B - 1) as b:
                    retrieve(b - 1, side_at(b, 7, ("tokens", 7)))
                retrieve(B - 2, side_at(B - 1, 7, ("tokens", 7), following=False))
                retrieve(B - 1, side_base(B) - SIDE1 + 8)

            @block.tensor
            def _(pe):
                pe.wait_ge(w_in, 16)
                pe.wait_ge(const_ready, 4)

                def fill(w, b, u, at, bank):
                    kind, n = w
                    wait_if(pe, side_saved, at - 1)
                    if kind == "max":
                        s, rest = divmod(n, 16)
                        i, h = divmod(rest, 2)
                        return pe.matmul(side[bank][:, :], qo[1 - u][0:KQ, s, i * C:(i + 1) * C],
                                         ko[1 - u][0:KQ, s, h * CH:(h + 1) * CH], start=True, stop=True)
                    if kind == "rows":
                        pe.wait_ge(row_step, 4 * (b + 1) + 1)
                        return pe.matmul(side[bank][0:64, 0:C], negmax[:, :], K["ident"][:, :], start=True, stop=True)
                    if kind == "tokens":
                        for q in range(4):
                            last = pe.transpose(side[bank][:, q * C:(q + 1) * C], sums[:, q, n * C:(n + 1) * C], K["ident"][:, :])
                        return last
                    if kind == "back":
                        pe.wait_ge(out_ready, b)
                        for r in range(4):
                            last = pe.transpose(side[bank][:, r * C:(r + 1) * C], ub[:, 4 * n + r, :], K["ident"][:, :])
                        return last
                    pe.wait_ge(side_saved, at - n)
                    return pe.matmul(side[bank][:, :], wout[:, :], oc[:, n * CH:(n + 1) * CH], start=True, stop=True)

                def scores(b, u, k, hp):
                    g, j = divmod(k, 8)
                    quad, half = divmod(g, 2)
                    wait_if(pe, p_ready, 64 * b + 2 * k - 1 + hp)
                    for i in range(2):
                        s = 4 * quad + 2 * hp + i
                        last = pe.matmul(S[hp][:, i, :], ko[u][:, s, j * C:(j + 1) * C],
                                         qo[u][:, s, half * CH:(half + 1) * CH], start=True, stop=True)
                    last.then_inc(s_ready, 1)

                def values(b, u, k, hp):
                    g, j = divmod(k, 8)
                    pe.wait_ge(p_ready, 64 * b + 2 * k + hp + 1)
                    if j == 0:
                        wait_if(pe, grp_saved, 4 * b + g)
                    for i in range(2):
                        last = pe.matmul(pv_acc[hp][64 * i:64 * i + 64, :], rvb[u][:, j, :], P[k % 2][:, 2 * hp + i, :],
                                         start=(j == 0), stop=(j == 7))
                    if hp:
                        last.then_inc(pv_done, 1)

                def lead(b, u, k):
                    if k == 0:
                        pe.wait_ge(row_in[u], 24 * (b - u) + 48)
                    for hp in range(2):
                        scores(b, u, k, hp)

                pe.wait_ge(op_in[0], 192)
                for n in range(MAX_UNITS):
                    fill(("max", n), -1, 1, n, n % 2).then_inc(side_ready, 1)
                fill(("rows", 0), -1, 1, MAX_UNITS, 0).then_inc(side_ready, 1)

                def slot(b, u, last):
                    post = not isinstance(b, int) or b > 0
                    at = 0
                    pe.wait_ge(rv_ready, b + 1)
                    if isinstance(b, int) and b == 0:
                        lead(b, u, 0)
                        lead(b, u, 1)
                    for k in range(STEPS):
                        if k == FIRST_MAX and not last:
                            pe.wait_ge(op_in[1 - u], 96 * (b + 1 - (1 - u)) + 192)
                        work = side_work(k, post, not last)
                        for part in range(4):
                            for w in work[(part * len(work) + 2) // 4:((part + 1) * len(work) + 2) // 4]:
                                fill(w, b, u, side_base(b) + at, (u + 1 + at) % 2).then_inc(side_ready, 1)
                                at += 1
                            if part < 2:
                                values(b, u, k, part)
                            elif k + 2 < STEPS:
                                scores(b, u, k + 2, part - 2)
                            elif not last and part == 2:
                                lead(b + 1, 1 - u, k + 2 - STEPS)

                over(pe, B, slot)
                pe.wait_ge(grp_saved, 4 * B)
                for at, w in enumerate([("tokens", k) for k in range(8)] + [("back", 0), ("back", 1), ("wout", 0), ("wout", 1)]):
                    fill(w, B, 0, side_base(B) - SIDE1 + at, at % 2).then_inc(side_ready, 1)

            @block.vector
            def _(v):
                def drain(w, b, at, bank):
                    kind, n = w
                    v.wait_ge(side_ready, at + 1)
                    if kind == "max":
                        v.reduce_max(mx[:, n // 2, n % 2:n % 2 + 1], side[bank][:, :], AX.X).then_inc(side_saved, 1)
                        if n == MAX_UNITS - 1:
                            v.wait_ge(side_saved, at + 1)
                            v.tensor_reduce(negmax[:, :], mx[:, :, :], AX.X, ALU.max, negate=True).then_inc(row_step, 1)
                    elif kind == "rows":
                        base = 4 * (b + 1)
                        src = side[bank][0:64, 0:C]
                        rows_free(b)
                        v.tensor_copy(mrow[:, 0, :], src).then_inc(row_step, 1)
                        v.wait_ge(row_step, base + 2)
                        v.tensor_tensor(mleft[:, :], src, mrow[:, 0, :], ALU.subtract).then_inc(row_step, 1)
                        v.wait_ge(row_step, base + 3)
                        v.tensor_copy(mrow[:, 1, :], mleft[:, :]).then_inc(row_step, 1)
                        v.wait_ge(row_step, base + 4)
                        v.tensor_tensor(mrow[:, 2, :], mleft[:, :], mrow[:, 1, :], ALU.subtract).then_inc(row_ready, 1)
                        v.sem_inc(side_saved, 1)
                    elif kind == "tokens":
                        if n == 0:
                            wait_if(v, out_ready, b - 1)
                        v.tensor_copy(numT[:, n, :].rearrange("p (s d) -> p s d", d=RH * DH),
                                      side[bank][:, :].rearrange("p (s w) -> p s w", w=VW)[:, :, 0:RH * DH])
                        v.reciprocal(recT[:, 8 * n:8 * n + 8], side[bank][:, RH * DH::VW]).then_inc(side_saved, 1)
                    elif kind == "back":
                        v.tensor_copy(oc[:, n * CH:(n + 1) * CH], side[bank][:, :]).then_inc(side_saved, 1)
                    else:
                        xb = X[:, bass.ds((b - 1) * N + n * CH, CH)]
                        v.tensor_tensor(xb, xb, side[bank][:, :], ALU.add).then_inc(side_saved, 1)

                def rows_free(b):
                    if not isinstance(b, int) or b >= 0:
                        v.wait_ge(row_in[U[0]], 24 * (b - U[0]) + 48)

                U = [0]
                for n in range(MAX_UNITS):
                    drain(("max", n), -1, n, n % 2)
                drain(("rows", 0), -1, MAX_UNITS, 0)

                def slot(b, u, last):
                    post = not isinstance(b, int) or b > 0
                    U[0] = u
                    wait_if(v, pv_done, 32 * b - 32)
                    v.tensor_copy(rvb[u][:, :, 0:RH * DH], RV[:, bass.ds(8 * b, 8), :]).then_inc(rv_ready, 1)
                    at = 0
                    for k in range(STEPS):
                        if k == SUM_AT and post:
                            v.wait_ge(esum_ready, b)
                            v.reciprocal(sm1[:, :], sm1[:, :]).then_inc(rsum_ready, 1)
                        for w in side_work(k, post, not last):
                            drain(w, b, side_base(b) + at, (u + 1 + at) % 2)
                            at += 1

                over(v, B, slot)
                for at, w in enumerate([("tokens", k) for k in range(8)] + [("back", 0), ("back", 1), ("wout", 0), ("wout", 1)]):
                    if at == 8:
                        v.wait_ge(esum_ready, B)
                        v.reciprocal(sm1[:, :], sm1[:, :]).then_inc(rsum_ready, 1)
                    drain(w, B, side_base(B) - SIDE1 + at, at % 2)

            @block.scalar
            def _(a):
                def exps(b, k):
                    for hp in range(2):
                        a.wait_ge(s_ready, 64 * b + 2 * k + hp + 1)
                        wait_if(a, pv_done, 32 * b + k - 1)
                        a.activation(P[k % 2][:, 2 * hp:2 * hp + 2, :], S[hp][:, :, :], ACT.Exp).then_inc(p_ready, 1)

                def save(b, g, post, last):
                    quad, half = divmod(g, 2)
                    cols = slice(half * CH, (half + 1) * CH)
                    a.wait_ge(pv_done, 32 * b + 8 * g + 8)
                    if g == 0 and post:
                        a.wait_ge(side_ready, side_at(b, 7, ("tokens", 7), following=not last))
                    a.copy(sums[:, 2 * quad, cols], pv_acc[0][:, :])
                    a.copy(sums[:, 2 * quad + 1, cols], pv_acc[1][:, :]).then_inc(grp_saved, 1)

                def softmax2(b):
                    a.wait_ge(sim_ready, b + 1)
                    a.activation(sim[:, :, 0], sm1[:, :], ACT.Relu, scale=-1.0).then_inc(far_ready, 1)
                    a.activation(sim[:, :, 1], sm1[:, :], ACT.Relu).then_inc(far_ready, 1)
                    a.wait_ge(far_ready, 2 * b + 2)
                    a.activation(sim[:, :, :], sim[:, :, :], ACT.Exp, scale=-SCALE).then_inc(e_ready, 1)

                def slot(b, u, last):
                    post = not isinstance(b, int) or b > 0
                    if isinstance(b, int) and b == 0:
                        exps(b, 0)
                    for k in range(STEPS):
                        if k + 1 < STEPS:
                            exps(b, k + 1)
                        elif not last:
                            exps(b + 1, 0)
                        if k == EXP_AT and post:
                            softmax2(b - 1)
                        if k % 8 == 7:
                            save(b, k // 8, post, last)

                over(a, B, slot)
                softmax2(B - 1)


def phase_norm(nc, K, X, Y, tag, tokens=None):
    with Mem(nc, tag) as m:
        R = 4
        ln = LayerNorm(m, K, X, R)
        tok_out = [m.sem(f"tok_out{u}") for u in range(R)]
        with nc.Block() as block:
            @block.sync
            def _(sp):
                over(sp, NCH, lambda n, u, last: ln.sync(sp, n, u), R)

            @block.gpsimd
            def _(g):
                over(g, NCH, lambda n, u, last: ln.gpsimd(g, n, u), R)

            @block.scalar
            def _(a):
                def step(n, u, last):
                    if tokens is None:
                        ln.scalar(a, n, u)
                        return
                    wait_if(a, tok_out[u], 16 // R * (n - u))
                    ln.scalar(a, n, u)
                    a.wait_ge(ln.xt_ready, n + 1)
                    a.dma_start(tokens[bass.ds(n * CH, CH), :].rearrange("(r p) c -> p r c", p=C), ln.xt[u][:, :, :])\
                     .then_inc(tok_out[u], 16)

                over(a, NCH, step, R)
                if tokens is not None:
                    for u in range(R):
                        a.wait_ge(tok_out[u], 16 * NCH // R)

            @block.tensor
            def _(pe):
                def step(n, u, last):
                    ln.tensor_back(pe, n, u)
                    if ahead(n, R):
                        ln.tensor_front(pe, n + R, u)

                for n in range(R):
                    ln.tensor_front(pe, n, n)
                over(pe, NCH, step, R)

            @block.vector
            def _(v):
                def step(n, u, last):
                    ln.vector_save(v, n, Y[:, bass.ds(n * CH, CH)])
                    if ahead(n, R):
                        ln.vector_stats(v, n + R, u)

                for n in range(R):
                    ln.vector_stats(v, n, n)
                over(v, NCH, step, R)



E6 = 6
NP11 = 11
F = 341
FT = 16
PARTITIONS_OF_6 = [(6,), (5, 1), (4, 2), (4, 1, 1), (3, 3), (3, 2, 1), (3, 1, 1, 1), (2, 2, 2), (2, 2, 1, 1),
                   (2, 1, 1, 1, 1), (1, 1, 1, 1, 1, 1)]


def partition_weights():
    import numpy as np
    w = np.zeros((NP11, E6), np.float32)
    for i, parts in enumerate(PARTITIONS_OF_6):
        for j, part in enumerate(parts):
            w[i, j] = part / 6
    return w


def phase_router(nc, K, D, Y, wcol, b2w):
    with Mem(nc, "rt") as m:
        rw = m.sb("rw", [C, NP11])
        pwx = m.sb("pwx", [NP11, FT * C])
        pw6 = m.sb("pw6", [NP11, E6])
        b2 = m.sb("b2", [E6, C])
        mean = m.sb("mean", [C, B])
        p = m.sb("p", [B, NP11])
        rev = m.sb("rev", [B, NP11])
        t1, oh1, oh2 = m.sb("t1", [B, NP11]), m.sb("oh1", [B, NP11]), m.sb("oh2", [B, NP11])
        cv = m.sb("cv", [B, 8])
        wT = m.sb("wT", [NP11, B])
        ew, ewt = m.sb("ew", [E6, B]), m.sb("ewt", [E6, B])
        wraw = m.sb("wraw", [C, FT, B])
        pl = m.ps("pl", [B, NP11])
        pt = m.ps("pt", [NP11, B])
        px = m.ps("px", [C, FT, B])
        p6 = m.ps("p6", [E6, B])
        pb = m.ps("pb", [C, B])
        w_in, vec, pe_s, act, rev_ready = (m.sem(x) for x in ("w_in", "vec", "pe", "act", "rev_ready"))
        mean_ready, max_ready, wt_ready, w11_ready, ew_ready = (
            m.sem(x) for x in ("mean_ready", "max_ready", "wt_ready", "w11_ready", "ew_ready"))
        NM, SUM, V1, V2, R1, S = (cv[:, i:i + 1] for i in range(6))
        with nc.Block() as block:
            @block.sync
            def _(sp):
                for dst, src in ((rw, "router_wT"), (pwx, "pwx"), (pw6, "pw6"), (b2, "ffn_b2")):
                    sp.dma_start(dst[:, :], D[src]).then_inc(w_in, 16)

            @block.gpsimd
            def _(g):
                g.iota(rev[:, :], pattern=[[-1, NP11]], base=NP11, channel_multiplier=0,
                       allow_small_or_imprecise_dtypes=True).then_inc(rev_ready, 1)

            @block.tensor
            def _(pe):
                pe.wait_ge(w_in, 64)
                pe.wait_ge(mean_ready, 1)
                pe.matmul(pl[:, :], mean[:, :], rw[:, :], start=True, stop=True).then_inc(pe_s, 1)
                pe.wait_ge(w11_ready, 1)
                pe.transpose(pt[:, :], t1[:, :], K["ident"][0:B, 0:B]).then_inc(pe_s, 1)
                pe.wait_ge(wt_ready, 1)
                for f in range(FT):
                    pe.matmul(px[:, f, :], pwx[:, f * C:(f + 1) * C], wT[:, :], start=True, stop=True)
                pe.matmul(p6[:, :], pw6[:, :], wT[:, :], start=True, stop=True).then_inc(pe_s, 1)
                pe.wait_ge(ew_ready, 1)
                pe.matmul(pb[:, :], b2[:, :], ew[:, :], start=True, stop=True).then_inc(pe_s, 1)

            @block.scalar
            def _(a):
                a.wait_ge(max_ready, 1)
                a.activation(p[:, :], pl[:, :], ACT.Exp, bias=NM, accum_out=SUM).then_inc(act, 1)

            @block.vector
            def _(v):
                step = Chain(v, vec)
                for b in range(0, B, 4):
                    last = v.reduce_sum(mean[:, b:b + 4], Y[:, b * N:(b + 4) * N].rearrange("c (b n) -> c b n", n=N), AX.X)
                    step(last)
                step(v.tensor_scalar(mean[:, :], mean[:, :], 1.0 / N, None, ALU.mult))
                v.sem_inc(mean_ready, 1)
                v.wait_ge(pe_s, 1)
                step(v.tensor_reduce(NM, pl[:, :], AX.X, ALU.max, negate=True))
                v.sem_inc(max_ready, 1)
                v.wait_ge(act, 1)
                v.wait_ge(rev_ready, 1)
                step(v.reciprocal(SUM, SUM))
                step(v.tensor_scalar(p[:, :], p[:, :], SUM, None, ALU.mult))
                for value, onehot in ((V1, oh1), (V2, oh2)):
                    step(v.reduce_max(value, p[:, :], AX.X))
                    step(v.scalar_tensor_tensor(t1[:, :], p[:, :], value, rev[:, :], ALU.is_equal, ALU.mult))
                    step(v.reduce_max(R1, t1[:, :], AX.X))
                    step(v.tensor_scalar(onehot[:, :], rev[:, :], R1, None, ALU.is_equal))
                    step(v.scalar_tensor_tensor(p[:, :], onehot[:, :], -2.0, p[:, :], ALU.mult, ALU.add))
                step(v.tensor_add(S, V1, V2))
                step(v.reciprocal(S, S))
                step(v.tensor_mul(V1, V1, S))
                step(v.tensor_mul(V2, V2, S))
                step(v.tensor_scalar(t1[:, :], oh1[:, :], V1, None, ALU.mult))
                step(v.scalar_tensor_tensor(t1[:, :], oh2[:, :], V2, t1[:, :], ALU.mult, ALU.add))
                v.sem_inc(w11_ready, 1)
                v.wait_ge(pe_s, 2)
                step(v.tensor_copy(wT[:, :], pt[:, :]))
                v.sem_inc(wt_ready, 1)
                v.wait_ge(pe_s, 3)
                step(v.tensor_copy(wraw[:, :, :], px[:, :, :]))
                step(v.scalar_tensor_tensor(wcol[:, :, :], wraw[:, :, :], 1e-6, wraw[:, :, :], ALU.is_gt, ALU.mult))
                step(v.tensor_copy(ewt[:, :], p6[:, :]))
                step(v.scalar_tensor_tensor(ew[:, :], ewt[:, :], 1e-6, ewt[:, :], ALU.is_gt, ALU.mult))
                v.sem_inc(ew_ready, 1)
                v.wait_ge(pe_s, 4)
                step(v.tensor_copy(b2w[:, :], pb[:, :]))


def phase_ffn(nc, K, D, X, Y, wcol, b2w):
    R = 4
    LEAD = 2
    with Mem(nc, "ff") as m:
        w1 = m.sb("w1", [C, FT, C])
        w2 = m.sb("w2", [C, FT, C])
        b1 = m.sb("b1", [C, FT])
        w2s = [m.sb(f"w2s{u}", [C, FT, C]) for u in range(2)]
        hs = [m.sb(f"hs{r}", [C, CH]) for r in range(R)]
        ph = [m.ps(f"ph{r}", [C, CH]) for r in range(R)]
        po = [m.ps(f"po{h}", [C, CH]) for h in range(2)]
        w_in, w2_ready, h_mm, h_ready, h_used, o_mm, x_ready = (
            m.sem(x) for x in ("w_in", "w2_ready", "h_mm", "h_ready", "h_used", "o_mm", "x_ready"))
        ITEMS = 2 * FT
        with nc.Block() as block:
            @block.sync
            def _(sp):
                sp.dma_start(w1[:, :, :], D["W1"]).then_inc(w_in, 16)
                sp.dma_start(w2[:, :, :], D["W2"]).then_inc(w_in, 16)
                sp.dma_start(b1[:, :], D["b1"]).then_inc(w_in, 16)

            @block.tensor
            def _(pe):
                pe.wait_ge(w_in, 48)

                def up(b, j):
                    wait_if(pe, h_ready, ITEMS * b + j - R + 1)
                    half, f = divmod(j, FT)
                    pe.matmul(ph[j % R][:, :], w1[:, f, :], Y[:, bass.ds(b * N + half * CH, CH)],
                              start=True, stop=True).then_inc(h_mm, 1)

                def batch(b, u, last):
                    pe.wait_ge(w2_ready, b + 1)
                    for j in range(ITEMS):
                        half, f = divmod(j, FT)
                        if j + LEAD < ITEMS:
                            up(b, j + LEAD)
                        elif not last:
                            up(b + 1, j + LEAD - ITEMS)
                        if f == 0:
                            wait_if(pe, x_ready, 2 * b + half - 1)
                        pe.wait_ge(h_ready, ITEMS * b + j + 1)
                        done = pe.matmul(po[half][:, :], w2s[u][:, f, :], hs[j % R][:, :],
                                         start=(f == 0), stop=(f == FT - 1)).then_inc(h_used, 1)

                for j in range(LEAD):
                    up(0, j)
                over_batches(pe, batch)

            @block.scalar
            def _(a):
                a.wait_ge(w_in, 48)

                def batch(b, u, last):
                    for j in range(ITEMS):
                        a.wait_ge(h_mm, ITEMS * b + j + 1)
                        wait_if(a, h_used, ITEMS * b + j - R + 1)
                        a.activation(hs[j % R][:, :], ph[j % R][:, :], ACT.Gelu,
                                     bias=b1[:, j % FT:j % FT + 1]).then_inc(h_ready, 1)

                over_batches(a, batch)

            @block.vector
            def _(v):
                v.wait_ge(w_in, 48)

                def scale(b, u):
                    wait_if(v, h_used, ITEMS * (b - 1))
                    v.tensor_tensor(w2s[u][:, :, :], w2[:, :, :],
                                    wcol[:, :, bass.ds(b, 1)].to_broadcast([C, FT, C]), ALU.mult).then_inc(w2_ready, 1)

                def batch(b, u, last):
                    for half in range(2):
                        v.wait_ge(h_used, ITEMS * b + FT * (half + 1))
                        xb = X[:, bass.ds(b * N + half * CH, CH)]
                        v.scalar_tensor_tensor(xb, po[half][:, :], b2w[:, bass.ds(b, 1)], xb, ALU.add, ALU.add)\
                         .then_inc(x_ready, 1)
                        if half == 0 and not last:
                            scale(b + 1, 1 - u)

                scale(0, 0)
                over_batches(v, batch)



G8 = 8
H4 = 4


def phase_gqa(nc, K, D, X, Y):
    GH = G8 * H4
    TL = N // C
    with Mem(nc, "gq") as m:
        wk = m.sb("wk", [C, G8, C])
        wqT = m.sb("wqT", [C, GH, C])
        wvT = m.sb("wvT", [C, G8, C])
        wo = m.sb("wo", [C, G8, C])
        bkT, bvT, bqT, bo = m.sb("bkT", [C, G8]), m.sb("bvT", [C, G8]), m.sb("bqT", [C, GH]), m.sb("bo", [C, 1])
        xsum = m.sb("xsum", [C, B])
        ksum = m.sb("ksum", [C, G8, B])
        bk_ = m.sb("bqk", [C, GH, B])
        sw = m.sb("sw", [C, B, GH])
        sb_ = m.sb("sbias", [C, B, GH])
        vo = m.sb("vo", [C, G8, C])
        bvo = m.sb("bvo", [C, G8])
        ys = [m.sb(f"ys{u}", [C, N]) for u in range(2)]
        sc = m.sb("sc", [C, TL, GH])
        red = m.sb("red", [C, TL * H4])
        wsum = m.sb("wsum", [C, G8])
        mix = m.sb("mix", [C, G8, C])
        A = [m.sb(f"A{u}", [C, C]) for u in range(2)]
        bias = [m.sb(f"bias{u}", [C, 1]) for u in range(2)]
        bt = m.sb("bt", [C, G8])
        pa = m.ps("pa", [C, CH])
        pc = m.ps("pc", [C, CH])
        pv = [m.ps(f"pv{h}", [C, 4, C]) for h in range(2)]
        psc = m.ps("psc", [C, TL, GH])
        pws = m.ps("pws", [C, TL, GH])
        po = [m.ps(f"po{h}", [C, CH]) for h in range(2)]
        w_in, vec, prep_mm, xs_ready, ks_ready, prep_done = (m.sem(x) for x in ("w_in", "vec", "prep_mm", "xs_ready", "ks_ready", "prep_done"))
        y_in = [m.sem("y_in0"), m.sem("y_in1")]
        s_mm, sub_ready, sub_ready2, e_ready, w_ready, ws_mm, a_ready, o_mm, x_ready, dstep = (
            m.sem(x) for x in ("s_mm", "biased", "below_max", "e_ready", "w_ready", "ws_mm", "a_ready", "o_mm", "x_ready", "dstep"))
        NW = 9

        def y_count(b, u):
            return (b // 2 + 1) * 16 if isinstance(b, int) else 8 * b + (16 - 8 * u)

        with nc.Block() as block:
            @block.sync
            def _(sp):
                for dst, src in ((wk, "Wk"), (wqT, "WqT"), (wvT, "WvT"), (wo, "Wo")):
                    sp.dma_start(dst[:, :, :], D[src]).then_inc(w_in, 16)
                for dst, src in ((bkT, "bkT"), (bvT, "bvT"), (bqT, "bqT"), (bo, "bo")):
                    sp.dma_start(dst[:, :], D[src]).then_inc(w_in, 16)

                def step(b, u, last):
                    wait_if(sp, s_mm, b - 1)
                    sp.dma_start(ys[u][:, :], Y[:, bass.ds(b * N, N)]).then_inc(y_in[u], 16)

                over(sp, B, step)

            @block.tensor
            def _(pe):
                pe.wait_ge(w_in, 128)
                pe.wait_ge(xs_ready, 1)
                for g in range(G8):
                    last = pe.matmul(pc[:, g * B:(g + 1) * B], wk[:, g, :], xsum[:, :], start=True, stop=True)
                last.then_inc(prep_mm, 1)
                for g in range(G8):
                    last = pe.matmul(pv[g // 4][:, g % 4, :], wvT[:, g, :], wo[:, g, :], start=True, stop=True)
                last.then_inc(prep_mm, 1)
                for g in range(G8):
                    last = pe.matmul(pws[:, 0, g:g + 1], wo[:, g, :], bvT[:, g:g + 1], start=True, stop=True)
                last.then_inc(prep_mm, 1)
                pe.wait_ge(ks_ready, 1)
                for i in range(GH):
                    last = pe.matmul(pa[:, i * B:(i + 1) * B], wqT[:, i, :], ksum[:, i // H4, :], start=True, stop=True)
                last.then_inc(prep_mm, 1)
                pe.wait_ge(ks_ready, 2)
                pe.matmul(pc[:, :], K["ones"][:, :], bk_[:, :, :].rearrange("p i b -> p (i b)"), start=True, stop=True).then_inc(prep_mm, 1)
                pe.wait_ge(prep_done, 1)

                def scores(b, u):
                    pe.wait_ge(y_in[u], y_count(b, u))
                    wait_if(pe, sub_ready, b)
                    for t in range(TL):
                        last = pe.matmul(psc[:, t, :], ys[u][:, t * C:(t + 1) * C], sw[:, bass.ds(b, 1), :].rearrange("p o g -> p (o g)"),
                                         start=True, stop=True)
                    last.then_inc(s_mm, 1)

                def sums(b):
                    pe.wait_ge(w_ready, b + 1)
                    pe.matmul(pws[:, :, :], K["ones"][:, :], sc[:, :, :], start=True, stop=True).then_inc(ws_mm, 1)

                scores(0, 0)
                sums(0)
                scores(1, 1)

                def step(b, u, last):
                    if not isinstance(b, int) or b + 2 < B:
                        scores(b + 2, u)
                    pe.wait_ge(a_ready, b + 1)
                    for h in range(2):
                        wait_if(pe, x_ready, 2 * b - 1 + h)
                        pe.matmul(po[h][:, :], A[u][:, :], Y[:, bass.ds(b * N + h * CH, CH)], start=True, stop=True).then_inc(o_mm, 1)
                    if not last:
                        sums(b + 1)

                over(pe, B, step)

            @block.scalar
            def _(a):
                with a.Fori(0, B) as b:
                    a.wait_ge(sub_ready2, b + 1)
                    a.activation(sc[:, :, :], sc[:, :, :], ACT.Exp, scale=C ** -0.5).then_inc(e_ready, 1)

            @block.vector
            def _(v):
                step0 = Chain(v, vec)
                v.wait_ge(w_in, 128)
                for b in range(0, B, 4):
                    step0(v.reduce_sum(xsum[:, b:b + 4], Y[:, b * N:(b + 4) * N].rearrange("c (b n) -> c b n", n=N), AX.X))
                v.sem_inc(xs_ready, 1)
                step0(v.tensor_scalar(bkT[:, :], bkT[:, :], float(N), None, ALU.mult))
                v.wait_ge(prep_mm, 1)
                step0(v.tensor_tensor(ksum[:, :, :], pc[:, 0:G8 * B].rearrange("p (g b) -> p g b", b=B),
                                      bkT[:, :].rearrange("p (g o) -> p g o", o=1).to_broadcast([C, G8, B]), ALU.add))
                v.sem_inc(ks_ready, 1)
                for g in range(G8):
                    last = v.tensor_tensor(bk_[:, g * H4:(g + 1) * H4, :],
                                           ksum[:, g:g + 1, :].to_broadcast([C, H4, B]),
                                           bqT[:, g * H4:(g + 1) * H4].rearrange("p (g o) -> p g o", o=1).to_broadcast([C, H4, B]), ALU.mult)
                step0(last)
                v.sem_inc(ks_ready, 1)
                v.wait_ge(prep_mm, 3)
                for h in range(2):
                    step0(v.tensor_copy(vo[:, 4 * h:4 * h + 4, :], pv[h][:, :, :]))
                step0(v.tensor_copy(bvo[:, :], pws[:, 0, 0:G8]))
                v.wait_ge(prep_mm, 5)
                for dst, src in ((sw, pa), (sb_, pc)):
                    for h in range(H4):
                        step0(v.tensor_copy(dst[:, :, h * G8:(h + 1) * G8],
                                            src[:, :].rearrange("p (g h b) -> p h b g", h=H4, b=B)[:, h, :, :]))
                v.sem_inc(prep_done, 1)

                scv = sc[:, :, :].rearrange("p t (h g) -> p (t h) g", g=G8)

                def below_max(b, st):
                    v.wait_ge(s_mm, b + 1)
                    wait_if(v, ws_mm, b)
                    v.tensor_tensor(sc[:, :, :], psc[:, :, :], sb_[:, bass.ds(b, 1), :].to_broadcast([C, TL, GH]), ALU.add)\
                     .then_inc(sub_ready, 1)
                    v.wait_ge(sub_ready, b + 1)
                    st(v.reduce_max(red[:, :], scv, AX.X))
                    v.tensor_tensor(scv, scv, red[:, :].rearrange("p (t o) -> p t o", o=1).to_broadcast([C, TL * H4, G8]),
                                    ALU.subtract).then_inc(sub_ready2, 1)

                def weights(b, st):
                    v.wait_ge(e_ready, b + 1)
                    st(v.reduce_sum(red[:, :], scv, AX.X))
                    st(v.reciprocal(red[:, :], red[:, :]))
                    v.tensor_tensor(scv, scv, red[:, :].rearrange("p (t o) -> p t o", o=1).to_broadcast([C, TL * H4, G8]),
                                    ALU.mult).then_inc(w_ready, 1)

                def mixing(b, u, st):
                    v.wait_ge(ws_mm, b + 1)
                    st(v.reduce_sum(wsum[:, :], pws[:, :, :].rearrange("p t (h g) -> p g (t h)", g=G8), AX.X))
                    st(v.tensor_tensor(mix[:, :, :], vo[:, :, :], wsum[:, :].rearrange("p (g o) -> p g o", o=1).to_broadcast([C, G8, C]), ALU.mult))
                    st(v.tensor_mul(bt[:, :], bvo[:, :], wsum[:, :]))
                    wait_if(v, o_mm, 2 * b - 2)
                    st(v.reduce_sum(A[u][:, :], mix[:, :, :].rearrange("p g n -> p n g"), AX.X))
                    st(v.reduce_sum(bias[u][:, :], bt[:, :], AX.X))
                    st(v.tensor_add(bias[u][:, :], bias[u][:, :], bo[:, :]))
                    v.sem_inc(a_ready, 1)

                st = Chain(v, dstep)
                below_max(0, st)
                weights(0, st)
                FIRST = st.n

                def step(b, u, last):
                    st = Chain(v, dstep, NW * b + FIRST)
                    if not last:
                        below_max(b + 1, st)
                    mixing(b, u, st)
                    if not last:
                        weights(b + 1, st)
                        assert st.n == NW
                    for h in range(2):
                        v.wait_ge(o_mm, 2 * b + h + 1)
                        xb = X[:, bass.ds(b * N + h * CH, CH)]
                        v.scalar_tensor_tensor(xb, po[h][:, :], bias[u][:, :], xb, ALU.add, ALU.add).then_inc(x_ready, 1)

                over(v, B, step)



E8 = 8
ITERS = 8
TOP = N // E8
NT = T // C
CLIP = 1e-10


def phase_route(nc, K, D, Y, ids, ws):
    with Mem(nc, "sk") as m:
        gw = m.sb("gw", [C, 4, C])
        gT = [m.sb(f"gT{u}", [C, CH]) for u in range(2)]
        G = m.sb("G", [C, NT, E8])
        tmp = m.sb("tmp", [C, NT, E8])
        cg = m.sb("cg", [C, NT, E8])
        mask = m.sb("mask", [C, NT, E8], BF16)
        oneb = m.sb("oneb", [C, C], BF16)
        lower = m.sb("lower", [C, C], BF16)
        uu = m.sb("uu", [C, NT])
        ss = m.sb("ss", [C, NT])
        vv = m.sb("vv", [C, E8])
        part = m.sb("part", [C, E8])
        thr = m.sb("thr", [C, E8], mybir.dt.int32)
        cand = m.sb("cand", [C, E8], mybir.dt.int32)
        bit = m.sb("bit", [C, E8], mybir.dt.int32)
        cnt = m.sb("cnt", [C, E8])
        need = m.sb("need", [C, E8])
        tot = m.sb("tot", [C, NT, E8])
        cum = m.sb("cum", [C, E8, NT])
        zero = m.sb("zero", [C, NT])
        slot, token = m.sb("slot", [C, 1]), m.sb("token", [C, C])
        before = m.sb("before", [C, E8, NT])
        onehot = m.sb("onehot", [C, E8, NT])
        upto = m.sb("upto", [C, E8, NT])
        wE = m.sb("wE", [C, E8, NT])
        onehotT = m.sb("onehotT", [C, E8, C])
        rows = m.sb("rows", [C, E8, 2, C])
        tile_of, base, rank, tok = (m.sb(x, [C, E8]) for x in ("tile_of", "base", "rank", "tok"))
        sel = m.sb("sel", [C, E8, C])
        zeros = m.sb("zeros", [C, 16, C])
        pcn = m.ps("pcn", [C, 16, E8])
        pp = [m.ps(f"pp{h}", [C, 64, E8]) for h in range(2)]
        pq = [m.ps(f"pq{h}", [C, 64, E8]) for h in range(2)]
        pw = [m.ps(f"pw{h}", [C, 64, E8]) for h in range(2)]
        pr = m.ps("pr", [C, E8])
        g_in, const_ready, pool = m.sem("g_in"), m.sem("const_ready"), m.sem("pool")
        g_copied, g_tp = m.sem("g_copied"), m.sem("g_tp")
        g_mm, g_saved, vec, pe_s, v_ready = (m.sem(x) for x in ("g_mm", "g_saved", "vec", "pe", "v_ready"))
        zero_out = m.sem("zero_out")
        bisect_mm, bisect_vec = m.sem("bisect_mm"), m.sem("bisect_vec")

        def bc_e(v8):
            return v8.rearrange("p (o e) -> p o e", o=1).to_broadcast([C, NT, E8])

        def bc_t(v):
            return v.rearrange("p (t o) -> p t o", o=1).to_broadcast([C, NT, E8])

        found = (*pp, *pq)

        def flat(bank):
            return bank[:, :, :].rearrange("p t e -> p (t e)")

        def bc_n(v8):
            return v8.rearrange("p (e o) -> p e o", o=1).to_broadcast([C, v8.shape[-1], C])

        BITS = 30
        NG4 = NCH // 4
        with nc.Block() as block:
            @block.sync
            def _(sp):
                sp.wait_ge(const_ready, 1)
                for j in range(4):
                    sp.dma_start(gw[:, j, 32 * j:32 * j + E8], D["gate_w"]).then_inc(g_in, 16)
                sp.wait_ge(const_ready, 2)
                for k in range(NT // 16):
                    sp.dma_start(D["res"][k * 16 * C:(k + 1) * 16 * C, :].rearrange("(t p) c -> p t c", p=C),
                                 zeros[:, :, :]).then_inc(zero_out, 16)
                sp.wait_ge(zero_out, 16 * (NT // 16))

            @block.gpsimd
            def _(g):
                step = Chain(g, pool)
                step(g.memset(gw[:, :, :], 0.0))
                g.sem_inc(const_ready, 1)
                step(g.memset(oneb[:, :], 1.0))
                step(g.memset(lower[:, :], 1.0))
                step(g.memset(zero[:, :], 0.0))
                step(g.memset(zeros[:, :, :], 0.0))
                step(g.iota(slot[:, :], pattern=[[0, 1]], base=0, channel_multiplier=1, allow_small_or_imprecise_dtypes=True))
                step(g.iota(token[:, :], pattern=[[1, C]], base=0, channel_multiplier=0, allow_small_or_imprecise_dtypes=True))
                step(g.affine_select(out=lower[:, :], in_=lower[:, :], pattern=[[1, C]], base=-1,
                                     channel_multiplier=-1, compare_op=ALU.is_ge, fill=0.0))
                g.sem_inc(const_ready, 1)

            @block.tensor
            def _(pe):
                pe.wait_ge(g_in, 64)
                pe.wait_ge(const_ready, 2)

                def step(n, u, last):
                    wait_if(pe, g_copied, n - 1)
                    for j in range(4):
                        done = pe.matmul(pp[u][:, :, :].rearrange("p t e -> p (t e)"), gw[:, j, :],
                                         Y[:, bass.ds((4 * n + j) * CH, CH)], start=(j == 0), stop=(j == 3))
                    done.then_inc(g_mm, 1)
                    if not isinstance(n, int) or n:
                        tokens(n - 1, 1 - u)

                def tokens(n, u):
                    pe.wait_ge(g_copied, n + 1)
                    wait_if(pe, g_saved, n - 1)
                    for k in range(4):
                        done = pe.transpose(pq[u][:, :, :].rearrange("p t e -> p (t e)")[:, k * C:(k + 1) * C],
                                            gT[u][:, k * C:(k + 1) * C], K["ident"][:, :])
                    done.then_inc(g_tp, 1)

                over(pe, NG4, step, 2, 2)
                tokens(NG4 - 1, 1)
                for i in range(ITERS):
                    pe.wait_ge(v_ready, i + 1)
                    pe.matmul(pr[:, :], K["ones"][:, :], part[:, :], start=True, stop=True).then_inc(pe_s, 1)
                with pe.Fori(0, BITS + 1) as i:
                    pe.wait_ge(bisect_vec, i + 1)
                    for c in range(8):
                        last = pe.matmul(pcn[:, :, :], oneb[:, :], mask[:, 16 * c:16 * c + 16, :], start=(c == 0), stop=(c == 7))
                    last.then_inc(bisect_mm, 1)
                pe.wait_ge(v_ready, ITERS + 1)
                for h in range(2):
                    pe.matmul(pp[h][:, :, :], lower[:, :], mask[:, 64 * h:64 * h + 64, :], start=True, stop=True)
                    last = pe.matmul(pq[h][:, :, :], oneb[:, :], mask[:, 64 * h:64 * h + 64, :], start=True, stop=True)
                last.then_inc(pe_s, 1)
                pe.wait_ge(v_ready, ITERS + 2)
                for h in range(2):
                    pe.matmul(pp[h][:, :, :], lower[:, :], mask[:, 64 * h:64 * h + 64, :], start=True, stop=True)
                    last = pe.matmul(pq[h][:, :, :], oneb[:, :], mask[:, 64 * h:64 * h + 64, :], start=True, stop=True)
                last.then_inc(pe_s, 1)
                pe.wait_ge(v_ready, ITERS + 3)
                for e in range(E8):
                    h, at = e // 4, slice((e % 4) * C, (e % 4 + 1) * C)
                    for bank, source in ((pp, onehot), (pq, upto), (pw, wE)):
                        last = pe.transpose(flat(bank[h])[:, at], source[:, e, :], K["ident"][:, :])
                last.then_inc(pe_s, 1)
                pe.wait_ge(v_ready, ITERS + 4)
                for e in range(E8):
                    last = pe.matmul(flat(found[e // 2])[:, (e % 2) * 2 * C:(e % 2 + 1) * 2 * C], onehotT[:, e, :],
                                     rows[:, e, :, :], start=True, stop=True)
                last.then_inc(pe_s, 1)

            @block.scalar
            def _(a):
                def step(n, u, last):
                    a.wait_ge(g_mm, n + 1)
                    wait_if(a, g_tp, n - 1)
                    a.copy(gT[u][:, :], pp[u][:, :, :].rearrange("p t e -> p (t e)")).then_inc(g_copied, 1)

                over(a, NG4, step)

            @block.vector
            def _(v):
                def save(n, u, last):
                    v.wait_ge(g_tp, n + 1)
                    v.tensor_scalar(G[:, bass.ds(16 * n, 16), :].rearrange("p (j k) e -> p j k e", k=4),
                                    pq[u][:, :, :].rearrange("p t e -> p (t e)")
                                    .rearrange("p (k j x) -> p j k x", j=4, x=32)[:, :, :, 0:E8],
                                    CLIP, None, ALU.max).then_inc(g_saved, 1)

                over(v, NG4, save)
                v.wait_ge(g_saved, NG4)
                step = Chain(v, vec)
                gt = G[:, :, :].rearrange("p t e -> p e t")
                for i in range(ITERS):
                    if i == 0:
                        step(v.reduce_sum(part[:, :], gt, AX.X))
                    else:
                        step(v.tensor_tensor(tmp[:, :, :], G[:, :, :], bc_t(uu[:, :]), ALU.mult))
                        step(v.reduce_sum(part[:, :], tmp[:, :, :].rearrange("p t e -> p e t"), AX.X))
                    v.sem_inc(v_ready, 1)
                    v.wait_ge(pe_s, i + 1)
                    step(v.reciprocal(vv[:, :], pr[:, :]))
                    step(v.tensor_tensor(tmp[:, :, :], G[:, :, :], bc_e(vv[:, :]), ALU.mult))
                    step(v.reduce_sum(ss[:, :], tmp[:, :, :], AX.X))
                    step(v.reciprocal(uu[:, :], ss[:, :]))
                step(v.tensor_tensor(cg[:, :, :], tmp[:, :, :], bc_t(uu[:, :]), ALU.mult))
                step(v.tensor_tensor(tmp[:, :, :], bc_t(ss[:, :]), tmp[:, :, :], ALU.subtract))
                step(v.tensor_tensor(tmp[:, :, :], tmp[:, :, :], bc_t(uu[:, :]), ALU.mult))
                step(v.tensor_scalar(tmp[:, :, :], tmp[:, :, :], -1.0, 1.0, ALU.mult, ALU.add))
                step(v.tensor_tensor(tmp[:, :, :], tmp[:, :, :], cg[:, :, :], ALU.subtract))
                step(v.scalar_tensor_tensor(tmp[:, :, :].rearrange("p t e -> p (t e)"), cg[:, :, :].rearrange("p t e -> p (t e)"), 0.5,
                                            tmp[:, :, :].rearrange("p t e -> p (t e)"), ALU.is_gt, ALU.mult))
                step(v.tensor_tensor(cg[:, :, :], cg[:, :, :], tmp[:, :, :], ALU.add))
                step(v.memset(thr[:, :], 0))
                for i in range(BITS):
                    step(v.tensor_single_scalar(cand[:, :], thr[:, :], 1 << (BITS - 1 - i), ALU.bitwise_or))
                    v.tensor_tensor(mask[:, :, :], cg[:, :, :], bc_e(cand[:, :].bitcast(F32)), ALU.is_ge).then_inc(bisect_vec, 1)
                    v.wait_ge(bisect_mm, i + 1)
                    step(v.reduce_sum(cnt[:, :], pcn[:, :, :].rearrange("p t e -> p e t"), AX.X))
                    step(v.tensor_scalar(bit[:, :], cnt[:, :], float(TOP), float(1 << (BITS - 1 - i)), ALU.is_ge, ALU.mult))
                    step(v.tensor_tensor(thr[:, :], thr[:, :], bit[:, :], ALU.bitwise_or))
                thf = thr[:, :].bitcast(F32)
                v.tensor_tensor(mask[:, :, :], cg[:, :, :], bc_e(thf), ALU.is_gt).then_inc(bisect_vec, 1)
                v.wait_ge(bisect_mm, BITS + 1)
                step(v.reduce_sum(cnt[:, :], pcn[:, :, :].rearrange("p t e -> p e t"), AX.X))
                step(v.tensor_scalar(need[:, :], cnt[:, :], -1.0, float(TOP), ALU.mult, ALU.add))
                step(v.tensor_copy(G[:, :, :], mask[:, :, :]))
                step(v.tensor_tensor(mask[:, :, :], cg[:, :, :], bc_e(thf), ALU.is_equal))
                v.sem_inc(v_ready, 1)
                v.wait_ge(pe_s, ITERS + 1)
                for h in range(2):
                    step(v.tensor_copy(tot[:, 64 * h:64 * h + 64, :], pq[h][:, :, :]))
                for e in range(E8):
                    step(v.tensor_tensor_scan(cum[:, e, :], tot[:, :, e], zero[:, :], 0.0, ALU.add, ALU.add))
                for h in range(2):
                    step(v.tensor_tensor(tot[:, 64 * h:64 * h + 64, :], pp[h][:, :, :], tot[:, 64 * h:64 * h + 64, :], ALU.subtract))
                step(v.tensor_tensor(tot[:, :, :], tot[:, :, :], cum[:, :, :].rearrange("p e t -> p t e"), ALU.add))
                step(v.tensor_tensor(tot[:, :, :], tot[:, :, :], bc_e(need[:, :]), ALU.is_lt))
                step(v.tensor_tensor(tot[:, :, :], tot[:, :, :], mask[:, :, :], ALU.mult))
                step(v.tensor_tensor(G[:, :, :], G[:, :, :], tot[:, :, :], ALU.add))
                step(v.reduce_sum(uu[:, :], G[:, :, :], AX.X))
                step(v.tensor_scalar(uu[:, :], uu[:, :], 1.0, None, ALU.add))
                step(v.reciprocal(uu[:, :], uu[:, :]))
                step(v.scalar_tensor_tensor(tmp[:, :, :].rearrange("p t e -> p (t e)"), cg[:, :, :].rearrange("p t e -> p (t e)"), 0.5,
                                            G[:, :, :].rearrange("p t e -> p (t e)"), ALU.is_gt, ALU.mult))
                step(v.tensor_tensor(wE[:, :, :].rearrange("p e t -> p t e"), tmp[:, :, :], bc_t(uu[:, :]), ALU.mult))
                step(v.tensor_copy(mask[:, :, :], G[:, :, :]))
                v.sem_inc(v_ready, 1)
                v.wait_ge(pe_s, ITERS + 2)
                for h in range(2):
                    tiles = slice(64 * h, 64 * h + 64)
                    step(v.tensor_copy(tot[:, tiles, :], pq[h][:, :, :]))
                    step(v.tensor_tensor(upto[:, :, tiles], pp[h][:, :, :].rearrange("p t e -> p e t"),
                                         mask[:, tiles, :].rearrange("p t e -> p e t"), ALU.add))
                for e in range(E8):
                    step(v.tensor_tensor_scan(cum[:, e, :], tot[:, :, e], zero[:, :], 0.0, ALU.add, ALU.add))
                step(v.tensor_scalar(before[:, :, :], cum[:, :, :], slot[:, :], None, ALU.is_le))
                step(v.tensor_tensor(onehot[:, :, 1:NT], before[:, :, 0:NT - 1], before[:, :, 1:NT], ALU.subtract))
                step(v.tensor_scalar(onehot[:, :, 0:1], before[:, :, 0:1], -1.0, 1.0, ALU.mult, ALU.add))
                v.sem_inc(v_ready, 1)
                step(v.reduce_sum(tile_of[:, :], before[:, :, :], AX.X))
                step(v.tensor_tensor(before[:, :, :], before[:, :, :], tot[:, :, :].rearrange("p t e -> p e t"), ALU.mult))
                step(v.reduce_sum(base[:, :], before[:, :, :], AX.X))
                step(v.tensor_scalar(rank[:, :], base[:, :], -1.0, slot[:, :], ALU.mult, ALU.add))
                v.wait_ge(pe_s, ITERS + 3)
                for h in range(2):
                    four = slice(4 * h, 4 * h + 4)
                    for dst, bank in ((onehotT[:, four, :], pp), (rows[:, four, 0, :], pq), (rows[:, four, 1, :], pw)):
                        step(v.tensor_copy(dst, flat(bank[h]).rearrange("p (k n) -> p k n", n=C)))
                v.sem_inc(v_ready, 1)
                v.wait_ge(pe_s, ITERS + 4)
                pair = [flat(found[k]).rearrange("p (e z n) -> p e z n", z=2, n=C) for k in range(4)]
                for k in range(4):
                    step(v.tensor_tensor(sel[:, 2 * k:2 * k + 2, :], pair[k][:, :, 0, :], bc_n(rank[:, 2 * k:2 * k + 2]), ALU.is_le))
                step(v.reduce_sum(tok[:, :], sel[:, :, :], AX.X))
                step(v.scalar_tensor_tensor(ids[:, :], tile_of[:, :], float(C), tok[:, :], ALU.mult, ALU.add))
                step(v.tensor_tensor(sel[:, :, :], token[:, :].rearrange("p (o n) -> p o n", o=1).to_broadcast([C, E8, C]),
                                     bc_n(tok[:, :]), ALU.is_equal))
                for k in range(4):
                    step(v.tensor_tensor(sel[:, 2 * k:2 * k + 2, :], sel[:, 2 * k:2 * k + 2, :], pair[k][:, :, 1, :], ALU.mult))
                step(v.reduce_sum(ws[:, :], sel[:, :, :], AX.X))


def phase_experts(nc, K, D, X, ids, ws):
    TI = N // C
    with Mem(nc, "ex") as m:
        ew = m.sb("ew", [C, E8, C])
        got = m.sb("got", [C, E8, C])
        gotT = m.sb("gotT", [C, E8, C])
        give = m.sb("give", [C, E8, C])
        rows = [m.sb(f"rows{u}", [C, TI, C]) for u in range(2)]
        pt = [m.ps(f"pt{u}", [C, C]) for u in range(2)]
        po = [m.ps(f"po{u}", [C, C]) for u in range(2)]
        px = [[m.ps(f"px{u}{h}", [C, 4, C]) for h in range(2)] for u in range(2)]
        e_in, got_in = m.sem("e_in"), m.sem("got_in")
        t_ready, t_saved, o_mm, o_saved, added = (m.sem(x) for x in ("t_ready", "t_saved", "o_mm", "o_saved", "added"))
        rows_in = [m.sem("rows_in0"), m.sem("rows_in1")]
        out = [m.sem("out0"), m.sem("out1")]
        x_mm, x_ready = m.sem("x_mm"), m.sem("x_ready")
        with nc.Block() as block:
            @block.gpsimd
            def _(g):
                for e in range(E8):
                    g.indirect_dma_start(got[:, e, :], None, D["tokens"], bass.IndirectOffsetOnAxis(ap=ids[:, e:e + 1], axis=0))\
                     .then_inc(got_in, 16)
                for e in range(E8):
                    g.wait_ge(o_saved, e + 1)
                    if e:
                        g.wait_ge(added, 16 * e)
                    g.indirect_dma_start(D["res"], bass.IndirectOffsetOnAxis(ap=ids[:, e:e + 1], axis=0), give[:, e, :], None,
                                         compute_op=ALU.add).then_inc(added, 16)

            @block.sync
            def _(sp):
                sp.dma_start(ew[:, :, :], D["experts"]).then_inc(e_in, 16)
                sp.wait_ge(added, 16 * E8)

                def step(b, u, last):
                    wait_if(sp, x_mm, 2 * b - 2)
                    sp.dma_start(rows[u][:, :, :], D["res"][bass.ds(b * N, N), :].rearrange("(t p) c -> p t c", p=C))\
                      .then_inc(rows_in[u], 16)

                over(sp, B, step)

            @block.tensor
            def _(pe):
                for e in range(E8):
                    pe.wait_ge(got_in, 16 * E8)
                    wait_if(pe, t_saved, e - 1)
                    pe.transpose(pt[e % 2][:, :], got[:, e, :], K["ident"][:, :]).then_inc(t_ready, 1)
                pe.wait_ge(e_in, 16)
                for e in range(E8):
                    pe.wait_ge(t_saved, e + 1)
                    wait_if(pe, o_saved, e - 1)
                    pe.matmul(po[e % 2][:, :], gotT[:, e, :], ew[:, e, :], start=True, stop=True).then_inc(o_mm, 1)

                def step(b, u, last):
                    pe.wait_ge(rows_in[u], 8 * (b - u) + 16)
                    for h in range(2):
                        wait_if(pe, x_ready, 2 * b + h - 3)
                        for r in range(4):
                            done = pe.transpose(px[u][h][:, r, :], rows[u][:, 4 * h + r, :], K["ident"][:, :])
                        done.then_inc(x_mm, 1)

                over(pe, B, step)

            @block.vector
            def _(v):
                for e in range(E8):
                    v.wait_ge(t_ready, e + 1)
                    v.tensor_copy(gotT[:, e, :], pt[e % 2][:, :]).then_inc(t_saved, 1)
                for e in range(E8):
                    v.wait_ge(o_mm, e + 1)
                    v.tensor_scalar(give[:, e, :], po[e % 2][:, :], ws[:, e:e + 1], None, ALU.mult).then_inc(o_saved, 1)

                def step(b, u, last):
                    for h in range(2):
                        v.wait_ge(x_mm, 2 * b + h + 1)
                        xb = X[:, bass.ds(b * N + h * CH, CH)]
                        v.tensor_tensor(xb, xb, px[u][h][:, :, :].rearrange("p r c -> p (r c)"), ALU.add).then_inc(x_ready, 1)

                over(v, B, step)

            @block.scalar
            def _(a):
                def step(b, u, last):
                    a.wait_ge(x_ready, 2 * b + 2)
                    a.dma_start(D["out"][bass.ds(b, 1)].rearrange("o c n -> c (o n)"), X[:, bass.ds(b * N, N)]).then_inc(out[u], 16)

                over(a, B, step)
                for u in range(2):
                    a.wait_ge(out[u], 16 * B // 2)


def build(nc, D):
    with ExitStack() as ctx:
        def sb(name, shape, dt=F32):
            return ctx.enter_context(nc.sbuf_tensor(name, shape, dt))

        K = {"ident": sb("ident", [C, C]), "ones": sb("ones", [C, C]),
             "neghalf": sb("neghalf", [C, C]), "mask8": sb("mask8", [C, C]),
             "eps": sb("eps", [C, 4]), "negone": sb("negone", [C, 4]),
             "stats": sb("bnstats", [C, NCH, 6])}
        X = sb("X", [C, T])
        D["proj"] = nc.dram_tensor("proj", [C, T], F32).ap()
        D["qk"] = nc.dram_tensor("qk", [2, 3, C, T], BF16).ap()
        D["tokens"] = nc.dram_tensor("tokens", [T, C], F32).ap()
        D["res"] = nc.dram_tensor("res", [T, C], F32).ap()
        D["u"] = nc.dram_tensor("u", [C, T // C, C], F32).ap()
        phase_constants(nc, K)
        phase_conv(nc, K, D, X)
        phase_linatt(nc, K, D, X)
        phase_linatt_norm(nc, K, D, X)
        with Mem(nc, "attn") as m:
            K["rv"] = m.sb("rv", [C, T // C, RH * DH])
            phase_attn_prep(nc, K, D, X)
            phase_attn(nc, K, D, X)
        with Mem(nc, "ffn") as m:
            Y = m.sb("Y", [C, T])
            wcol, b2w = m.sb("wcol", [C, FT, B]), m.sb("b2w", [C, B])
            phase_norm(nc, K, X, Y, "n2")
            phase_router(nc, K, D, Y, wcol, b2w)
            phase_ffn(nc, K, D, X, Y, wcol, b2w)
        with Mem(nc, "gqa") as m:
            Y = m.sb("Y", [C, T])
            phase_norm(nc, K, X, Y, "n3")
            phase_gqa(nc, K, D, X, Y)
        with Mem(nc, "moe") as m:
            Y = m.sb("Y", [C, T])
            ids, ws = m.sb("ids", [C, E8], mybir.dt.int32), m.sb("ws", [C, E8])
            phase_norm(nc, K, X, Y, "n4", D["tokens"])
            phase_route(nc, K, D, Y, ids, ws)
            phase_experts(nc, K, D, X, ids, ws)


def layout(inputs):
    import numpy as np
    x = {k: np.asarray(v) for k, v in inputs.items()}
    w = x["L0_conv_conv_w"]
    out = {"x": x["x"].reshape(B, C, N),
           "conv_w": w.reshape(C, 72),
           "conv_wt": np.tile(w.reshape(C, 8, 9).transpose(1, 2, 0), (16, 1, 1))}
    for k in ("bn1_gamma", "bn1_beta", "bn2_gamma", "bn2_beta", "prelu_a"):
        out["L0_conv_" + k] = x["L0_conv_" + k]
    out["w_qkvT"] = x["L1_conv_w_qkv"].reshape(16, 3, 8, C).transpose(3, 1, 0, 2).reshape(C, 3, C)
    out["w_projT"] = x["L1_conv_w_proj"].reshape(C, 2, C).transpose(2, 1, 0)
    out["w_pwT"] = np.tile(x["L1_conv_w_pw"].reshape(4, 4, 3, 8, 8).transpose(4, 2, 0, 1, 3).reshape(8, 3, 4, 32), (16, 1, 1, 1))
    out["w_taps"] = tap_weights(x["L1_conv_w_dw"])
    out["w_qtaps"] = x["L1_conv_w_dw"].reshape(16, PARTS, HD, TAPS)[:, 0].reshape(C, TAPS)
    for k in ("bn_gamma", "bn_beta"):
        out["L1_conv_" + k] = x["L1_conv_" + k]
    for k in ("wq_s", "wk_s", "wv_r", "w_out"):
        out[k] = x["L2_attn_" + k]
    out["wq_rT"] = x["L2_attn_wq_r"].T
    out["wk_retT"] = np.tile(x["L2_attn_wk_ret"].T, (8, 8))
    out["router_wT"] = x["L2_ffn_router_w"].T
    out["pw6"] = partition_weights()
    pad = FT * C - E6 * F
    out["pwx"] = np.pad(np.repeat(partition_weights(), F, axis=1), ((0, 0), (0, pad)))
    out["ffn_b2"] = x["L2_ffn_b2"]
    out["W1"] = np.pad(x["L2_ffn_W1"].transpose(1, 0, 2).reshape(C, E6 * F), ((0, 0), (0, pad))).reshape(C, FT, C)
    out["b1"] = np.pad(x["L2_ffn_b1"].reshape(-1), (0, pad)).reshape(FT, C).T
    out["W2"] = np.pad(x["L2_ffn_W2"].reshape(E6 * F, C), ((0, pad), (0, 0))).reshape(FT, C, C).transpose(1, 0, 2)
    out["Wk"] = x["L3_attn_Wk"].reshape(C, G8, C)
    out["WqT"] = x["L3_attn_Wq"].reshape(C, G8 * H4, C).transpose(2, 1, 0)
    out["WvT"] = x["L3_attn_Wv"].reshape(C, G8, C).transpose(2, 1, 0)
    out["Wo"] = x["L3_attn_Wo"].reshape(G8, C, C).transpose(1, 0, 2)
    out["bkT"] = x["L3_attn_bk"].reshape(G8, C).T
    out["bvT"] = x["L3_attn_bv"].reshape(G8, C).T
    out["bqT"] = x["L3_attn_bq"].reshape(G8 * H4, C).T
    out["bo"] = x["L3_attn_bo"].reshape(C, 1)
    out["gate_w"] = x["L3_ffn_gate_w"][0]
    out["experts"] = x["L3_ffn_experts"].transpose(1, 0, 2)
    return {k: np.ascontiguousarray(v) for k, v in out.items()}


def kernel(**inputs):
    import concourse.bacc as _bacc
    from concourse.bass_utils import run_bass_kernel_spmd as _run

    nc = _bacc.Bacc("TRN2", target_bir_lowering=False, num_devices=1)
    data = layout(inputs)
    arrays, D = {}, {}
    for name, a in data.items():
        arrays[f"in_{name}_dram"] = a
        D[name] = nc.dram_tensor(f"in_{name}_dram", a.shape, mybir.dt.from_np(a.dtype), kind="ExternalInput").ap()
    D["out"] = nc.dram_tensor("out_0_dram", [B, C, N], F32, kind="ExternalOutput").ap()
    build(nc, D)
    r = _run(nc, [arrays], core_ids=[0])
    return r.results[0]["out_0_dram"].reshape(B, C, HW, HW)
```
